# Optimizing a Trainium2 kernel written in Bass

```python
import numpy as np
import jax
import jax.numpy as jnp

def _softmax(x, axis=-1):
    return jax.nn.softmax(x, axis=axis)

def _gelu(x):
    return jax.nn.gelu(x, approximate=True)

def _silu(x):
    return jax.nn.silu(x)

def _sigmoid(x):
    return jax.nn.sigmoid(x)

def _layernorm(x, axis=-1, eps=1e-05):
    m = jnp.mean(x, axis=axis, keepdims=True)
    v = jnp.var(x, axis=axis, keepdims=True)
    return (x - m) / jnp.sqrt(v + eps)

def _scatter_add(tgt, idx, src, axis=0):
    return tgt.at[idx].add(src)

def _segment_sum(src, seg, n):
    return jax.ops.segment_sum(src, seg, n)
kernel_name = 'mk_seq_preln_d2_jaxref_r8_546dac'

def setup_inputs(seed: int=0):
    np.random.seed(seed)
    _w = jnp.asarray

    def _L0_attn_setup():
        import jax, jax.numpy as jnp
        import numpy as np
        NUM_HEADS = 8
        CHUNK = 64

        def _retention(q, k, v):
            B, Hn, L, DK = q.shape
            DV = v.shape[-1]
            C = CHUNK
            N = L // C
            dt = q.dtype
            gamma = (1.0 - jnp.exp2(-5.0 - jnp.arange(Hn, dtype=jnp.float32))).astype(dt)
            q = q * DK ** (-0.5)
            idx = jnp.arange(C)
            diff = idx[:, None] - idx[None, :]
            D = jnp.where(diff >= 0, gamma[:, None, None] ** diff, 0.0).astype(dt)
            decay_q = (gamma[:, None] ** (idx[None, :] + 1)).astype(dt)
            decay_k = (gamma[:, None] ** (C - 1 - idx[None, :])).astype(dt)
            decay_s = (gamma ** C).astype(dt)

            def to_chunks(x):
                return jnp.moveaxis(x.reshape(B, Hn, N, C, -1), 2, 0)
            qs, ks, vs = map(to_chunks, (q, k, v))

            def step(S, x):
                qc, kc, vc = x
                attn = jnp.einsum('bhid,bhjd->bhij', qc, kc) * D
                o_intra = jnp.einsum('bhij,bhje->bhie', attn, vc)
                o_inter = jnp.einsum('bhid,bhde->bhie', qc * decay_q[None, :, :, None], S)
                S_new = decay_s[None, :, None, None] * S + jnp.einsum('bhjd,bhje->bhde', kc * decay_k[None, :, :, None], vc)
                return (S_new, o_intra + o_inter)
            S0 = jnp.zeros((B, Hn, DK, DV), dt)
            _, o = jax.lax.scan(step, S0, (qs, ks, vs))
            return jnp.moveaxis(o, 0, 2).reshape(B, Hn, L, DV)

        def _xavier(key, fan_in, fan_out, gain=2 ** (-2.5)):
            limit = gain * np.sqrt(6.0 / (fan_in + fan_out))
            return jax.random.uniform(key, (fan_in, fan_out), jnp.float32, -limit, limit)
        key = jax.random.key(seed)
        k0, k1, k2, k3, k4 = jax.random.split(key, 5)
        B, L, D = (2, 512, 128)
        return {'hidden_states': jax.random.normal(k0, (B, L, D), jnp.float32), 'rel_pos': jnp.zeros((1,), jnp.float32), 'Wq': _xavier(k1, D, D), 'Wk': _xavier(k2, D, D), 'Wv': _xavier(k3, D, D), 'Wo': _xavier(k4, D, D)}
    _L0_attn_in = _L0_attn_setup()

    def _L0_ffn_setup():
        import jax, jax.numpy as jnp
        import numpy as np
        E = 16
        H = 128
        F = 256
        TOP_K = 1
        B, S = (2, 128)
        key = jax.random.key(seed)
        ks = jax.random.split(key, 7)
        s = 0.02
        return {'hidden_states': jax.random.normal(ks[0], (B, S, H), jnp.float32), 'w_router': jax.random.normal(ks[1], (E, H), jnp.float32) * s, 'gate_up_proj': jax.random.normal(ks[2], (E, H, 2 * F), jnp.float32) * s, 'down_proj': jax.random.normal(ks[3], (E, F, H), jnp.float32) * s, 'w_gate': jax.random.normal(ks[4], (F, H), jnp.float32) * s, 'w_up': jax.random.normal(ks[5], (F, H), jnp.float32) * s, 'w_down': jax.random.normal(ks[6], (H, F), jnp.float32) * s}
    _L0_ffn_in = _L0_ffn_setup()

    def _L1_attn_setup():
        import jax, jax.numpy as jnp
        import numpy as np
        HIDDEN = 128
        HEADS = 16
        HEAD_DIM = HIDDEN // HEADS
        SCALE = HEAD_DIM ** (-0.5)
        key = jax.random.key(seed)
        ks = jax.random.split(key, 9)
        init = 1.0 / np.sqrt(HIDDEN)
        hidden_states = jax.random.normal(ks[0], (8, 128, HIDDEN), dtype=jnp.float32)

        def lin(k):
            kw, kb = jax.random.split(k)
            W = jax.random.uniform(kw, (HIDDEN, HIDDEN), jnp.float32, -init, init)
            b = jax.random.uniform(kb, (HIDDEN,), jnp.float32, -init, init)
            return (W, b)
        Wq, bq = lin(ks[1])
        Wk, bk = lin(ks[2])
        Wv, bv = lin(ks[3])
        Wo, bo = lin(ks[4])
        return {'hidden_states': hidden_states, 'Wq': Wq, 'bq': bq, 'Wk': Wk, 'bk': bk, 'Wv': Wv, 'bv': bv, 'Wo': Wo, 'bo': bo}
    _L1_attn_in = _L1_attn_setup()

    def _L1_ffn_setup():
        import jax, jax.numpy as jnp
        import numpy as np
        B, S, D, H, F = (4, 512, 128, 16, 512)
        CAP = 0.125
        ROPE_BASE = 10000.0

        def rmsnorm(x, g):
            return x * jax.lax.rsqrt(jnp.mean(x * x, -1, keepdims=True) + 1e-06) * g

        def rope(t, pos):
            hd = t.shape[-1]
            inv = 1.0 / ROPE_BASE ** (jnp.arange(0, hd, 2, dtype=jnp.float32) / hd)
            f = pos[:, None, :, None].astype(jnp.float32) * inv
            emb = jnp.concatenate([f, f], axis=-1)
            cos, sin = (jnp.cos(emb), jnp.sin(emb))
            rot = jnp.concatenate([-t[..., hd // 2:], t[..., :hd // 2]], axis=-1)
            return t * cos + rot * sin
        key = jax.random.key(seed)
        ks = jax.random.split(key, 9)
        scale = 0.02
        x = jax.random.normal(ks[0], (B, S, D), jnp.float32)
        causal = jnp.where(jnp.tril(jnp.ones((S, S), bool)), 0.0, -1000000000.0).astype(jnp.float32)
        attention_mask = jnp.broadcast_to(causal[None, None], (B, 1, S, S))
        position_ids = jnp.broadcast_to(jnp.arange(S, dtype=jnp.int32), (B, S))
        return {'x': x, 'attention_mask': attention_mask, 'position_ids': position_ids, 'router_w': jax.random.normal(ks[1], (D, 1), jnp.float32) * scale, 'router_b': jnp.zeros((1,), jnp.float32), 'wq': jax.random.normal(ks[2], (D, D), jnp.float32) * scale, 'wk': jax.random.normal(ks[3], (D, D), jnp.float32) * scale, 'wv': jax.random.normal(ks[4], (D, D), jnp.float32) * scale, 'wo': jax.random.normal(ks[5], (D, D), jnp.float32) * scale, 'w1': jax.random.normal(ks[6], (D, F), jnp.float32) * scale, 'w2': jax.random.normal(ks[7], (F, D), jnp.float32) * scale, 'ln1': jnp.ones((D,), jnp.float32), 'ln2': jnp.ones((D,), jnp.float32)}
    _L1_ffn_in = _L1_ffn_setup()
    _d = {'L0_attn_hidden_states': _L0_attn_in['hidden_states'], 'L0_attn_rel_pos': _L0_attn_in['rel_pos'], 'L0_attn_Wq': _L0_attn_in['Wq'], 'L0_attn_Wk': _L0_attn_in['Wk'], 'L0_attn_Wv': _L0_attn_in['Wv'], 'L0_attn_Wo': _L0_attn_in['Wo'], 'L0_ffn_w_router': _L0_ffn_in['w_router'], 'L0_ffn_gate_up_proj': _L0_ffn_in['gate_up_proj'], 'L0_ffn_down_proj': _L0_ffn_in['down_proj'], 'L0_ffn_w_gate': _L0_ffn_in['w_gate'], 'L0_ffn_w_up': _L0_ffn_in['w_up'], 'L0_ffn_w_down': _L0_ffn_in['w_down'], 'L1_attn_Wq': _L1_attn_in['Wq'], 'L1_attn_bq': _L1_attn_in['bq'], 'L1_attn_Wk': _L1_attn_in['Wk'], 'L1_attn_bk': _L1_attn_in['bk'], 'L1_attn_Wv': _L1_attn_in['Wv'], 'L1_attn_bv': _L1_attn_in['bv'], 'L1_attn_Wo': _L1_attn_in['Wo'], 'L1_attn_bo': _L1_attn_in['bo'], 'L1_ffn_attention_mask': _L1_ffn_in['attention_mask'], 'L1_ffn_position_ids': _L1_ffn_in['position_ids'], 'L1_ffn_router_w': _L1_ffn_in['router_w'], 'L1_ffn_router_b': _L1_ffn_in['router_b'], 'L1_ffn_wq': _L1_ffn_in['wq'], 'L1_ffn_wk': _L1_ffn_in['wk'], 'L1_ffn_wv': _L1_ffn_in['wv'], 'L1_ffn_wo': _L1_ffn_in['wo'], 'L1_ffn_w1': _L1_ffn_in['w1'], 'L1_ffn_w2': _L1_ffn_in['w2'], 'L1_ffn_ln1': _L1_ffn_in['ln1'], 'L1_ffn_ln2': _L1_ffn_in['ln2']}
    _x0 = _d['L0_attn_hidden_states']
    _d['L0_attn_hidden_states'] = jax.random.normal(jax.random.fold_in(jax.random.key(seed), 1), (32, 256, 128), dtype=_x0.dtype)
    del _x0
    return _d

def reference(L0_attn_hidden_states, L0_attn_rel_pos, L0_attn_Wq, L0_attn_Wk, L0_attn_Wv, L0_attn_Wo, L0_ffn_w_router, L0_ffn_gate_up_proj, L0_ffn_down_proj, L0_ffn_w_gate, L0_ffn_w_up, L0_ffn_w_down, L1_attn_Wq, L1_attn_bq, L1_attn_Wk, L1_attn_bk, L1_attn_Wv, L1_attn_bv, L1_attn_Wo, L1_attn_bo, L1_ffn_attention_mask, L1_ffn_position_ids, L1_ffn_router_w, L1_ffn_router_b, L1_ffn_wq, L1_ffn_wk, L1_ffn_wv, L1_ffn_wo, L1_ffn_w1, L1_ffn_w2, L1_ffn_ln1, L1_ffn_ln2):

    def _L0_attn_ref(hidden_states, rel_pos, Wq, Wk, Wv, Wo):
        import jax, jax.numpy as jnp
        import numpy as np
        NUM_HEADS = 8
        CHUNK = 64

        def _retention(q, k, v):
            B, Hn, L, DK = q.shape
            DV = v.shape[-1]
            C = CHUNK
            N = L // C
            dt = q.dtype
            gamma = (1.0 - jnp.exp2(-5.0 - jnp.arange(Hn, dtype=jnp.float32))).astype(dt)
            q = q * DK ** (-0.5)
            idx = jnp.arange(C)
            diff = idx[:, None] - idx[None, :]
            D = jnp.where(diff >= 0, gamma[:, None, None] ** diff, 0.0).astype(dt)
            decay_q = (gamma[:, None] ** (idx[None, :] + 1)).astype(dt)
            decay_k = (gamma[:, None] ** (C - 1 - idx[None, :])).astype(dt)
            decay_s = (gamma ** C).astype(dt)

            def to_chunks(x):
                return jnp.moveaxis(x.reshape(B, Hn, N, C, -1), 2, 0)
            qs, ks, vs = map(to_chunks, (q, k, v))

            def step(S, x):
                qc, kc, vc = x
                attn = jnp.einsum('bhid,bhjd->bhij', qc, kc) * D
                o_intra = jnp.einsum('bhij,bhje->bhie', attn, vc)
                o_inter = jnp.einsum('bhid,bhde->bhie', qc * decay_q[None, :, :, None], S)
                S_new = decay_s[None, :, None, None] * S + jnp.einsum('bhjd,bhje->bhde', kc * decay_k[None, :, :, None], vc)
                return (S_new, o_intra + o_inter)
            S0 = jnp.zeros((B, Hn, DK, DV), dt)
            _, o = jax.lax.scan(step, S0, (qs, ks, vs))
            return jnp.moveaxis(o, 0, 2).reshape(B, Hn, L, DV)

        def _xavier(key, fan_in, fan_out, gain=2 ** (-2.5)):
            limit = gain * np.sqrt(6.0 / (fan_in + fan_out))
            return jax.random.uniform(key, (fan_in, fan_out), jnp.float32, -limit, limit)
        B, L, Dm = hidden_states.shape
        Hd = Dm // NUM_HEADS
        q = (hidden_states @ Wq).reshape(B, L, NUM_HEADS, Hd).transpose(0, 2, 1, 3)
        k = (hidden_states @ Wk).reshape(B, L, NUM_HEADS, Hd).transpose(0, 2, 1, 3)
        v = (hidden_states @ Wv).reshape(B, L, NUM_HEADS, Hd).transpose(0, 2, 1, 3)
        o = _retention(q, k, v)
        o = o.transpose(0, 2, 1, 3).reshape(B, L, Dm)
        return o @ Wo

    def _L0_ffn_ref(hidden_states, w_router, gate_up_proj, down_proj, w_gate, w_up, w_down):
        import jax, jax.numpy as jnp
        import numpy as np
        E = 16
        H = 128
        F = 256
        TOP_K = 1
        B, S = (2, 128)
        b, s, h = hidden_states.shape
        x = hidden_states.reshape(-1, h)
        logits = x @ w_router.T
        _, top_idx = jax.lax.top_k(logits, TOP_K)
        mask = jax.nn.one_hot(top_idx, E, dtype=logits.dtype).sum(axis=1)
        scores = jax.nn.sigmoid(logits) * mask
        masked_inputs = scores.T[:, :, None] * x[None, :, :]
        gate_up = jnp.einsum('eth,ehf->etf', masked_inputs, gate_up_proj)
        gate, up = jnp.split(gate_up, 2, axis=-1)
        expert_out = jnp.einsum('etf,efh->eth', up * jax.nn.silu(gate), down_proj)
        shared = jax.nn.silu(x @ w_gate.T) * (x @ w_up.T) @ w_down.T
        out = shared + expert_out.sum(axis=0)
        return out.reshape(b, s, h)

    def _L1_attn_ref(hidden_states, Wq, bq, Wk, bk, Wv, bv, Wo, bo):
        import jax, jax.numpy as jnp
        import numpy as np
        HIDDEN = 128
        HEADS = 16
        HEAD_DIM = HIDDEN // HEADS
        SCALE = HEAD_DIM ** (-0.5)
        b, s, d = hidden_states.shape
        q = (hidden_states @ Wq.T + bq).reshape(b, s, HEADS, HEAD_DIM)
        k = (hidden_states @ Wk.T + bk).reshape(b, s, HEADS, HEAD_DIM)
        v = (hidden_states @ Wv.T + bv).reshape(b, s, HEADS, HEAD_DIM)
        q = q * SCALE
        scores = jnp.einsum('bqhd,bkhd->bhqk', q, k)
        probs = jax.nn.softmax(scores.astype(jnp.float32), axis=-1).astype(scores.dtype)
        out = jnp.einsum('bhqk,bkhd->bqhd', probs, v).reshape(b, s, d)
        return out @ Wo.T + bo

    def _L1_ffn_ref(x, attention_mask, position_ids, router_w, router_b, wq, wk, wv, wo, w1, w2, ln1, ln2):
        import jax, jax.numpy as jnp
        import numpy as np
        B, S, D, H, F = (4, 512, 128, 16, 512)
        CAP = 0.125
        ROPE_BASE = 10000.0

        def rmsnorm(x, g):
            return x * jax.lax.rsqrt(jnp.mean(x * x, -1, keepdims=True) + 1e-06) * g

        def rope(t, pos):
            hd = t.shape[-1]
            inv = 1.0 / ROPE_BASE ** (jnp.arange(0, hd, 2, dtype=jnp.float32) / hd)
            f = pos[:, None, :, None].astype(jnp.float32) * inv
            emb = jnp.concatenate([f, f], axis=-1)
            cos, sin = (jnp.cos(emb), jnp.sin(emb))
            rot = jnp.concatenate([-t[..., hd // 2:], t[..., :hd // 2]], axis=-1)
            return t * cos + rot * sin
        b, s, d = x.shape
        hd = d // H
        weights = (x @ router_w)[..., 0] + router_b[0]
        k = int(CAP * s)
        topv, topi = jax.lax.top_k(weights, k)
        thr = topv[:, -1]
        sel_mask = (weights > thr[:, None]).astype(x.dtype)
        kc = k - 1
        sel_idx = jnp.sort(topi[:, :kc], axis=1)
        bidx = jnp.arange(b)[:, None]
        x_sel = x[bidx, sel_idx]
        pos_sel = position_ids[bidx, sel_idx]
        w_sel = weights[bidx, sel_idx]
        m = attention_mask[:, 0]
        m_sel = m[bidx[:, :, None], sel_idx[:, :, None], sel_idx[:, None, :]]
        hn = rmsnorm(x_sel, ln1)

        def heads(t):
            return t.reshape(b, kc, H, hd).transpose(0, 2, 1, 3)
        q = rope(heads(hn @ wq), pos_sel)
        kk = rope(heads(hn @ wk), pos_sel)
        v = heads(hn @ wv)
        sc = jnp.einsum('bhqd,bhkd->bhqk', q, kk) / np.sqrt(hd).astype(np.float32)
        sc = sc + m_sel[:, None]
        a = jax.nn.softmax(sc, axis=-1)
        o = jnp.einsum('bhqk,bhkd->bhqd', a, v).transpose(0, 2, 1, 3).reshape(b, kc, d) @ wo
        x1 = x_sel + o
        x2 = x1 + jax.nn.gelu(rmsnorm(x1, ln2) @ w1) @ w2
        proc = x2 * w_sel[..., None]
        out = jnp.zeros_like(x).at[bidx, sel_idx].set(proc)
        return out + x * (1.0 - sel_mask)[..., None]
    x = L0_attn_hidden_states
    x = x + _L0_attn_ref(_layernorm(x, axis=-1), L0_attn_rel_pos, L0_attn_Wq, L0_attn_Wk, L0_attn_Wv, L0_attn_Wo)
    x = x + _L0_ffn_ref(_layernorm(x, axis=-1), L0_ffn_w_router, L0_ffn_gate_up_proj, L0_ffn_down_proj, L0_ffn_w_gate, L0_ffn_w_up, L0_ffn_w_down)
    x = x + _L1_attn_ref(_layernorm(x, axis=-1), L1_attn_Wq, L1_attn_bq, L1_attn_Wk, L1_attn_bk, L1_attn_Wv, L1_attn_bv, L1_attn_Wo, L1_attn_bo)
    x = x + _L1_ffn_ref(_layernorm(x, axis=-1), L1_ffn_attention_mask, L1_ffn_position_ids, L1_ffn_router_w, L1_ffn_router_b, L1_ffn_wq, L1_ffn_wk, L1_ffn_wv, L1_ffn_wo, L1_ffn_w1, L1_ffn_w2, L1_ffn_ln1, L1_ffn_ln2)
    return x

_drawn_inputs = setup_inputs


def setup_inputs(seed=0):
    import zlib

    import numpy as np

    out = dict(_drawn_inputs(seed))
    spreads = {'L1_ffn_ln1': (1.0, 0.6), 'L1_ffn_ln2': (1.0, 0.6)}
    factors = {'L0_attn_Wq': 3.063,
     'L0_attn_Wk': 2.968,
     'L0_attn_Wv': 3.243,
     'L0_attn_Wo': 3.618,
     'L0_ffn_w_router': 5.323,
     'L0_ffn_gate_up_proj': 5.282,
     'L0_ffn_down_proj': 5.763,
     'L0_ffn_w_gate': 4.082,
     'L0_ffn_w_up': 3.93,
     'L0_ffn_w_down': 3.482,
     'L1_attn_Wq': 3.248,
     'L1_attn_bq': 8.0,
     'L1_attn_Wk': 2.993,
     'L1_attn_bk': 8.0,
     'L1_ffn_wq': 8.0,
     'L1_ffn_wk': 8.0,
     'L1_ffn_wv': 8.0,
     'L1_ffn_wo': 8.0,
     'L1_ffn_w1': 8.0,
     'L1_ffn_w2': 8.0}
    for name, (base, spread) in spreads.items():
        noise = np.random.default_rng([zlib.crc32(name.encode()), seed]).standard_normal(out[name].shape)
        drawn = base * np.exp(spread * noise) if base else spread * noise
        out[name] = jnp.asarray(drawn.astype(out[name].dtype))
    for name, factor in factors.items():
        out[name] = (out[name] * factor).astype(out[name].dtype)
    return out
```

```python
from contextlib import ExitStack

import numpy as np

import concourse.bass as bass
from concourse import mybir

F32 = mybir.dt.float32
BF16 = mybir.dt.bfloat16
I32 = mybir.dt.int32
U32 = mybir.dt.uint32
ALU = mybir.AluOpType
ACT = mybir.ActivationFunctionType
AX = mybir.AxisListType

P = 128
B, S, D = 32, 256, 128
TPS = S // P
NT = B * TPS
LN_EPS = 1e-5

RH, RD = 8, D // 8
RPAD = 32
RG = RH * RPAD // P
RQ = P // RPAD

NE = 16
EF = 256
ZERO_DMA = 1024
NX = NT + NE


def after(engine, sem, count):
    if isinstance(count, int) and count <= 0:
        return
    engine.wait_ge(sem, count)


def after_apart(engine, sem, count, always):
    engine.wait_ge(*always)
    after(engine, sem, count)


def pipeline(engine, steps, n, first):
    def written(it):
        for step, lag in steps:
            if 0 <= it - lag < n:
                step(it - lag, (it - lag) % 2, (it - lag) // 2)

    for it in range(first):
        written(it)
    with engine.Fori(first // 2, n // 2) as k:
        for turn in range(2):
            for step, lag in steps:
                c = turn - lag
                step(k * 2 + c, c % 2, k + c // 2)
    for it in range(n, n + 1 + max(lag for _, lag in steps)):
        written(it)


FIRST = 8
X_PARTS = (1, 4, 8, B)


class Memory:

    def __init__(self, nc):
        self.nc, self.ctx, self.sems = nc, ExitStack(), []

    def __enter__(self):
        self.ctx.__enter__()
        return self

    def __exit__(self, *e):
        self.ctx.__exit__(*e)
        self.nc.clear_and_free_semaphores(self.sems)
        self.nc.all_engine_barrier()

    def sbuf(self, name, shape, dtype=F32):
        return self.ctx.enter_context(self.nc.sbuf_tensor(name, shape, dtype))

    def psum(self, name, shape, dtype=F32):
        return self.ctx.enter_context(self.nc.psum_tensor(name, shape, dtype))

    def sem(self, name):
        self.sems.append(self.nc.alloc_semaphore(name))
        return self.sems[-1]


def retention_phase(nc, w, keep):
    with Memory(nc) as m:
        x_sb, h2_all, h2T_all, logits_all = keep["x"], keep["h2"], keep["h2T"], keep["logits"]
        ident = keep["ident"]

        wq = m.sbuf("r_wq", [P, D])
        wk = m.sbuf("r_wk", [P, D])
        wv = m.sbuf("r_wv", [P, D])
        wo = m.sbuf("r_wo", [P, RG, D])
        router = m.sbuf("r_router", [P, NE])
        decay = m.sbuf("r_decay", [P, RH, P])
        q_decay = m.sbuf("r_q_decay", [P, P])
        k_decay = m.sbuf("r_k_decay", [P, D])
        own_head = m.sbuf("r_own_head", [P, RH, RPAD])
        half = m.sbuf("r_half", [P, TPS])
        eps = m.sbuf("r_eps", [P, TPS])

        stats = m.sbuf("r_stats", [P, 2, 2, TPS, 6])
        mv1 = m.sbuf("r_mv1", [P, 2, TPS, 2])
        mv2 = m.sbuf("r_mv2", [P, 2, TPS, 2])
        ve1 = m.sbuf("r_ve1", [P, TPS])
        ve2 = m.sbuf("r_ve2", [P, TPS])
        rstd1 = m.sbuf("r_rstd1", [P, 2, TPS])
        rstd2 = m.sbuf("r_rstd2", [P, 2, TPS])
        h = m.sbuf("r_h", [P, 2, TPS, D])
        hT = m.sbuf("r_hT", [P, 2, S])
        qT = m.sbuf("r_qT", [P, 2, S])
        kT = m.sbuf("r_kT", [P, 2, S])
        q_spread = m.sbuf("r_q_spread", [P, 2, RH, S])
        v_pad = m.sbuf("r_v_pad", [P, 2, TPS, RH, RPAD])
        k_tok = m.sbuf("r_k_tok", [P, 2, D])
        q_late = m.sbuf("r_q_late", [P, 2, P])
        state = m.sbuf("r_state", [P, 2, RH, RPAD])
        score = m.sbuf("r_score", [P, 2, TPS * RG, RQ, P])
        oT = m.sbuf("r_oT", [P, 2, RG, S])
        h2 = m.sbuf("r_h2", [P, 2, TPS, D])
        h2T = m.sbuf("r_h2T", [P, 2, S])

        ps_hT = m.psum("ps_hT", [P, S])
        ps_qk = m.psum("ps_qk", [P, 2, S])
        ps_kv = m.psum("ps_kv", [P, 3, D])
        ps_score = [m.psum(f"ps_score{i}", [P, RQ, P]) for i in range(2)]
        ps_state = m.psum("ps_state", [P, RH * RPAD])
        ps_oT = m.psum("ps_oT", [P, RG, S])
        ps_tail = m.psum("ps_tail", [P, 512])

        loaded = m.sem("r_loaded")
        x_loaded = [m.sem(f"r_x_loaded{i}") for i in range(len(X_PARTS))]
        zeroed = m.sem("r_zeroed")
        stats1_part = m.sem("r_stats1_part")
        stats1_done = m.sem("r_stats1_done")
        ve1_done = m.sem("r_ve1_done")
        rstd1_done = m.sem("r_rstd1_done")
        h_done = m.sem("r_h_done")
        hT_done = m.sem("r_hT_done")
        hT_copied = m.sem("r_hT_copied")
        qk_done = m.sem("r_qk_done")
        kv_done = m.sem("r_kv_done")
        qT_copied = m.sem("r_qT_copied")
        kT_copied = m.sem("r_kT_copied")
        v_copied = m.sem("r_v_copied")
        k_tok_done = m.sem("r_k_tok_done")
        q_late_done = m.sem("r_q_late_done")
        q_spread_done = [m.sem(f"r_q_spread_done{i}") for i in range(2)]
        state_sum = m.sem("r_state_sum")
        state_done = m.sem("r_state_done")
        score_sum = m.sem("r_score_sum")
        score_done = m.sem("r_score_done")
        oT_sum = m.sem("r_oT_sum")
        oT_copied = m.sem("r_oT_copied")
        y_done = m.sem("r_y_done")
        x1_done = m.sem("r_x1_done")
        stats2_part = m.sem("r_stats2_part")
        stats2_done = m.sem("r_stats2_done")
        ve2_done = m.sem("r_ve2_done")
        rstd2_done = m.sem("r_rstd2_done")
        h2_done = m.sem("r_h2_done")
        h2_kept = m.sem("r_h2_kept")
        h2T_done = m.sem("r_h2T_done")
        h2T_copied = m.sem("r_h2T_copied")
        h2T_kept = m.sem("r_h2T_kept")
        logits_sum = m.sem("r_logits_sum")
        logits_kept = m.sem("r_logits_kept")

        zero_rows = m.sbuf("r_zero_rows", [P, ZERO_DMA])
        prepared = m.sem("r_prepared")
        LOADS = 10
        UNITS = TPS * RG
        block = m.ctx.enter_context(nc.Block())

        @block.sync
        def _(sp):
            for part, end in enumerate(X_PARTS):
                tiles = slice(TPS * X_PARTS[part - 1] if part else 0, TPS * end)
                sp.dma_start(x_sb[:, tiles], w["x"][:, tiles]).then_inc(x_loaded[part], 16)
                if part == 0:
                    for to, name in ((wq, "r_wq"), (wk, "r_wk"), (wv, "r_wv"), (ident, "ident"), (k_decay, "k_decay"),
                                     (q_decay, "q_decay"), (decay, "decay"), (own_head, "own_head"), (wo, "r_wo"),
                                     (router, "router")):
                        sp.dma_start(to[:], w[name]).then_inc(loaded, 16)
            sp.wait_ge(zeroed, 5)

            def spread_q(s, p, r):
                after(sp, qT_copied, s + 1)
                after(sp, score_sum, UNITS * (s - 1))
                for head in range(RH):
                    rows = slice(head * RD, (head + 1) * RD)
                    sp.dma_start(q_spread[rows, p, head, :], qT[rows, p, :]).then_inc(q_spread_done[p], 16)

            pipeline(sp, [(spread_q, 3)], B, 8)
            sp.wait_ge(loaded, 16 * LOADS)
            for done in q_spread_done:
                sp.wait_ge(done, 16 * RH * B // 2)

        @block.gpsimd
        def _(pool):
            nc.gpsimd.memset(zero_rows[:], 0.0).then_inc(zeroed, 1)
            nc.gpsimd.memset(half[:], -0.5).then_inc(zeroed, 1)
            nc.gpsimd.memset(eps[:], LN_EPS).then_inc(zeroed, 1)
            nc.gpsimd.memset(v_pad[:], 0.0).then_inc(zeroed, 1)
            nc.gpsimd.memset(q_spread[:], 0.0).then_inc(zeroed, 1)
            pool.wait_ge(zeroed, 5)

            def inv_std(s, p, mv, stats_done, ve, ve_done, rstd, done, used):
                after(pool, stats_done, s + 1)
                after(pool, done, s)
                nc.gpsimd.tensor_tensor(ve[:], mv[:, p, :, 1], eps[:], ALU.add).then_inc(ve_done, 1)
                after(pool, ve_done, s + 1)
                after(pool, used, s - 1)
                nc.gpsimd.tensor_tensor(rstd[:, p], ve[:], half[:], ALU.pow).then_inc(done, 1)

            def inv_std1(s, p, r):
                inv_std(s, p, mv1, stats1_done, ve1, ve1_done, rstd1, rstd1_done, h_done)

            def inv_std2(s, p, r):
                inv_std(s, p, mv2, stats2_done, ve2, ve2_done, rstd2, rstd2_done, h2_done)

            def keep_h2(s, p, r):
                after(pool, h2_done, s + 1)
                nc.gpsimd.tensor_copy(h2_all[:, bass.ds(s * TPS, TPS), :], h2[:, p]).then_inc(h2_kept, 1)

            def keep_h2T(s, p, r):
                after(pool, h2T_copied, s + 1)
                nc.gpsimd.tensor_copy(h2T_all[:, bass.ds(s * S, S)], h2T[:, p]).then_inc(h2T_kept, 1)

            def decay_q(s, p, r):
                after(pool, qT_copied, s + 1)
                after(pool, oT_sum, s - 1)
                nc.gpsimd.tensor_tensor(q_late[:, p], qT[:, p, P:], q_decay[:], ALU.mult).then_inc(q_late_done, 1)

            pipeline(pool, [(decay_q, 3), (keep_h2, 6), (keep_h2T, 6), (inv_std1, 0), (inv_std2, 5)], B, 8)

        @block.vector
        def _(dve):
            def stats1_of(s, p, r):
                if isinstance(s, int) and s < FIRST:
                    for part, end in enumerate(X_PARTS):
                        if s == (X_PARTS[part - 1] if part else 0) or s == FIRST - 1 and end > FIRST:
                            dve.wait_ge(x_loaded[part], 16)
                for t in range(TPS):
                    nc.vector.bn_stats(stats[:, 0, p, t], x_sb[:, s * TPS + t, :]).then_inc(stats1_part, 1)

            def settle1(s, p, r):
                after(dve, stats1_part, TPS * (s + 1))

            def moments1(s, p, r):
                for t in range(TPS):
                    ins = nc.vector.bn_aggr(mv1[:, p, t], stats[:, 0, p, t])
                ins.then_inc(stats1_done, 1)

            def norm1(s, p, r):
                after(dve, rstd1_done, s + 1)
                after(dve, hT_done, s - 1)
                for t in range(TPS):
                    ins = nc.vector.tensor_scalar(h[:, p, t], x_sb[:, s * TPS + t, :], mv1[:, p, t, 0:1],
                                                  rstd1[:, p, t:t + 1], ALU.subtract, ALU.mult)
                ins.then_inc(h_done, 1)

            def decayed(s, p, r):
                if isinstance(s, int) and s == 0:
                    dve.wait_ge(loaded, 16 * LOADS)
                after(dve, kv_done, s + 1)
                after(dve, v_copied, s + 1)
                after(dve, state_sum, s - 1)
                nc.vector.tensor_tensor(k_tok[:, p], ps_kv[:, 0], k_decay[:], ALU.mult).then_inc(k_tok_done, 1)

            def mask_state(s, p, r):
                after(dve, state_sum, s + 1)
                after(dve, oT_sum, s - 1)
                nc.vector.tensor_tensor(state[:, p], ps_state[:].rearrange("p (h e) -> p h e", h=RH), own_head[:],
                                        ALU.mult).then_inc(state_done, 1)

            def decay_scores(s, p, r):
                after(dve, oT_sum, s - 1)
                for u in range(UNITS):
                    after(dve, score_sum, UNITS * s + u + 1)
                    g = u % RG
                    nc.vector.tensor_tensor(score[:, p, u], ps_score[u % 2][:], decay[:, g * RQ:(g + 1) * RQ],
                                            ALU.mult).then_inc(score_done, 1)

            def residual(s, p, r):
                after(dve, y_done, s + 1)
                tiles = x_sb[:, bass.ds(s * TPS, TPS), :]
                nc.vector.tensor_tensor(tiles, tiles, ps_tail[:, 0:S].rearrange("p (t d) -> p t d", t=TPS),
                                        ALU.add).then_inc(x1_done, 1)

            def stats2_of(s, p, r):
                after_apart(dve, x1_done, s + 1, (loaded, 16 * LOADS))
                for t in range(TPS):
                    nc.vector.bn_stats(stats[:, 1, p, t], x_sb[:, s * TPS + t, :]).then_inc(stats2_part, 1)

            def settle2(s, p, r):
                after(dve, stats2_part, TPS * (s + 1))

            def moments2(s, p, r):
                for t in range(TPS):
                    ins = nc.vector.bn_aggr(mv2[:, p, t], stats[:, 1, p, t])
                ins.then_inc(stats2_done, 1)

            def norm2(s, p, r):
                after(dve, rstd2_done, s + 1)
                after(dve, h2T_done, s - 1)
                after(dve, h2_kept, s - 1)
                for t in range(TPS):
                    ins = nc.vector.tensor_scalar(h2[:, p, t], x_sb[:, s * TPS + t, :], mv2[:, p, t, 0:1],
                                                  rstd2[:, p, t:t + 1], ALU.subtract, ALU.mult)
                ins.then_inc(h2_done, 1)

            pipeline(dve, [(decayed, 3), (mask_state, 4), (decay_scores, 4), (residual, 5), (stats2_of, 5),
                           (stats1_of, 0), (settle2, 5), (settle1, 0), (norm1, 1), (moments2, 5), (moments1, 0),
                           (norm2, 5)], B, 8)

        @block.scalar
        def _(act):
            act.wait_ge(zeroed, 4)

            def prepare(s, p, r):
                if isinstance(s, int) and s == FIRST - 2:
                    nc.scalar.dma_start(keep["expert_up"][:], w["eu"]).then_inc(prepared, 16)
                    sorted_rows = keep["sorted_in"].rearrange("(p r) d -> p (r d)", p=P)
                    for at in range(0, NX * D, ZERO_DMA):
                        nc.scalar.dma_start(sorted_rows[:, at:at + ZERO_DMA], zero_rows[:]).then_inc(prepared, 16)

            def copy_qkv(s, p, r):
                after(act, qk_done, s + 1)
                after(act, q_spread_done[p], 16 * RH * r)
                after(act, q_late_done, s - 1)
                nc.scalar.mul(qT[:, p], ps_qk[:, 0], RD ** -0.5).then_inc(qT_copied, 1)
                after(act, score_sum, UNITS * (s - 1))
                nc.scalar.copy(kT[:, p], ps_qk[:, 1]).then_inc(kT_copied, 1)
                after(act, kv_done, s + 1)
                after(act, oT_sum, s - 1)
                nc.scalar.copy(v_pad[:, p, :, :, 0:RD],
                               ps_kv[:, 1:3].rearrange("p t (h e) -> p t h e", h=RH)).then_inc(v_copied, 1)

            def copy_oT(s, p, r):
                after(act, oT_sum, s + 1)
                after(act, y_done, s - 1)
                nc.scalar.copy(oT[:, p], ps_oT[:]).then_inc(oT_copied, 1)

            def copy_hT(s, p, r):
                after(act, hT_done, s + 1)
                after(act, kv_done, s - 1)
                nc.scalar.copy(hT[:, p], ps_hT[:]).then_inc(hT_copied, 1)

            def copy_h2T(s, p, r):
                after(act, h2T_done, s + 1)
                after(act, h2T_kept, s - 1)
                after(act, logits_sum, s - 1)
                nc.scalar.copy(h2T[:, p], ps_tail[:, 0:S]).then_inc(h2T_copied, 1)

            def copy_logits(s, p, r):
                after(act, logits_sum, s + 1)
                nc.scalar.copy(logits_all[:, bass.ds(s * TPS, TPS), :],
                               ps_tail[:, 0:TPS * NE].rearrange("p (t e) -> p t e", t=TPS)).then_inc(logits_kept, 1)

            pipeline(act, [(copy_qkv, 3), (copy_oT, 5), (copy_h2T, 6), (copy_hT, 2), (copy_logits, 6), (prepare, 0)], B, FIRST)
            act.wait_ge(prepared, 16 * (1 + NX * D // ZERO_DMA))

        @block.tensor
        def _(pe):
            pe.wait_ge(loaded, 16 * LOADS)

            def transpose_h(s, p, r):
                after(pe, h_done, s + 1)
                after(pe, hT_copied, s)
                for t in range(TPS):
                    ins = nc.tensor.transpose(ps_hT[:, t * P:(t + 1) * P], h[:, p, t], ident[:])
                ins.then_inc(hT_done, 1)

            def project(s, p, r):
                after(pe, hT_copied, s + 1)
                after(pe, qT_copied, s)
                after(pe, kT_copied, s)
                nc.tensor.matmul(ps_qk[:, 0], wq[:], hT[:, p], start=True, stop=True)
                nc.tensor.matmul(ps_qk[:, 1], wk[:], hT[:, p], start=True, stop=True).then_inc(qk_done, 1)
                after(pe, k_tok_done, s)
                after(pe, v_copied, s)
                nc.tensor.matmul(ps_kv[:, 0], hT[:, p, 0:P], wk[:], start=True, stop=True)
                for t in range(TPS):
                    ins = nc.tensor.matmul(ps_kv[:, 1 + t], hT[:, p, t * P:(t + 1) * P], wv[:], start=True, stop=True)
                ins.then_inc(kv_done, 1)

            def sum_state(s, p, r):
                after(pe, k_tok_done, s + 1)
                after(pe, v_copied, s + 1)
                after(pe, state_done, s)
                nc.tensor.matmul(ps_state[:], k_tok[:, p], v_pad[:, p, 0], start=True, stop=True).then_inc(state_sum, 1)

            def scores(units):
                def step(s, p, r):
                    after(pe, kT_copied, s + 1)
                    after(pe, q_spread_done[p], 16 * RH * (r + 1))
                    for u in units:
                        c, g = u // RG, u % RG
                        after(pe, score_done, UNITS * s + u - 1)
                        nc.tensor.matmul(ps_score[u % 2][:], kT[:, p, c * P:(c + 1) * P],
                                         q_spread[:, p, g * RQ:(g + 1) * RQ, c * P:(c + 1) * P],
                                         start=True, stop=True).then_inc(score_sum, 1)
                return step

            def sum_values(s, p, r):
                after(pe, q_late_done, s + 1)
                after(pe, state_done, s + 1)
                after(pe, score_done, UNITS * (s + 1))
                after(pe, oT_copied, s)
                last = P * (TPS - 1)
                for g in range(RG):
                    nc.tensor.matmul(ps_oT[:, g, last:], state[:, p, g * RQ:(g + 1) * RQ], q_late[:, p],
                                     start=g == 0, stop=False, skip_group_check=True)
                for c in range(TPS):
                    for g in range(RG):
                        for q in range(RQ):
                            rows = slice(q * RPAD, (q + 1) * RPAD)
                            ins = nc.tensor.matmul(ps_oT[rows, g, c * P:(c + 1) * P], v_pad[:, p, c, g * RQ + q],
                                                   score[:, p, c * RG + g, q], start=False,
                                                   stop=c == TPS - 1 and g == RG - 1, skip_group_check=True)
                ins.then_inc(oT_sum, 1)

            def output(s, p, r):
                after(pe, oT_copied, s + 1)
                after(pe, logits_kept, s)
                for t in range(TPS):
                    for g in range(RG):
                        ins = nc.tensor.matmul(ps_tail[:, t * D:(t + 1) * D], oT[:, p, g, t * P:(t + 1) * P], wo[:, g],
                                               start=g == 0, stop=g == RG - 1)
                ins.then_inc(y_done, 1)

            def transpose_h2(s, p, r):
                after(pe, h2_done, s + 1)
                after(pe, x1_done, s + 1)
                for t in range(TPS):
                    ins = nc.tensor.transpose(ps_tail[:, t * P:(t + 1) * P], h2[:, p, t], ident[:])
                ins.then_inc(h2T_done, 1)

            def route(s, p, r):
                after(pe, h2T_copied, s + 1)
                for t in range(TPS):
                    ins = nc.tensor.matmul(ps_tail[:, t * NE:(t + 1) * NE], h2T[:, p, t * P:(t + 1) * P], router[:],
                                           start=True, stop=True)
                ins.then_inc(logits_sum, 1)

            pipeline(pe, [(transpose_h2, 6), (transpose_h, 2), (sum_state, 4), (scores((0, 1)), 4), (route, 6),
                          (scores((2, 3)), 4), (output, 5), (project, 2), (sum_values, 4)], B, 8)


def constants():
    gamma = (1.0 - np.exp2(-5.0 - np.arange(RH))).astype(np.float32).astype(np.float64)
    i = np.arange(P)
    gap = i[None, :] - i[:, None]
    decay = np.where(gap >= 0, gamma[:, None, None] ** np.maximum(gap, 0), 0.0).transpose(1, 0, 2)
    head = np.arange(D) // RD
    q_decay = gamma[head][:, None] ** (i[None, :] + 1)
    k_decay = gamma[head][None, :] ** (P - 1 - i[:, None])
    own = np.zeros((P, RH, RPAD))
    for c in range(D):
        own[c, head[c], :RD] = 1.0
    f = lambda a: np.ascontiguousarray(a, dtype=np.float32)
    return {"decay": f(decay), "q_decay": f(q_decay), "k_decay": f(k_decay), "own_head": f(own),
            "ident": f(np.eye(P))}


def pad_heads(wo, size):
    groups = D // size * RPAD // P
    padded = np.zeros((groups, P // RPAD, RPAD, D), wo.dtype)
    padded[:, :, :size] = wo.reshape(groups, P // RPAD, size, D)
    return np.ascontiguousarray(padded.reshape(groups, P, D).transpose(1, 0, 2))


EB = EF // P
PAIR = 2


GATHERS = [range(0, 6)] + [range(6 + (NT - 6) * n // 8, 6 + (NT - 6) * (n + 1) // 8) for n in range(8)]


def gather_tiles(nc, keep, n):
    for t in GATHERS[n]:
        nc.gpsimd.indirect_dma_start(keep["h2"][:, t, :], None, keep["sorted_out"],
                                     bass.IndirectOffsetOnAxis(ap=keep["slot"][:, t:t + 1], axis=0)
                                     ).then_inc(keep["gathered"][n], 16)


def mixture_phase(nc, w, keep):
    with Memory(nc) as m:
        x_sb, h2_all, h2T_all, logits = keep["x"], keep["h2"], keep["h2T"], keep["logits"]
        ident, w_up = keep["ident"], keep["expert_up"]
        sorted_in, sorted_out = keep["sorted_in"], keep["sorted_out"]

        before = m.sbuf("m_before", [P, P])
        ones = m.sbuf("m_ones", [P, P])
        rank = m.sbuf("m_rank", [P, NE])
        tile_no = m.sbuf("m_tile_no", [1, NX])
        shared_up = m.sbuf("m_shared_up", [P, 2, EB, P])
        w_down = m.sbuf("m_expert_down", [P, NE, EB, D])
        shared_down = m.sbuf("m_shared_down", [P, EB, D])

        best = m.sbuf("m_best", [P, NT])
        score = m.sbuf("m_score", [P, NT])
        first = m.sbuf("m_first", [P, NT])
        chosen = m.sbuf("m_chosen", [P, NT, NE])
        work = m.sbuf("m_work", [P, NT, NE])
        total = m.sbuf("m_total", [P, NE, NT])
        running = m.sbuf("m_running", [P, NE, NT])
        same = m.sbuf("m_same", [P, NE, NT])
        count_i = m.sbuf("m_count_i", [P, NE], I32)
        tiles_i = m.sbuf("m_tiles_i", [P, NE], I32)
        tiles = m.sbuf("m_tiles", [P, NE])
        end = m.sbuf("m_end", [P, NE])
        base = m.sbuf("m_base", [P, NE])
        slot_f = m.sbuf("m_slot_f", [P, NT])
        slot = keep["slot"]
        reached = m.sbuf("m_reached", [1, NX, NE])
        expert_f = m.sbuf("m_expert_f", [1, NX])
        expert_i = m.sbuf("m_expert_i", [1, NX], I32)

        gate = m.sbuf("m_gate", [P, 2, EB, S])
        hidden = m.sbuf("m_hidden", [P, 2, EB, S])
        xe = m.sbuf("m_xe", [P, 2, PAIR, D])
        xeT = m.sbuf("m_xeT", [P, 2, PAIR, P])
        gate_e = m.sbuf("m_gate_e", [P, 2, PAIR, EF])
        hidden_e = m.sbuf("m_hidden_e", [P, 2, PAIR, EF])
        hiddenT_e = m.sbuf("m_hiddenT_e", [P, 2, PAIR, EB, P])
        ye = m.sbuf("m_ye", [P, 2, PAIR, D])

        banks = m.psum("m_banks", [P, 8, 512])
        bank = [banks[:, i] for i in range(8)]

        loaded = m.sem("m_loaded")
        tables = m.sem("m_tables")
        chain = m.sem("m_chain")
        best_done = m.sem("m_best_done")
        chosen_done = m.sem("m_chosen_done")
        counted = m.sem("m_counted")
        score_done = m.sem("m_score_done")
        slot_done = m.sem("m_slot_done")
        expert_done = m.sem("m_expert_done")
        scaled = m.sem("m_scaled")
        scattered = m.sem("m_scattered")
        up_done = m.sem("m_up_done")
        gate_done = m.sem("m_gate_done")
        hidden_done = m.sem("m_hidden_done")
        down_done = m.sem("m_down_done")
        shared_added = m.sem("m_shared_added")
        xe_loaded = [m.sem(f"m_xe_loaded{i}") for i in range(2)]
        xeT_done = m.sem("m_xeT_done")
        xeT_copied = m.sem("m_xeT_copied")
        up_e_done = m.sem("m_up_e_done")
        gate_e_done = m.sem("m_gate_e_done")
        hidden_e_done = m.sem("m_hidden_e_done")
        hiddenT_done = m.sem("m_hiddenT_done")
        hiddenT_copied = m.sem("m_hiddenT_copied")
        ye_done = m.sem("m_ye_done")
        ye_copied = m.sem("m_ye_copied")
        stored = [m.sem(f"m_stored{i}") for i in range(2)]

        PER_SCALE = 8
        LOADS = 6
        block = m.ctx.enter_context(nc.Block())

        @block.sync
        def _(sp):
            for to, name in ((before, "before"), (rank, "rank"), (tile_no, "tile_no"), (shared_up, "shared_up"),
                             (shared_down, "shared_down"), (w_down, "ed")):
                sp.dma_start(to[:], w[name]).then_inc(loaded, 16)
            sp.wait_ge(scattered, 16 * NT)

            def load(t, p, r):
                after(sp, xeT_done, t - 1)
                sp.dma_start(xe[:, p], sorted_in[bass.ds(t * PAIR * P, PAIR * P), :].rearrange("(j p) d -> p j d", p=P)
                             ).then_inc(xe_loaded[p], 16)

            def store(t, p, r):
                after(sp, ye_copied, t + 1)
                sp.dma_start(sorted_out[bass.ds(t * PAIR * P, PAIR * P), :].rearrange("(j p) d -> p j d", p=P), ye[:, p]
                             ).then_inc(stored[p], 16)

            pipeline(sp, [(load, 0), (store, 6)], NX // PAIR, 8)
            for s in stored:
                sp.wait_ge(s, 16 * NX // PAIR // 2)
            for s in xe_loaded:
                sp.wait_ge(s, 16 * NX // PAIR // 2)
            sp.wait_ge(loaded, 16 * LOADS)

        @block.gpsimd
        def _(pool):
            nc.gpsimd.memset(ones[:], 1.0).then_inc(tables, 1)
            nc.gpsimd.memset(same[:], 1.0).then_inc(tables, 1)
            pool.wait_ge(tables, 2)
            nc.gpsimd.memset(same[:, :, 0:1], 0.0).then_inc(tables, 1)
            pool.wait_ge(slot_done, 1)
            for t in range(NT):
                if t % PER_SCALE == 0:
                    pool.wait_ge(scaled, t // PER_SCALE + 1)
                nc.gpsimd.indirect_dma_start(sorted_in, bass.IndirectOffsetOnAxis(ap=slot[:, t:t + 1], axis=0),
                                             h2_all[:, t, :], None).then_inc(scattered, 16)
            pool.wait_ge(scattered, 16 * NT)
            for s in stored:
                pool.wait_ge(s, 16 * NX // PAIR // 2)
            gather_tiles(nc, keep, 0)

        @block.vector
        def _(dve):
            steps = [0]

            def chained(ins):
                steps[0] += 1
                ins.then_inc(chain, 1)
                dve.wait_ge(chain, steps[0])

            over_experts = lambda a: a.unsqueeze(2).to_broadcast([P, NT, NE])
            over_tiles = lambda a: a.unsqueeze(1).to_broadcast([P, NT, NE])
            nc.vector.tensor_reduce(best[:], logits[:], AX.X, ALU.max).then_inc(best_done, 1)
            dve.wait_ge(best_done, 1)
            dve.wait_ge(loaded, 16 * LOADS)
            chained(nc.vector.tensor_tensor(work[:], logits[:], over_experts(best[:]), ALU.is_equal))
            chained(nc.vector.tensor_tensor(work[:], work[:], over_tiles(rank[:]), ALU.mult))
            chained(nc.vector.tensor_reduce(first[:], work[:], AX.X, ALU.max))
            nc.vector.tensor_tensor(chosen[:], over_tiles(rank[:]), over_experts(first[:]),
                                    ALU.is_equal).then_inc(chosen_done, 1)
            dve.wait_ge(counted, 2)
            dve.wait_ge(tables, 3)
            for half in range(2):
                ins = nc.vector.tensor_copy(total[:, :, half * NT // 2:(half + 1) * NT // 2],
                                            bank[2 + half].rearrange("p (t e) -> p e t", e=NE))
            chained(ins)
            flat = lambda a: a[:].rearrange("p e t -> p (e t)")
            chained(nc.vector.tensor_tensor_scan(flat(running), flat(same), flat(total), 0.0, ALU.mult, ALU.add))
            chained(nc.vector.tensor_scalar(count_i[:], running[:, :, NT - 1], float(P - 1), None, ALU.add))
            chained(nc.vector.tensor_scalar(tiles_i[:], count_i[:], P.bit_length() - 1, None, ALU.arith_shift_right))
            chained(nc.vector.tensor_copy(tiles[:], tiles_i[:]))
            chained(nc.vector.tensor_tensor_scan(end[:], ones[:, 0:NE], tiles[:], 0.0, ALU.mult, ALU.add))
            chained(nc.vector.tensor_tensor(base[:], end[:], tiles[:], ALU.subtract))
            chained(nc.vector.tensor_scalar(base[:], base[:], float(P), None, ALU.mult))
            chained(nc.vector.tensor_tensor(running[:], running[:], total[:], ALU.subtract))
            chained(nc.vector.tensor_tensor(running[:], running[:], base[:].unsqueeze(2).to_broadcast([P, NE, NT]),
                                            ALU.add))
            for half in range(2):
                ts = slice(half * NT // 2, (half + 1) * NT // 2)
                ins = nc.vector.tensor_tensor(work[:, ts], bank[half].rearrange("p (t e) -> p t e", e=NE),
                                              running[:, :, ts].rearrange("p e t -> p t e"), ALU.add)
            chained(ins)
            chained(nc.vector.tensor_tensor(work[:], work[:], chosen[:], ALU.mult))
            chained(nc.vector.tensor_reduce(slot_f[:], work[:], AX.X, ALU.add))
            nc.vector.tensor_copy(slot[:], slot_f[:]).then_inc(slot_done, 1)
            dve.wait_ge(score_done, 1)
            for t in range(0, NT, PER_SCALE):
                some = h2_all[:, t:t + PER_SCALE, :]
                nc.vector.tensor_tensor(some, some, score[:, t:t + PER_SCALE].unsqueeze(2).to_broadcast([P, PER_SCALE, D]),
                                        ALU.mult).then_inc(scaled, 1)
            chained(nc.vector.tensor_tensor(reached[:], tile_no[:].unsqueeze(2).to_broadcast([1, NX, NE]),
                                            end[0:1].unsqueeze(1).to_broadcast([1, NX, NE]), ALU.is_ge))
            chained(nc.vector.tensor_reduce(expert_f[:], reached[:], AX.X, ALU.add))
            nc.vector.tensor_scalar(expert_i[:], expert_f[:], float(NE - 1), None, ALU.min).then_inc(expert_done, 1)

            def gated(s, p, r):
                after(dve, gate_done, s + 1)
                after(dve, down_done, s - 1)
                nc.vector.tensor_tensor(hidden[:, p], gate[:, p], bank[2 + p].rearrange("p (f s) -> p f s", f=EB),
                                        ALU.mult).then_inc(hidden_done, 1)

            def add_shared(s, p, r):
                after(dve, down_done, s + 1)
                some = x_sb[:, bass.ds(s * TPS, TPS), :]
                nc.vector.tensor_tensor(some, some, bank[4 + p][:, 0:S].rearrange("p (t d) -> p t d", t=TPS),
                                        ALU.add).then_inc(shared_added, 1)

            pipeline(dve, [(gated, 1), (add_shared, 3)], B, 4)

            def gated_e(t, p, r):
                after(dve, gate_e_done, t + 1)
                after(dve, hiddenT_done, t - 1)
                nc.vector.tensor_tensor(hidden_e[:, p], gate_e[:, p], banks[:, PAIR * p:PAIR * (p + 1), EF:], ALU.mult
                                        ).then_inc(hidden_e_done, 1)

            def copy_hiddenT(t, p, r):
                after(dve, hiddenT_done, t + 1)
                after(dve, ye_done, t - 1)
                nc.vector.tensor_copy(hiddenT_e[:, p], bank[4].rearrange("p (j f s) -> p j f s", j=PAIR, f=EB)
                                      ).then_inc(hiddenT_copied, 1)

            pipeline(dve, [(gated_e, 3), (copy_hiddenT, 4)], NX // PAIR, 8)

        @block.scalar
        def _(act):
            act.wait_ge(best_done, 1)
            nc.scalar.activation(score[:], best[:], ACT.Sigmoid).then_inc(score_done, 1)
            nc.scalar.preload_act_table(ACT.Silu)

            def gate_of(s, p, r):
                after(act, up_done, s + 1)
                after(act, hidden_done, s - 1)
                nc.scalar.activation(gate[:, p], bank[p].rearrange("p (f s) -> p f s", f=EB), ACT.Silu
                                     ).then_inc(gate_done, 1)

            pipeline(act, [(gate_of, 1)], B, 4)

            def copy_xeT(t, p, r):
                after(act, xeT_done, t + 1)
                after(act, up_e_done, t - 1)
                nc.scalar.copy(xeT[:, p], bank[6][:, 0:PAIR * P].rearrange("p (j s) -> p j s", j=PAIR)).then_inc(xeT_copied, 1)

            def gate_of_e(t, p, r):
                after(act, up_e_done, t + 1)
                after(act, hidden_e_done, t - 1)
                nc.scalar.activation(gate_e[:, p], banks[:, PAIR * p:PAIR * (p + 1), 0:EF], ACT.Silu).then_inc(gate_e_done, 1)

            def copy_ye(t, p, r):
                after(act, ye_done, t + 1)
                after(act, stored[p], 16 * r)
                nc.scalar.copy(ye[:, p], bank[5][:, 0:PAIR * D].rearrange("p (j d) -> p j d", j=PAIR)).then_inc(ye_copied, 1)

            pipeline(act, [(gate_of_e, 3), (copy_xeT, 1), (copy_ye, 6)], NX // PAIR, 8)

        @block.tensor
        def _(pe):
            pe.wait_ge(loaded, 16 * LOADS)
            pe.wait_ge(tables, 2)
            pe.wait_ge(chosen_done, 1)
            for to, table in ((0, before), (2, ones)):
                for half in range(2):
                    ins = nc.tensor.matmul(bank[to + half], table[:], chosen[:, half * NT // 2:(half + 1) * NT // 2],
                                           start=True, stop=True)
                ins.then_inc(counted, 1)
            pe.wait_ge(slot_done, 1)

            def up(s, p, r):
                after(pe, gate_done, s - 1)
                after(pe, hidden_done, s - 1)
                for which in range(2):
                    for f in range(EB):
                        ins = nc.tensor.matmul(bank[2 * which + p][:, f * S:(f + 1) * S], shared_up[:, which, f],
                                               h2T_all[:, bass.ds(s * S, S)], start=True, stop=True)
                ins.then_inc(up_done, 1)

            def down(s, p, r):
                after(pe, hidden_done, s + 1)
                after(pe, shared_added, s - 1)
                for t in range(TPS):
                    for f in range(EB):
                        ins = nc.tensor.matmul(bank[4 + p][:, t * D:(t + 1) * D], hidden[:, p, f, t * P:(t + 1) * P],
                                               shared_down[:, f], start=f == 0, stop=f == EB - 1)
                ins.then_inc(down_done, 1)

            pipeline(pe, [(up, 0), (down, 2)], B, 4)
            pe.wait_ge(shared_added, B)
            pe.wait_ge(expert_done, 1)

            def transpose_xe(t, p, r):
                after(pe, xe_loaded[p], 16 * (r + 1))
                after(pe, xeT_copied, t)
                for j in range(PAIR):
                    ins = nc.tensor.transpose(bank[6][:, j * P:(j + 1) * P], xe[:, p, j], ident[:])
                ins.then_inc(xeT_done, 1)

            def up_e(t, p, r):
                expert = [pe.value_load(expert_i[0:1, bass.ds(t * PAIR + j, 1)], min_val=0, max_val=NE - 1)
                          for j in range(PAIR)]
                after(pe, xeT_copied, t + 1)
                after(pe, hidden_e_done, t - 1)
                for j in range(PAIR):
                    ins = nc.tensor.matmul(bank[PAIR * p + j], xeT[:, p, j], w_up[:, expert[j]], start=True, stop=True)
                ins.then_inc(up_e_done, 1)

            def transpose_hidden(t, p, r):
                after(pe, hidden_e_done, t + 1)
                after(pe, hiddenT_copied, t)
                for j in range(PAIR):
                    for f in range(EB):
                        ins = nc.tensor.transpose(bank[4][:, (j * EB + f) * P:(j * EB + f + 1) * P],
                                                  hidden_e[:, p, j, f * P:(f + 1) * P], ident[:])
                ins.then_inc(hiddenT_done, 1)

            def down_e(t, p, r):
                expert = [pe.value_load(expert_i[0:1, bass.ds(t * PAIR + j, 1)], min_val=0, max_val=NE - 1)
                          for j in range(PAIR)]
                after(pe, hiddenT_copied, t + 1)
                after(pe, ye_copied, t)
                for j in range(PAIR):
                    for f in range(EB):
                        ins = nc.tensor.matmul(bank[5][:, j * D:(j + 1) * D], hiddenT_e[:, p, j, f],
                                               w_down[:, expert[j], f], start=f == 0, stop=f == EB - 1)
                ins.then_inc(ye_done, 1)

            pipeline(pe, [(transpose_xe, 1), (transpose_hidden, 4), (up_e, 2), (down_e, 5)], NX // PAIR, 8)


def constants2():
    i = np.arange(P)
    f = lambda a: np.ascontiguousarray(a, dtype=np.float32)
    return {"before": f(i[:, None] < i[None, :]), "rank": f(np.broadcast_to(NE - np.arange(NE), (P, NE))),
            "tile_no": f(np.arange(NX)[None, :])}


AH, AD = 16, D // 16
HALVES = 2
HH = AH // HALVES
PARTS = 3
PAIRS = PARTS * PARTS
QK_ROWS = PAIRS * AD
EXP_ROWS = QK_ROWS + PARTS
UNIT = 4
M_UNITS = AH // UNIT * TPS
PT_RING = 4
APAD = 32
AG = AH // 4

ROUNDS = 10

SLOT_OF = {}
for _i in range(2 * M_UNITS):
    SLOT_OF["me"[_i % 2], _i // 2] = 1 if _i == 2 * M_UNITS - 1 else _i % 3


def last_user(kind, slot, at):
    for back in range(1, 2 * M_UNITS + 1):
        i = at - back
        j = i % (2 * M_UNITS)
        if "me"[j % 2] == kind and SLOT_OF[kind, j // 2] == slot:
            return (0 if i >= 0 else 1), j // 2
    raise ValueError(slot)


def twice(half_factor, n):
    return n * half_factor * 2


def after_most(engine, sem, count, most):
    after(engine, sem, min(count, most) if isinstance(count, int) else count)


def attention_phase(nc, w, keep, out):
    with Memory(nc) as m:
        x_sb, given = keep["x"], keep["h2"]
        ident = keep["ident"]
        gathered = keep["gathered"]

        wq = m.sbuf("a_wq", [P, D])
        wk = m.sbuf("a_wk", [P, D])
        wv = m.sbuf("a_wv", [P, D])
        wo = m.sbuf("a_wo", [P, D])
        bq = m.sbuf("a_bq", [P, 1])
        bk = m.sbuf("a_bk", [P, 1])
        bq_scaled = m.sbuf("a_bq_scaled", [P, 1])
        bv = m.sbuf("a_bv", [P, D])
        bo = m.sbuf("a_bo", [P, D])
        ident_b = m.sbuf("a_ident_b", [P, P], BF16)
        zeros = m.sbuf("a_zeros", [P, 1])
        half_pow = m.sbuf("a_half_pow", [P, TPS])
        eps = m.sbuf("a_eps", [P, TPS])
        ones_b = m.sbuf("a_ones_b", [PARTS, HH, S], BF16)

        stats = m.sbuf("a_stats", [P, 2, TPS, 6])
        mv = m.sbuf("a_mv", [P, 2, TPS, 2])
        ve = m.sbuf("a_ve", [P, TPS])
        rstd = m.sbuf("a_rstd", [P, 2, TPS])
        h = m.sbuf("a_h", [P, 2, TPS, D])
        hT = m.sbuf("a_hT", [P, 2, S])
        qk = m.sbuf("a_qk", [P, 2, 2, S])
        rest = m.sbuf("a_rest", [P, 2, S])
        part = m.sbuf("a_part", [P, 2, 2, PARTS, S], BF16)
        part_dram = nc.dram_tensor("part_dram", (2, HALVES, 2, PARTS, HH * AD, S), BF16, kind="Internal").ap()
        max_dram = nc.dram_tensor("max_dram", (2, HALVES, PARTS * HH * S), BF16, kind="Internal").ap()
        q_stack = m.sbuf("a_q_stack", [P, 2, HALVES, HH, S], BF16)
        k_stack = m.sbuf("a_k_stack", [P, 2, HALVES, HH, S], BF16)
        v_tok = m.sbuf("a_v_tok", [P, 2, TPS, D])
        v_pad = m.sbuf("a_v_pad", [P, 2, TPS, AH, APAD])
        neg_max = m.sbuf("a_neg_max", [P, 2, HALVES, TPS, HH])
        max_rest = m.sbuf("a_max_rest", [P, TPS, HH])
        max_part = m.sbuf("a_max_part", [P, HALVES, TPS, PARTS, HH], BF16)
        max_T = m.sbuf("a_max_T", [PARTS * HH, HALVES, S], BF16)
        pT = m.sbuf("a_pT", [P, PT_RING, UNIT, S])
        oT_pad = m.sbuf("a_oT_pad", [P, AG, S])
        inv_sum = m.sbuf("a_inv_sum", [P, TPS, AH])
        o_tok = m.sbuf("a_o_tok", [P, 2, TPS, AH, AD])
        oT = m.sbuf("a_oT", [P, 2, S])

        router = m.sbuf("e_router", [P, D])
        stats3 = m.sbuf("e_stats", [P, 2, TPS, 6])
        mv3 = m.sbuf("e_mv", [P, 2, TPS, 2])
        ve3 = m.sbuf("e_ve", [P, TPS])
        minus_mean = m.sbuf("e_minus_mean", [P, TPS])
        rstd3 = m.sbuf("e_rstd", [P, 2, TPS])
        shift = m.sbuf("e_shift", [P, 2, TPS])
        h3 = m.sbuf("e_h", [P, 2, TPS, D])
        product = m.sbuf("e_product", [P, 2, TPS, D])
        x_plus_h = m.sbuf("e_x_plus_h", [P, 2, TPS, D])
        w_tok = keep["w_tok"]

        slots = [m.psum(f"a_slot{i}", [P, UNIT, S]) for i in range(3)]
        ps_o = m.psum("a_ps_o", [P, 2, S])
        ps_misc = m.psum("a_ps_misc", [P, 512])

        loaded = m.sem("a_loaded")
        preset = m.sem("a_preset")
        preset_v = m.sem("a_preset_v")
        ones_in = m.sem("a_ones_in")
        biased = m.sem("a_biased")
        added = m.sem("a_added")
        stats_part = m.sem("a_stats_part")
        stats_done = m.sem("a_stats_done")
        ve_done = m.sem("a_ve_done")
        rstd_done = m.sem("a_rstd_done")
        h_done = m.sem("a_h_done")
        hT_done = m.sem("a_hT_done")
        hT_copied = m.sem("a_hT_copied")
        qk_done = m.sem("a_qk_done")
        qk_copied = m.sem("a_qk_copied")
        v_done = m.sem("a_v_done")
        v_copied = m.sem("a_v_copied")
        v_padded = m.sem("a_v_padded")
        part_step = m.sem("a_part_step")
        part_stored = [[m.sem(f"a_part_stored{i}{j}") for j in range(2)] for i in range(2)]
        max_stored = [[m.sem(f"a_max_stored{i}{j}") for j in range(2)] for i in range(2)]
        filled = [[m.sem(f"a_filled{i}{j}") for j in range(2)] for i in range(2)]
        m_filled = m.sem("a_m_filled")
        m_read = m.sem("a_m_read")
        max_step = m.sem("a_max_step")
        maxT_done = m.sem("a_maxT_done")
        maxT_copied = m.sem("a_maxT_copied")
        max_in = [[m.sem(f"a_max_in{i}{j}") for j in range(2)] for i in range(2)]
        e_filled = m.sem("a_e_filled")
        e_read = m.sem("a_e_read")
        o_done = m.sem("a_o_done")
        o_copied = m.sem("a_o_copied")
        otok_done = m.sem("a_otok_done")
        inv_done = m.sem("a_inv_done")
        otok_copied = m.sem("a_otok_copied")
        oT_done = m.sem("a_oT_done")
        oT_copied = m.sem("a_oT_copied")
        y_done = m.sem("a_y_done")
        y_added = m.sem("a_y_added")
        stats3_part = m.sem("e_stats_part")
        stats3_done = m.sem("e_stats_done")
        ve3_done = m.sem("e_ve_done")
        rstd3_done = m.sem("e_rstd_done")
        shift_done = m.sem("e_shift_done")
        h3_done = m.sem("e_h_done")
        product_done = m.sem("e_product_done")
        w_done = m.sem("e_w_done")
        out_done = m.sem("e_out_done")
        x_stored = [m.sem(f"e_x_stored{i}") for i in range(2)]
        out_stored = [m.sem(f"e_out_stored{i}") for i in range(2)]

        LOADS = 9
        FILLS = PARTS + 1
        ALL_M, ALL_E = M_UNITS * B, M_UNITS * B
        SCALE = AD ** -0.5
        block = m.ctx.enter_context(nc.Block())

        @block.sync
        def _(sp):
            for to, name in ((wq, "a_wq"), (wk, "a_wk"), (wv, "a_wv"), (wo, "a_wo"), (bq, "a_bq"), (bk, "a_bk"),
                             (bv, "a_bv"), (bo, "a_bo"), (router, "d_rw")):
                sp.dma_start(to[:], w[name]).then_inc(loaded, 16)
            sp.wait_ge(preset, 4)
            for p in range(2):
                for half in range(HALVES):
                    sp.dma_start(k_stack[QK_ROWS:EXP_ROWS, p, half], ones_b[:]).then_inc(ones_in, 16)

            def store_parts(s, p, r):
                after(sp, part_step, 8 * (s + 1))
                for half in range(HALVES):
                    after(sp, filled[p][half], twice(8 * FILLS, r))
                    rows = slice(half * HH * AD, (half + 1) * HH * AD)
                    sp.dma_start(part_dram[p, half].rearrange("w a r s -> r (w a) s"),
                                 part[rows, p].rearrange("r w a s -> r (w a) s")).then_inc(part_stored[p][half], 16)

            def fill(half):
                def step(s, p, r):
                    after(sp, part_stored[p][half], 16 * (r + 1))
                    after(sp, e_filled, ((s - 2) * 4 + 2 * half + 2) * (M_UNITS // 8) * 2)
                    for a in range(PARTS):
                        sp.dma_start(q_stack[a * PARTS * AD:(a + 1) * PARTS * AD, p, half],
                                     part_dram[p, half, 0, a].rearrange("(d h) s -> d (h s)", d=AD).unsqueeze(0)
                                     .to_broadcast([PARTS, AD, HH * S])).then_inc(filled[p][half], 16)
                    sp.dma_start(k_stack[0:QK_ROWS, p, half],
                                 part_dram[p, half, 1].rearrange("b (d h) s -> (b d) (h s)", d=AD).unsqueeze(0)
                                 .to_broadcast([PARTS, PARTS * AD, HH * S])).then_inc(filled[p][half], 16)
                return step

            def store_max(half):
                def step(s, p, r):
                    after(sp, maxT_copied, HALVES * s + half + 1)
                    after(sp, max_in[p][half], 16 * r)
                    sp.dma_start(max_dram[p, half].rearrange("(c s) -> c s", s=S), max_T[:, half]
                                 ).then_inc(max_stored[p][half], 16)
                return step

            def fill_max(half):
                def step(s, p, r):
                    after(sp, max_stored[p][half], 16 * (r + 1))
                    sp.dma_start(q_stack[QK_ROWS:EXP_ROWS, p, half],
                                 max_dram[p, half].rearrange("(a n) -> a n", a=PARTS)).then_inc(max_in[p][half], 16)
                return step

            by_token = lambda rows, s: rows[bass.ds(s * S, S), :].rearrange("(t p) d -> p t d", p=P)

            def store_x(s, p, r):
                after(sp, y_added, s + 1)
                sp.dma_start(by_token(keep["x_rows"], s), x_sb[:, bass.ds(s * TPS, TPS), :]).then_inc(x_stored[p], 16)

            def store_out(s, p, r):
                after(sp, out_done, s + 1)
                sp.dma_start(by_token(out, s), x_plus_h[:, p]).then_inc(out_stored[p], 16)

            pipeline(sp, [(fill(1), 3), (store_max(1), 4), (fill_max(1), 4), (store_parts, 2), (fill(0), 2),
                          (store_x, 7), (store_out, 8), (store_max(0), 3), (fill_max(0), 3)], B, ROUNDS)
            for p in range(2):
                sp.wait_ge(x_stored[p], 16 * B // 2)
                sp.wait_ge(out_stored[p], 16 * B // 2)
            for p in range(2):
                for half in range(HALVES):
                    sp.wait_ge(filled[p][half], 16 * FILLS * B // 2)
                    sp.wait_ge(max_in[p][half], 16 * B // 2)

        @block.gpsimd
        def _(pool):
            nc.gpsimd.memset(half_pow[:], -0.5).then_inc(preset, 1)
            nc.gpsimd.memset(eps[:], LN_EPS).then_inc(preset, 1)
            nc.gpsimd.memset(zeros[:], 0.0).then_inc(preset, 1)
            nc.gpsimd.memset(ones_b[:], 1.0).then_inc(preset, 1)
            pool.wait_ge(preset, 4)
            pool.wait_ge(loaded, 16 * LOADS)
            pool.wait_ge(preset_v, 3)

            def bias(s, p, r):
                after(pool, h_done, s + 1)
                some = x_sb[:, bass.ds(s * TPS, TPS), :]
                nc.gpsimd.tensor_tensor(some, some, bo[:].unsqueeze(1).to_broadcast([P, TPS, D]), ALU.add
                                        ).then_inc(biased, 1)

            def inv_std(s, p, r):
                after(pool, stats_done, s + 1)
                after(pool, rstd_done, s)
                nc.gpsimd.tensor_tensor(ve[:], mv[:, p, :, 1], eps[:], ALU.add).then_inc(ve_done, 1)
                after(pool, ve_done, s + 1)
                after(pool, h_done, s - 1)
                nc.gpsimd.tensor_tensor(rstd[:, p], ve[:], half_pow[:], ALU.pow).then_inc(rstd_done, 1)

            def split(steps, at, value, left, high, mid, low, shape):
                none = zeros[:].unsqueeze(1).to_broadcast(shape) if len(shape) == 3 else zeros[:].to_broadcast(shape)
                for n, (to, a, b, op) in enumerate(((high, value, none, ALU.add), (left, value, high, ALU.subtract),
                                                    (mid, left, none, ALU.add), (low, left, mid, ALU.subtract))):
                    nc.gpsimd.tensor_tensor(to, a, b, op).then_inc(steps, 1)
                    after(pool, steps, at + n + 1)

            def split_qk(s, p, r):
                after(pool, qk_copied, s + 1)
                for half in range(HALVES):
                    after(pool, part_stored[p][half], 16 * r)
                for which in range(2):
                    split(part_step, 8 * s + 4 * which, qk[:, p, which], rest[:, which], part[:, p, which, 0],
                          part[:, p, which, 1], part[:, p, which, 2], [P, S])

            def split_max(half):
                def step(s, p, r):
                    after(pool, m_read, M_UNITS * s + (half + 1) * M_UNITS // 2)
                    after(pool, maxT_done, HALVES * (s - 1) + half + 1)
                    split(max_step, 8 * s + 4 * half, neg_max[:, p, half], max_rest[:], max_part[:, half, :, 0],
                          max_part[:, half, :, 1], max_part[:, half, :, 2], [P, TPS, HH])
                return step

            def pad_v(s, p, r):
                after(pool, v_copied, s + 1)
                after(pool, o_done, AG * (s - 1))
                nc.gpsimd.tensor_tensor(v_pad[:, p, :, :, 0:AD].rearrange("p t h e -> p (t h) e"),
                                        v_tok[:, p].rearrange("p t (h e) -> p (t h) e", h=AH),
                                        zeros[:].unsqueeze(1).to_broadcast([P, TPS * AH, AD]), ALU.add
                                        ).then_inc(v_padded, 1)

            def inv_std3(s, p, r):
                after(pool, stats3_done, s + 1)
                after(pool, rstd3_done, s)
                nc.gpsimd.tensor_tensor(ve3[:], mv3[:, p, :, 1], eps[:], ALU.add).then_inc(ve3_done, 1)
                after(pool, shift_done, s)
                nc.gpsimd.tensor_tensor(minus_mean[:], zeros[:].to_broadcast([P, TPS]), mv3[:, p, :, 0], ALU.subtract
                                        ).then_inc(ve3_done, 1)
                after(pool, ve3_done, 2 * (s + 1))
                after(pool, h3_done, s - 1)
                nc.gpsimd.tensor_tensor(rstd3[:, p], ve3[:], half_pow[:], ALU.pow).then_inc(rstd3_done, 1)
                after(pool, rstd3_done, s + 1)
                nc.gpsimd.tensor_tensor(shift[:, p], minus_mean[:], rstd3[:, p], ALU.mult).then_inc(shift_done, 1)

            def weigh(s, p, r):
                after(pool, h3_done, s + 1)
                after(pool, w_done, s - 1)
                nc.gpsimd.tensor_tensor(product[:, p], h3[:, p], router[:].unsqueeze(1).to_broadcast([P, TPS, D]),
                                        ALU.mult).then_inc(product_done, 1)
                after(pool, out_stored[p], 16 * r)
                nc.gpsimd.tensor_tensor(x_plus_h[:, p], x_sb[:, bass.ds(s * TPS, TPS), :], h3[:, p], ALU.add
                                        ).then_inc(out_done, 1)

            def gather_more(s, p, r):
                if isinstance(s, int) and s < 8:
                    gather_tiles(nc, keep, s + 1)

            pipeline(pool, [(gather_more, 0), (split_max(1), 4), (bias, 1), (split_qk, 2), (pad_v, 3), (split_max(0), 3), (inv_std3, 6), (weigh, 7),
                            (inv_std, 0)], B, ROUNDS)

        @block.vector
        def _(dve):
            nc.vector.memset(v_pad[:], 0.0).then_inc(preset_v, 1)
            dve.wait_ge(preset_v, 1)
            nc.vector.memset(v_pad[:, :, :, :, AD:AD + 1], 1.0).then_inc(preset_v, 1)
            dve.wait_ge(loaded, 16 * LOADS)
            nc.vector.tensor_copy(ident_b[:], ident[:])
            nc.vector.tensor_scalar(bq_scaled[:], bq[:], SCALE, None, ALU.mult).then_inc(preset_v, 1)

            def add_given(s, p, r):
                if isinstance(s, int) and s < 8:
                    for n, tiles in enumerate(GATHERS):
                        if s * TPS <= tiles[-1] and (tiles[0] < (s + 1) * TPS or s == 7):
                            dve.wait_ge(gathered[n], 16 * len(tiles))
                some = x_sb[:, bass.ds(s * TPS, TPS), :]
                nc.vector.tensor_tensor(some, some, given[:, bass.ds(s * TPS, TPS), :], ALU.add).then_inc(added, 1)

            def given_added(s, p, r):
                after(dve, added, s + 1)

            def stats_of(s, p, r):
                for t in range(TPS):
                    nc.vector.bn_stats(stats[:, p, t], x_sb[:, s * TPS + t, :]).then_inc(stats_part, 1)

            def settle(s, p, r):
                after(dve, stats_part, TPS * (s + 1))

            def moments(s, p, r):
                for t in range(TPS):
                    ins = nc.vector.bn_aggr(mv[:, p, t], stats[:, p, t])
                ins.then_inc(stats_done, 1)

            def norm(s, p, r):
                after(dve, rstd_done, s + 1)
                after(dve, hT_done, s - 1)
                for t in range(TPS):
                    ins = nc.vector.tensor_scalar(h[:, p, t], x_sb[:, s * TPS + t, :], mv[:, p, t, 0:1],
                                                  rstd[:, p, t:t + 1], ALU.subtract, ALU.mult)
                ins.then_inc(h_done, 1)

            def maximum(j):
                half, t, g = j // 4, j % 4 // 2, j % 2
                def step(s, p, r):
                    after(dve, m_filled, M_UNITS * s + j + 1)
                    if j % 4 == 0:
                        after(dve, max_step, 8 * (s - 2) + 4 * half + 4)
                    nc.vector.tensor_reduce(neg_max[:, p, half, t, g * UNIT:(g + 1) * UNIT], slots[SLOT_OF["m", j]][:],
                                            AX.X, ALU.max, negate=True).then_inc(m_read, 1)
                return step

            def normalise(t):
                def step(s, p, r):
                    after(dve, otok_done, TPS * s + t + 1)
                    o = ps_misc[:].rearrange("p (h e) -> p h e", h=AH)
                    nc.vector.reciprocal(inv_sum[:, t], o[:, :, AD]).then_inc(inv_done, 1)
                    after(dve, inv_done, TPS * s + t + 1)
                    if t == 0:
                        after(dve, oT_done, s - 1)
                    nc.vector.tensor_tensor(o_tok[:, p, t], o[:, :, 0:AD],
                                            inv_sum[:, t].unsqueeze(2).to_broadcast([P, AH, AD]), ALU.mult
                                            ).then_inc(otok_copied, 1)
                return step

            def copy_v(s, p, r):
                after(dve, v_done, s + 1)
                after(dve, v_padded, s - 1)
                nc.vector.tensor_tensor(v_tok[:, p], ps_misc[:, 0:S].rearrange("p (t d) -> p t d", t=TPS),
                                        bv[:].unsqueeze(1).to_broadcast([P, TPS, D]), ALU.add).then_inc(v_copied, 1)

            def add_y(s, p, r):
                after(dve, biased, s + 1)
                after(dve, y_done, s + 1)
                some = x_sb[:, bass.ds(s * TPS, TPS), :]
                nc.vector.tensor_tensor(some, some, ps_misc[:, 0:S].rearrange("p (t d) -> p t d", t=TPS), ALU.add
                                        ).then_inc(y_added, 1)

            def y_is_added(s, p, r):
                after(dve, y_added, s + 1)

            def stats3_of(s, p, r):
                for t in range(TPS):
                    nc.vector.bn_stats(stats3[:, p, t], x_sb[:, s * TPS + t, :]).then_inc(stats3_part, 1)

            def settle3(s, p, r):
                after(dve, stats3_part, TPS * (s + 1))

            def moments3(s, p, r):
                for t in range(TPS):
                    ins = nc.vector.bn_aggr(mv3[:, p, t], stats3[:, p, t])
                ins.then_inc(stats3_done, 1)

            def add_up(s, p, r):
                after(dve, product_done, s + 1)
                nc.vector.tensor_reduce(w_tok[:, bass.ds(s * TPS, TPS)], product[:, p], AX.X, ALU.add).then_inc(w_done, 1)

            pipeline(dve, [(maximum(0), 3), (y_is_added, 6), (maximum(1), 3), (stats3_of, 6), (add_given, 0),
                           (given_added, 0), (settle3, 6), (maximum(2), 3),
                           (stats_of, 0), (moments3, 6), (normalise(0), 5), (settle, 0), (maximum(3), 3), (moments, 0),
                           (maximum(4), 3), (add_up, 8), (normalise(1), 5), (maximum(5), 3), (maximum(6), 3), (copy_v, 1), (maximum(7), 3),
                           (norm, 0), (add_y, 5)], B, ROUNDS)

        @block.scalar
        def _(act):
            act.wait_ge(preset_v, 3)
            nc.scalar.preload_act_table(ACT.Exp)

            def copy_hT(s, p, r):
                after(act, hT_done, s + 1)
                after(act, v_done, s - 1)
                nc.scalar.copy(hT[:, p], ps_misc[:, 0:S]).then_inc(hT_copied, 1)

            def copy_qk(s, p, r):
                after(act, qk_done, s + 1)
                after(act, part_step, 8 * (s - 1))
                nc.scalar.activation(qk[:, p, 0], ps_misc[:, 0:S], ACT.Identity, bias=bq_scaled[:], scale=SCALE)
                nc.scalar.activation(qk[:, p, 1], ps_misc[:, S:], ACT.Identity, bias=bk[:]).then_inc(qk_copied, 1)

            def copy_maxT(half):
                def step(s, p, r):
                    after(act, maxT_done, HALVES * s + half + 1)
                    after(act, max_stored[1 - p][half], 16 * (r + p))
                    nc.scalar.copy(max_T[:, half], ps_misc[:].bitcast(BF16)[0:PARTS * HH, 0:S]).then_inc(maxT_copied, 1)
                return step

            def exponential(j):
                def step(s, p, r):
                    after(act, e_filled, M_UNITS * s + j + 1)
                    after(act, o_done, AG * s + j // 2 - 1)
                    nc.scalar.activation(pT[:, j % PT_RING], slots[SLOT_OF["e", j]][:], ACT.Exp).then_inc(e_read, 1)
                return step

            def copy_o(half):
                def step(s, p, r):
                    after(act, o_done, AG * s + 2 * half + 2)
                    after(act, otok_done, TPS * s)
                    nc.scalar.copy(oT_pad[:, 2 * half:2 * half + 2], ps_o[:]).then_inc(o_copied, 1)
                return step

            def copy_oT(s, p, r):
                after(act, oT_done, s + 1)
                after(act, y_done, s - 1)
                nc.scalar.copy(oT[:, p], ps_misc[:, 0:S]).then_inc(oT_copied, 1)

            def norm3(s, p, r):
                after(act, shift_done, s + 1)
                after(act, out_done, s - 1)
                for t in range(TPS):
                    ins = nc.scalar.activation(h3[:, p, t], x_sb[:, s * TPS + t, :], ACT.Identity,
                                               bias=shift[:, p, t:t + 1], scale=rstd3[:, p, t:t + 1])
                ins.then_inc(h3_done, 1)

            e = [(exponential(j), 4) for j in range(M_UNITS)]
            pipeline(act, [e[0], (copy_hT, 1), e[1], (copy_o(1), 5), (copy_maxT(1), 4), e[2], e[3], (copy_qk, 1),
                           e[4], e[5], (copy_o(0), 4), (copy_maxT(0), 3), e[6], (norm3, 7), e[7], (copy_oT, 5)], B, ROUNDS)

        @block.tensor
        def _(pe):
            pe.wait_ge(loaded, 16 * LOADS)
            pe.wait_ge(preset_v, 3)
            pe.wait_ge(ones_in, 16 * 2 * HALVES)

            def free_slot(kind, j, s):
                slot, at = SLOT_OF[kind, j], 2 * j + (kind == "e")
                s_m, s_e = (s, s - 1) if kind == "m" else (s + 1, s)
                back, unit = last_user("m", slot, at)
                after_most(pe, m_read, M_UNITS * (s_m - back) + unit + 1, ALL_M)
                back, unit = last_user("e", slot, at)
                after_most(pe, e_read, M_UNITS * (s_e - back) + unit + 1, ALL_E)

            def for_maximum(j):
                half, t, g = j // 4, j % 4 // 2, j % 2
                def step(s, p, r):
                    if j % 4 == 0:
                        after(pe, filled[p][half], 16 * FILLS * (r + 1))
                    free_slot("m", j, s)
                    for q in range(UNIT):
                        head = g * UNIT + q
                        ins = nc.tensor.matmul(slots[SLOT_OF["m", j]][:, q],
                                               q_stack[0:QK_ROWS, p, half, head, t * P:(t + 1) * P],
                                               k_stack[0:QK_ROWS, p, half, head], start=True, stop=True)
                    ins.then_inc(m_filled, 1)
                return step

            def for_exponential(j):
                half, g, t = j // 4, j % 4 // 2, j % 2
                def step(s, p, r):
                    if j % 4 == 0:
                        after(pe, max_in[p][half], 16 * (r + 1))
                    free_slot("e", j, s)
                    for q in range(UNIT):
                        head = g * UNIT + q
                        ins = nc.tensor.matmul(slots[SLOT_OF["e", j]][:, q],
                                               k_stack[0:EXP_ROWS, p, half, head, t * P:(t + 1) * P],
                                               q_stack[0:EXP_ROWS, p, half, head], start=True, stop=True)
                    ins.then_inc(e_filled, 1)
                return step

            def values(g):
                def step(s, p, r):
                    if g == 0:
                        after(pe, v_padded, s + 1)
                    if g % 2 == 0:
                        after(pe, o_copied, HALVES * s + g // 2)
                    after(pe, e_read, M_UNITS * s + 2 * g + 2)
                    for t in range(TPS):
                        for q in range(UNIT):
                            ins = nc.tensor.matmul(ps_o[q * APAD:(q + 1) * APAD, g % 2], v_pad[:, p, t, g * UNIT + q],
                                                   pT[:, (2 * g + t) % PT_RING, q], start=t == 0, stop=t == TPS - 1,
                                                   skip_group_check=True)
                    ins.then_inc(o_done, 1)
                return step

            TURNS = (("hT", 1, hT_copied, 1, 0), ("max1", 4, maxT_copied, 2, 1), ("token0", 5, otok_copied, 2, 0),
                     ("qk", 1, qk_copied, 1, 0), ("token1", 5, otok_copied, 2, 1), ("max0", 3, maxT_copied, 2, 0),
                     ("v", 1, v_copied, 1, 0), ("oT", 5, oT_copied, 1, 0), ("y", 5, y_added, 1, 0))

            def misc_free(name, s):
                at = [turn[0] for turn in TURNS].index(name)
                lag = TURNS[at][1]
                for n, (_, other_lag, read, per, which) in enumerate(TURNS):
                    if isinstance(s, int) or n == (at - 1) % len(TURNS):
                        other = s + lag - other_lag - (1 if n >= at else 0)
                        if isinstance(s, int):
                            if other < 0:
                                continue
                            other = min(other, B - 1)
                        after(pe, read, per * other + which + 1)

            def transpose_h(s, p, r):
                after(pe, h_done, s + 1)
                misc_free("hT", s)
                for t in range(TPS):
                    ins = nc.tensor.transpose(ps_misc[:, t * P:(t + 1) * P], h[:, p, t], ident[:])
                ins.then_inc(hT_done, 1)

            def transpose_max(half):
                def step(s, p, r):
                    after(pe, max_step, 8 * s + 4 * half + 4)
                    misc_free(f"max{half}", s)
                    for t in range(TPS):
                        ins = nc.tensor.transpose(ps_misc[:].bitcast(BF16)[0:PARTS * HH, t * P:(t + 1) * P],
                                                  max_part[:, half, t].rearrange("p a h -> p (a h)"), ident_b[:])
                    ins.then_inc(maxT_done, 1)
                return step

            def by_token(t):
                def step(s, p, r):
                    if t == 0:
                        after(pe, o_copied, HALVES * (s + 1))
                    misc_free(f"token{t}", s)
                    for g in range(AG):
                        ins = nc.tensor.transpose(ps_misc[:, g * P:(g + 1) * P], oT_pad[:, g, t * P:(t + 1) * P],
                                                  ident[:])
                    ins.then_inc(otok_done, 1)
                return step

            def project_qk(s, p, r):
                after(pe, hT_copied, s + 1)
                misc_free("qk", s)
                nc.tensor.matmul(ps_misc[:, 0:S], wq[:], hT[:, p], start=True, stop=True)
                nc.tensor.matmul(ps_misc[:, S:], wk[:], hT[:, p], start=True, stop=True).then_inc(qk_done, 1)

            def project_v(s, p, r):
                misc_free("v", s)
                for t in range(TPS):
                    ins = nc.tensor.matmul(ps_misc[:, t * D:(t + 1) * D], hT[:, p, t * P:(t + 1) * P], wv[:],
                                           start=True, stop=True)
                ins.then_inc(v_done, 1)

            def transpose_o(s, p, r):
                after(pe, otok_copied, TPS * (s + 1))
                misc_free("oT", s)
                for t in range(TPS):
                    ins = nc.tensor.transpose(ps_misc[:, t * P:(t + 1) * P],
                                              o_tok[:, p, t].rearrange("p h e -> p (h e)"), ident[:])
                ins.then_inc(oT_done, 1)

            def output(s, p, r):
                after(pe, oT_copied, s + 1)
                misc_free("y", s)
                for t in range(TPS):
                    ins = nc.tensor.matmul(ps_misc[:, t * D:(t + 1) * D], oT[:, p, t * P:(t + 1) * P], wo[:],
                                           start=True, stop=True)
                ins.then_inc(y_done, 1)

            M = [(for_maximum(j), 3) for j in range(M_UNITS)]
            E = [(for_exponential(j), 4) for j in range(M_UNITS)]
            pipeline(pe, [M[0], E[0], (transpose_h, 1), M[1], E[1], (values(3), 5), (transpose_max(1), 4),
                          M[2], E[2], (by_token(0), 5), M[3], E[3], (values(0), 4), (project_qk, 1),
                          M[4], E[4], (by_token(1), 5), M[5], E[5], (values(1), 4), (transpose_max(0), 3),
                          M[6], E[6], (project_v, 1), M[7], E[7], (values(2), 4), (transpose_o, 5), (output, 5)],
                     B, ROUNDS)


def by_half(weight):
    return np.ascontiguousarray(weight.reshape(-1, HALVES, HH, AD).transpose(0, 1, 3, 2).reshape(-1, D))


SEL = S // 8
GB = P // SEL
G = B // GB
HG = 4
FF = 512
FB = FF // P
IDS = 4
RMS_EPS = 1e-6
TWO_PI = 2 * np.pi
C1 = 6.28125
C2 = float(np.float32(np.round((TWO_PI - C1) * 2.0 ** 21) / 2.0 ** 21))
C3 = float(TWO_PI - C1 - C2)
ROUND = 1.5 * 2.0 ** 23


def routed_phase(nc, w, keep, out):
    with Memory(nc) as m:
        work, w_tok = keep["h2"], keep["w_tok"]
        ident = keep["ident"]

        names = {"d_rb": [P, 1], "d_wqkv": [P, 3 * D], "d_wo": [P, AG, D], "d_w1": [P, FF],
                 "d_w2": [P, FB, D], "d_ln1": [P, 1], "d_ln2": [P, 1], "d_own_head": [P, AH], "d_pick": [B, GB, G],
                 "d_row": [P, G], "d_row_ids": [P, G], "d_real": [P, 1], "d_inv": [P, AD // 2], "d_column": [P, TPS]}
        t = {name: m.sbuf(name + "_sb", shape) for name, shape in names.items()}
        LOADS = len(names)
        half_pow = m.sbuf("d_half_pow", [P, G])
        ones = m.sbuf("d_ones", [B, P])
        w_row = m.sbuf("d_w_row", [B, S])
        top = m.sbuf("d_top", [B, SEL])
        top_u = m.sbuf("d_top_u", [B, SEL], U32)
        top_i = m.sbuf("d_top_i", [B, SEL])
        coef_row = m.sbuf("d_coef_row", [B, SEL])
        spread_i = m.sbuf("d_spread_i", [B, B, SEL])
        row_f = m.sbuf("d_row_f", [P, G])
        rows = m.sbuf("d_rows", [P, G], I32)
        row_ids_f = m.sbuf("d_row_ids_f", [P, G])
        rows_ids = m.sbuf("d_rows_ids", [P, G], I32)
        w_sel = m.sbuf("d_w_sel", [P, G])
        coef = m.sbuf("d_coef", [P, G])
        one_hot = m.sbuf("d_one_hot", [P, TPS, B * SEL])
        flat = work[:].rearrange("p t d -> p (t d)")
        half_flat = NT * D // 2
        prob = flat[:, 0:half_flat].rearrange("p (g h j) -> p g h j", g=G, h=AH)
        mask_rows = flat[:, half_flat:half_flat + G * S].rearrange("p (g s) -> p g s", g=G)
        mask_T = flat[:, half_flat + G * S:].rearrange("p (g c i) -> p g c i", g=G, c=TPS)
        hidden = flat[:, half_flat:].rearrange("p (f n) -> p f n", f=FB)
        mask = m.sbuf("d_mask", [P, G, SEL])
        pos = m.sbuf("d_pos", [P, G], I32)
        pos_f = m.sbuf("d_pos_f", [P, G])
        angle = m.sbuf("d_angle", [P, G, AD // 2])
        turns = m.sbuf("d_turns", [P, G, AD // 2])
        angle_c = m.sbuf("d_angle_c", [P, G, AD // 2])
        cos = m.sbuf("d_cos", [P, G, 2, AD // 2])
        sin = m.sbuf("d_sin", [P, G, 2, AD // 2])
        x_sel = m.sbuf("d_x_sel", [P, G, D])
        h_sel = m.sbuf("d_h_sel", [P, G, D])
        stats_sel = m.sbuf("d_stats_sel", [P, G, 6])
        mv_sel = m.sbuf("d_mv_sel", [P, G, 2])
        square = m.sbuf("d_square", [P, G, D])
        ms = m.sbuf("d_ms", [P, G])
        rstd = m.sbuf("d_rstd", [P, G])
        xn = m.sbuf("d_xn", [P, G, D])
        xnT = m.sbuf("d_xnT", [P, G, P])
        qk = m.sbuf("d_qk", [P, G, 2 * AH, AD])
        swapped = m.sbuf("d_swapped", [P, G, 2 * AH, AD])
        v_pad = m.sbuf("d_v_pad", [P, G, AH, APAD])
        qT = m.sbuf("d_qT", [P, G, P])
        kT = m.sbuf("d_kT", [P, G, P])
        k_spread = m.sbuf("d_k_spread", [P, 2, GB, AH, SEL])
        top_score = m.sbuf("d_top_score", [P, G, AH])
        total = m.sbuf("d_total", [P, G, AH])
        probT = m.sbuf("d_probT", [P, 2, AH, P])
        oT = m.sbuf("d_oT", [P, 2, AG, P])
        ps = m.psum("d_ps", [P, G, 512])

        loaded = m.sem("d_loaded")
        preset = m.sem("d_preset")
        chain = m.sem("d_chain")
        wT_done = m.sem("d_wT_done")
        top_done = m.sem("d_top_done")
        picked = m.sem("d_picked")
        picked_read = m.sem("d_picked_read")
        mask_in = m.sem("d_mask_in")
        pos_in = m.sem("d_pos_in")
        x_in = m.sem("d_x_in")
        clamped = m.sem("d_clamped")
        maskT_done = m.sem("d_maskT_done")
        maskT_copied = m.sem("d_maskT_copied")
        mask_done = m.sem("d_mask_done")
        mask_read = m.sem("d_mask_read")
        angle_done = m.sem("d_angle_done")
        rope_ready = m.sem("d_rope_ready")
        ms_done = m.sem("d_ms_done")
        rstd_done = m.sem("d_rstd_done")
        xn_done = m.sem("d_xn_done")
        xnT_done = m.sem("d_xnT_done")
        xnT_copied = m.sem("d_xnT_copied")
        qkv_done = m.sem("d_qkv_done")
        v_copied = m.sem("d_v_copied")
        roped = m.sem("d_roped")
        qkT_done = m.sem("d_qkT_done")
        qkT_copied = m.sem("d_qkT_copied")
        k_spread_dve = m.sem("d_k_spread_dve")
        k_spread_pool = m.sem("d_k_spread_pool")
        score_done = m.sem("d_score_done")
        score_read = m.sem("d_score_read")
        less_max = m.sem("d_less_max")
        exp_done = m.sem("d_exp_done")
        probT_done = m.sem("d_probT_done")
        oT_done = m.sem("d_oT_done")
        oT_copied = m.sem("d_oT_copied")
        y_done = m.sem("d_y_done")
        x1_done = m.sem("d_x1_done")
        up_done = m.sem("d_up_done")
        gelu_done = m.sem("d_gelu_done")
        down_done = m.sem("d_down_done")
        result_done = m.sem("d_result_done")
        scattered = m.sem("d_scattered")
        block = m.ctx.enter_context(nc.Block())

        @block.sync
        def _(sp):
            for name in names:
                sp.dma_start(t[name][:], w[name]).then_inc(loaded, 16)
            sp.wait_ge(scattered, 16 * G)

        @block.gpsimd
        def _(pool):
            nc.gpsimd.memset(half_pow[:], -0.5).then_inc(preset, 1)
            nc.gpsimd.memset(ones[:], 1.0).then_inc(preset, 1)
            nc.gpsimd.memset(v_pad[:], 0.0).then_inc(preset, 1)
            nc.gpsimd.memset(probT[:], 0.0).then_inc(preset, 1)
            pool.wait_ge(preset, 4)
            pool.wait_ge(picked_read, 1)
            index = lambda a, g: bass.IndirectOffsetOnAxis(ap=a[:, g:g + 1], axis=0)
            for g in range(G):
                nc.gpsimd.indirect_dma_start(pos[:, g:g + 1], None, w["d_position"], index(rows_ids, g)).then_inc(pos_in, 16)
            for g in range(G):
                nc.gpsimd.indirect_dma_start(mask_rows[:, g], None, w["d_mask"], index(rows_ids, g)).then_inc(mask_in, 16)
            for g in range(G):
                nc.gpsimd.indirect_dma_start(x_sel[:, g], None, keep["x_rows"], index(rows, g)).then_inc(x_in, 16)
            for n in range(2):
                pool.wait_ge(ms_done, n + 1)
                nc.gpsimd.tensor_tensor(rstd[:], ms[:], half_pow[:], ALU.pow).then_inc(rstd_done, 1)
            pool.wait_ge(loaded, 16 * LOADS)
            for g in range(1, G, 2):
                pool.wait_ge(qkT_copied, g + 1)
                after(pool, score_done, g - 1)
                nc.gpsimd.tensor_tensor(k_spread[:, 1], kT[:, g].rearrange("p (b j) -> p b j", b=GB).unsqueeze(2)
                                        .to_broadcast([P, GB, AH, SEL]),
                                        t["d_own_head"][:].unsqueeze(1).unsqueeze(3).to_broadcast([P, GB, AH, SEL]),
                                        ALU.mult).then_inc(k_spread_pool, 1)
            pool.wait_ge(ms_done, 3)
            nc.gpsimd.tensor_tensor(rstd[:], ms[:], half_pow[:], ALU.pow).then_inc(rstd_done, 1)
            pool.wait_ge(result_done, 1)
            for g in range(G):
                nc.gpsimd.indirect_dma_start(out, index(rows, g), square[:, g], None).then_inc(scattered, 16)

        @block.vector
        def _(dve):
            steps = [0]

            def chained(ins):
                steps[0] += 1
                ins.then_inc(chain, 1)
                dve.wait_ge(chain, steps[0])

            v = nc.vector
            dve.wait_ge(loaded, 16 * LOADS)
            dve.wait_ge(wT_done, 1)
            chained(v.tensor_scalar(w_row[:], ps[0:B, 0, 0:S], t["d_rb"][0:B], None, ALU.add))
            for k in range(0, SEL, 8):
                chained(v.max(top[:, k:k + 8], w_row[:]))
                chained(v.max_index(top_u[:, k:k + 8], top[:, k:k + 8], w_row[:]))
                if k + 8 < SEL:
                    chained(v.match_replace(w_row[:], top[:, k:k + 8], w_row[:], -3.0e38))
            chained(v.tensor_scalar(coef_row[:], top[:], top[:, SEL - 1:SEL], None, ALU.is_gt))
            chained(v.tensor_scalar(coef_row[:], coef_row[:], -1.0, 1.0, ALU.mult, ALU.add))
            chained(v.tensor_copy(top_i[:], top_u[:]))
            v.tensor_tensor(spread_i[:], top_i[:].unsqueeze(1).to_broadcast([B, B, SEL]),
                            ident[0:B, 0:B].unsqueeze(2).to_broadcast([B, B, SEL]), ALU.mult).then_inc(top_done, 1)
            dve.wait_ge(picked, 1)
            v.tensor_tensor(row_f[:], ps[:, 3, 0:G], t["d_row"][:], ALU.add)
            chained(v.tensor_tensor(row_ids_f[:], ps[:, 3, 0:G], t["d_row_ids"][:], ALU.add))
            v.tensor_copy(rows[:], row_f[:])
            v.tensor_copy(rows_ids[:], row_ids_f[:]).then_inc(picked_read, 1)
            v.tensor_scalar(w_sel[:], ps[:, 3, G:2 * G], t["d_real"][:], None, ALU.mult)
            v.tensor_copy(coef[:], ps[:, 3, 2 * G:3 * G])
            for c in range(TPS):
                ins = v.tensor_scalar(one_hot[:, c].rearrange("p (a n) -> p a n", a=2), ps[:, 1:3],
                                      t["d_column"][:, c:c + 1], None, ALU.is_equal)
            ins.then_inc(picked_read, 1)
            dve.wait_ge(pos_in, 16 * G)
            chained(v.tensor_copy(pos_f[:], pos[:]))
            chained(v.tensor_tensor(angle[:], pos_f[:].unsqueeze(2).to_broadcast([P, G, AD // 2]),
                                    t["d_inv"][:].unsqueeze(1).to_broadcast([P, G, AD // 2]), ALU.mult))
            chained(v.tensor_scalar(turns[:], angle[:], 1 / TWO_PI, ROUND, ALU.mult, ALU.add))
            chained(v.tensor_scalar(turns[:], turns[:], ROUND, None, ALU.subtract))
            for part in (C1, C2, C3):
                chained(v.tensor_scalar(angle_c[:], turns[:], -part, None, ALU.mult))
                chained(v.tensor_tensor(angle[:], angle[:], angle_c[:], ALU.add))
            PI = 3.1415925
            chained(v.tensor_scalar(angle[:], angle[:], PI, -PI, ALU.min, ALU.max))
            chained(v.tensor_scalar(angle_c[:], angle[:], np.pi / 2, None, ALU.add))
            chained(v.tensor_scalar(turns[:], angle_c[:], PI, -TWO_PI, ALU.is_gt, ALU.mult))
            chained(v.tensor_tensor(angle_c[:], angle_c[:], turns[:], ALU.add))
            v.tensor_scalar(angle_c[:], angle_c[:], PI, -PI, ALU.min, ALU.max).then_inc(angle_done, 1)
            dve.wait_ge(mask_in, 16 * G)
            v.tensor_scalar(mask_rows, mask_rows, -3.0e38, None, ALU.max).then_inc(clamped, 1)

            dve.wait_ge(x_in, 16 * G)
            for g in range(G):
                ins = v.bn_stats(stats_sel[:, g], x_sel[:, g])
            chained(ins)
            for g in range(G):
                ins = v.bn_aggr(mv_sel[:, g], stats_sel[:, g])
            chained(ins)
            v.tensor_scalar(ms[:], mv_sel[:, :, 1], LN_EPS, None, ALU.add).then_inc(ms_done, 1)
            dve.wait_ge(rstd_done, 1)
            for g in range(G):
                ins = v.tensor_scalar(h_sel[:, g], x_sel[:, g], mv_sel[:, g, 0:1], rstd[:, g:g + 1],
                                      ALU.subtract, ALU.mult)
            chained(ins)

            def mean_square(x):
                chained(v.tensor_tensor(square[:], x[:], x[:], ALU.mult))
                chained(v.tensor_reduce(ms[:], square[:], AX.X, ALU.add))
                v.tensor_scalar(ms[:], ms[:], 1.0 / D, RMS_EPS, ALU.mult, ALU.add).then_inc(ms_done, 1)

            by_token = lambda a: a[:].unsqueeze(2).to_broadcast([P, G, D])
            mean_square(h_sel)
            dve.wait_ge(rstd_done, 2)
            v.tensor_tensor(xn[:], h_sel[:], by_token(rstd), ALU.mult).then_inc(xn_done, 1)
            dve.wait_ge(rope_ready, 1)
            for half in range(2):
                gs = slice(half * HG, (half + 1) * HG)
                dve.wait_ge(qkv_done, (half + 1) * HG)
                dve.wait_ge(v_copied, (half + 1) * HG)
                value = ps[:, gs, 0:2 * D].rearrange("p g (h e) -> p g h e", e=AD)
                v.tensor_tensor(qk[:, gs], value,
                                cos[:, gs].rearrange("p g u f -> p g (u f)").unsqueeze(2).to_broadcast([P, HG, 2 * AH, AD]),
                                ALU.mult)
                F = AD // 2
                for u in range(2):
                    ins = v.tensor_tensor(swapped[:, gs, :, u * F:(u + 1) * F], value[:, :, :, (1 - u) * F:(2 - u) * F],
                                          sin[:, gs, u].unsqueeze(2).to_broadcast([P, HG, 2 * AH, F]), ALU.mult)
                chained(ins)
                v.tensor_tensor(qk[:, gs], qk[:, gs], swapped[:, gs], ALU.add).then_inc(roped, 1)
            for g in range(0, G, 2):
                dve.wait_ge(qkT_copied, g + 1)
                after(dve, score_done, g - 1)
                v.tensor_tensor(k_spread[:, 0], kT[:, g].rearrange("p (b j) -> p b j", b=GB).unsqueeze(2)
                                .to_broadcast([P, GB, AH, SEL]),
                                t["d_own_head"][:].unsqueeze(1).unsqueeze(3).to_broadcast([P, GB, AH, SEL]),
                                ALU.mult).then_inc(k_spread_dve, 1)
            K = SEL - 1
            dve.wait_ge(mask_read, G)
            chained(v.memset(prob[:, :, :, K:SEL], 0.0))
            halves = [slice(half * HG, (half + 1) * HG) for half in range(2)]
            for half, gs in enumerate(halves):
                dve.wait_ge(score_done, (half + 1) * HG)
                ins = v.tensor_tensor(prob[:, gs, :, 0:K],
                                      ps[:, gs].rearrange("p g (h j) -> p g h j", h=AH)[:, :, :, 0:K],
                                      mask[:, gs, 0:K].unsqueeze(2).to_broadcast([P, HG, AH, K]), ALU.add)
                steps[0] += 1
                ins.then_inc(chain, 1)
                v_read = steps[0]
                dve.wait_ge(chain, v_read)
                chained(v.tensor_reduce(top_score[:, gs], prob[:, gs, :, 0:K], AX.X, ALU.max))
                v.tensor_tensor(prob[:, gs, :, 0:K], prob[:, gs, :, 0:K],
                                top_score[:, gs].unsqueeze(3).to_broadcast([P, HG, AH, K]), ALU.subtract
                                ).then_inc(less_max, 1)
            for half, gs in enumerate(halves):
                dve.wait_ge(exp_done, half + 1)
                chained(v.tensor_reduce(total[:, gs], prob[:, gs, :, 0:K], AX.X, ALU.add))
                chained(v.reciprocal(total[:, gs], total[:, gs]))
                chained(v.tensor_tensor(prob[:, gs, :, 0:K], prob[:, gs, :, 0:K],
                                        total[:, gs].unsqueeze(3).to_broadcast([P, HG, AH, K]), ALU.mult))
                dve.wait_ge(preset, 4)
                for g in range(half * HG, (half + 1) * HG):
                    after(dve, oT_done, g - 1)
                    for b in range(GB):
                        rows_b = slice(b * SEL, (b + 1) * SEL)
                        ins = v.transpose(probT[rows_b, g % 2, :, rows_b], prob[rows_b, g])
                    ins.then_inc(probT_done, 1)
            dve.wait_ge(y_done, G)
            x1 = xn
            v.tensor_tensor(x1[:], h_sel[:], ps[:, :, 0:D], ALU.add).then_inc(x1_done, 1)
            dve.wait_ge(x1_done, 1)
            mean_square(x1)
            chained(v.tensor_tensor(h_sel[:], h_sel[:], by_token(coef), ALU.mult))
            chained(v.tensor_tensor(x_sel[:], x_sel[:], h_sel[:], ALU.add))
            dve.wait_ge(rstd_done, 3)
            v.tensor_tensor(square[:], x1[:], by_token(rstd), ALU.mult).then_inc(xn_done, 1)
            dve.wait_ge(down_done, G)
            chained(v.tensor_tensor(xn[:], x1[:], ps[:, :, 0:D], ALU.add))
            chained(v.tensor_tensor(xn[:], xn[:], by_token(w_sel), ALU.mult))
            v.tensor_tensor(square[:], xn[:], x_sel[:], ALU.add).then_inc(result_done, 1)

        @block.scalar
        def _(act):
            act.wait_ge(angle_done, 1)
            for u in range(2):
                nc.scalar.activation(cos[:, :, u], angle_c[:], ACT.Sin)
            nc.scalar.activation(sin[:, :, 0], angle[:], ACT.Sin, scale=-1.0)
            nc.scalar.activation(sin[:, :, 1], angle[:], ACT.Sin).then_inc(rope_ready, 1)
            for g in range(G):
                act.wait_ge(maskT_done, g + 1)
                nc.scalar.copy(mask_T[:, g].rearrange("p c i -> p (c i)"), ps[:, g, 0:S]).then_inc(maskT_copied, 1)
            for g in range(G):
                act.wait_ge(mask_done, g + 1)
                nc.scalar.copy(mask[:, g], ps[:, g, 0:SEL]).then_inc(mask_read, 1)
            act.wait_ge(loaded, 16 * LOADS)
            for g in range(G):
                act.wait_ge(xnT_done, g + 1)
                nc.scalar.activation(xnT[:, g], ps[:, g, 0:P], ACT.Copy, scale=t["d_ln1"][:]).then_inc(xnT_copied, 1)
            act.wait_ge(preset, 4)
            for g in range(G):
                act.wait_ge(qkv_done, g + 1)
                nc.scalar.copy(v_pad[:, g, :, 0:AD], ps[:, g, 2 * D:3 * D].rearrange("p (h e) -> p h e", h=AH)
                               ).then_inc(v_copied, 1)
            for g in range(G):
                act.wait_ge(qkT_done, g + 1)
                nc.scalar.mul(qT[:, g], ps[:, g, 0:P], AD ** -0.5)
                nc.scalar.copy(kT[:, g], ps[:, g, P:2 * P]).then_inc(qkT_copied, 1)
            for half in range(2):
                act.wait_ge(less_max, half + 1)
                some = prob[:, half * HG:(half + 1) * HG, :, 0:SEL - 1]
                nc.scalar.activation(some, some, ACT.Exp).then_inc(exp_done, 1)
            for g in range(G):
                act.wait_ge(oT_done, g + 1)
                after(act, y_done, g - 1)
                nc.scalar.copy(oT[:, g % 2].rearrange("p a i -> p (a i)"), ps[:, g]).then_inc(oT_copied, 1)
            for g in range(G):
                act.wait_ge(xnT_done, G + g + 1)
                nc.scalar.activation(xnT[:, g], ps[:, g, 0:P], ACT.Copy, scale=t["d_ln2"][:]).then_inc(xnT_copied, 1)
            for u in range(2 * FB):
                act.wait_ge(up_done, u + 1)
                half, f = u // FB, u % FB
                nc.scalar.activation(hidden[:, f, half * 512:(half + 1) * 512], ps[:, u], ACT.Gelu_apprx_tanh
                                     ).then_inc(gelu_done, 1)

        @block.tensor
        def _(pe):
            pe.wait_ge(loaded, 16 * LOADS)
            for c in range(TPS):
                ins = nc.tensor.transpose(ps[0:B, 0, c * P:(c + 1) * P], w_tok[:].rearrange("p (b c) -> p b c", c=TPS)[:, :, c],
                                          ident[:])
            ins.then_inc(wT_done, 1)
            pe.wait_ge(top_done, 1)
            pe.wait_ge(preset, 2)
            for n, row in enumerate((top_i, top, coef_row)):
                for b in range(GB):
                    nc.tensor.matmul(ps[b * SEL:(b + 1) * SEL, 3, n * G:(n + 1) * G], row[:], t["d_pick"][:, b],
                                     start=True, stop=True)
            for half in range(2):
                ins = nc.tensor.matmul(ps[:, 1 + half], ones[:],
                                       spread_i[:, half * B // 2:(half + 1) * B // 2], start=True, stop=True)
            ins.then_inc(picked, 1)
            pe.wait_ge(clamped, 1)
            pe.wait_ge(picked_read, 2)
            for g in range(G):
                for c in range(TPS):
                    ins = nc.tensor.transpose(ps[:, g, c * P:(c + 1) * P], mask_rows[:, g, c * P:(c + 1) * P], ident[:])
                ins.then_inc(maskT_done, 1)
            for g in range(G):
                pe.wait_ge(maskT_copied, g + 1)
                for b in range(GB):
                    rows_b = slice(b * SEL, (b + 1) * SEL)
                    for c in range(TPS):
                        ins = nc.tensor.matmul(ps[rows_b, g, 0:SEL], mask_T[:, g, c, rows_b],
                                               one_hot[:, c, (g * GB + b) * SEL:(g * GB + b + 1) * SEL],
                                               start=c == 0, stop=c == TPS - 1)
                ins.then_inc(mask_done, 1)

            def transpose_xn(n, xn):
                pe.wait_ge(xn_done, n + 1)
                for g in range(G):
                    if n == 0:
                        pe.wait_ge(mask_read, g + 1)
                    nc.tensor.transpose(ps[:, g, 0:P], xn[:, g], ident[:]).then_inc(xnT_done, 1)

            transpose_xn(0, xn)
            for g in range(G):
                pe.wait_ge(xnT_copied, g + 1)
                nc.tensor.matmul(ps[:, g, 0:3 * D], xnT[:, g], t["d_wqkv"][:], start=True, stop=True).then_inc(qkv_done, 1)
            for g in range(G):
                pe.wait_ge(roped, g // HG + 1)
                for which in range(2):
                    ins = nc.tensor.transpose(ps[:, g, which * P:(which + 1) * P],
                                              qk[:, g, which * AH:(which + 1) * AH].rearrange("p h e -> p (h e)"), ident[:])
                ins.then_inc(qkT_done, 1)
            for g in range(G):
                pe.wait_ge(qkT_copied, g + 1)
                pe.wait_ge(k_spread_pool if g % 2 else k_spread_dve, g // 2 + 1)
                for b in range(GB):
                    rows_b = slice(b * SEL, (b + 1) * SEL)
                    ins = nc.tensor.matmul(ps[rows_b, g], qT[:, g, rows_b], k_spread[:, g % 2, b], start=True, stop=True)
                ins.then_inc(score_done, 1)

            def transpose_and_output(g):
                pe.wait_ge(oT_copied, g + 1)
                for a in range(AG):
                    ins = nc.tensor.matmul(ps[:, g, 0:D], oT[:, g % 2, a], t["d_wo"][:, a], start=a == 0, stop=a == AG - 1)
                ins.then_inc(y_done, 1)

            for g in range(G):
                pe.wait_ge(probT_done, g + 1)
                for head in range(AH):
                    a, q = head // 4, head % 4
                    ins = nc.tensor.matmul(ps[q * APAD:(q + 1) * APAD, g, a * P:(a + 1) * P], v_pad[:, g, head],
                                           probT[:, g % 2, head], start=True, stop=True, skip_group_check=True)
                ins.then_inc(oT_done, 1)
                if g > 0:
                    transpose_and_output(g - 1)
            transpose_and_output(G - 1)
            pe.wait_ge(x1_done, 1)
            transpose_xn(1, square)
            for u in range(2 * FB):
                half, f = u // FB, u % FB
                pe.wait_ge(xnT_copied, 2 * G)
                nc.tensor.matmul(ps[:, u], t["d_w1"][:, f * P:(f + 1) * P], xnT[:, half * HG:(half + 1) * HG],
                                 start=True, stop=True).then_inc(up_done, 1)
            pe.wait_ge(gelu_done, 2 * FB)
            for g in range(G):
                for f in range(FB):
                    ins = nc.tensor.matmul(ps[:, g, 0:D], hidden[:, f, g * P:(g + 1) * P], t["d_w2"][:, f],
                                           start=f == 0, stop=f == FB - 1)
                ins.then_inc(down_done, 1)


def constants4():
    f = lambda a: np.ascontiguousarray(a, dtype=np.float32)
    p, g = np.arange(P), np.arange(G)
    b = g[None, :] * GB + p[:, None] // SEL
    return {"d_own_head": f(p[:, None] // AD == np.arange(AH)), "d_row": f(b * S), "d_row_ids": f(np.minimum(b, IDS - 1) * S),
            "d_pick": f(np.arange(B)[:, None, None] == g[None, None, :] * GB + np.arange(GB)[None, :, None]),
            "d_real": f((p % SEL != SEL - 1)[:, None]), "d_column": f(p[:, None] + P * np.arange(TPS)),
            "d_inv": f(np.broadcast_to(1.0 / np.float32(10000.0) ** (np.arange(0, AD, 2, dtype=np.float32) / AD),
                                       (P, AD // 2)))}


def two_layers(nc, w, out):
    with Memory(nc) as m:
        internal = lambda name, rows: nc.dram_tensor(name, (rows, D), F32, kind="Internal").ap()
        keep = {"x": m.sbuf("x", [P, NT, D]), "h2": m.sbuf("h2", [P, NT, D]), "ident": m.sbuf("ident", [P, P]),
                "w_tok": m.sbuf("w_tok", [P, NT]), "slot": m.sbuf("slot", [P, NT], I32), "gathered": [m.sem(f"gathered{n}") for n in range(len(GATHERS))], "x_rows": internal("x_rows", NT * P),
                "sorted_in": internal("sorted_in", NX * P), "sorted_out": internal("sorted_out", NX * P)}
        with Memory(nc) as early:
            keep.update(h2T=early.sbuf("h2T", [P, B * S]), logits=early.sbuf("logits", [P, NT, NE]),
                        expert_up=early.sbuf("expert_up", [P, NE, 2 * EF]))
            retention_phase(nc, w, keep)
            mixture_phase(nc, w, keep)
        attention_phase(nc, w, keep, out)
        routed_phase(nc, w, keep, out)


def layouts(inputs):
    a0 = {k[8:]: v for k, v in inputs.items() if k.startswith("L0_attn_")}
    f0 = {k[7:]: v for k, v in inputs.items() if k.startswith("L0_ffn_")}
    a1 = {k[8:]: v for k, v in inputs.items() if k.startswith("L1_attn_")}
    f1 = {k[7:]: v for k, v in inputs.items() if k.startswith("L1_ffn_")}
    on_all = lambda v: np.broadcast_to(v[None], (P,) + v.shape)
    w = {**constants(), **constants2(), **constants4(),
         "x": a0["hidden_states"].reshape(NT, P, D).transpose(1, 0, 2),
         "r_wq": a0["Wq"], "r_wk": a0["Wk"], "r_wv": a0["Wv"], "r_wo": pad_heads(a0["Wo"], RD),
         "router": f0["w_router"].T, "eu": f0["gate_up_proj"].transpose(1, 0, 2),
         "ed": f0["down_proj"].reshape(NE, EB, P, D).transpose(2, 0, 1, 3),
         "shared_up": np.stack([f0["w_gate"].T, f0["w_up"].T], 1).reshape(P, 2, EB, P),
         "shared_down": f0["w_down"].T.reshape(EB, P, D).transpose(1, 0, 2),
         "a_wq": by_half(a1["Wq"].T), "a_wk": by_half(a1["Wk"].T), "a_wv": a1["Wv"].T, "a_wo": a1["Wo"].T,
         "a_bq": by_half(a1["bq"][None]).T, "a_bk": by_half(a1["bk"][None]).T,
         "a_bv": on_all(a1["bv"]), "a_bo": on_all(a1["bo"]),
         "d_rw": on_all(f1["router_w"][:, 0]), "d_rb": on_all(f1["router_b"]),
         "d_wqkv": np.concatenate([f1["wq"], f1["wk"], f1["wv"]], 1), "d_wo": pad_heads(f1["wo"], AD),
         "d_w1": f1["w1"], "d_w2": f1["w2"].reshape(FB, P, D).transpose(1, 0, 2),
         "d_ln1": f1["ln1"][:, None], "d_ln2": f1["ln2"][:, None],
         "d_position": f1["position_ids"][:, :S].reshape(IDS * S, 1),
         "d_mask": f1["attention_mask"][:, 0, :S, :S].reshape(IDS * S, S)}
    return {name: np.ascontiguousarray(a) for name, a in w.items()}


def kernel(**inputs):
    import concourse.bacc as _bacc
    from concourse.bass_utils import run_bass_kernel_spmd as _run

    nc = _bacc.Bacc("TRN2", target_bir_lowering=False, num_devices=1)
    arrays, w = {}, {}
    for name, a in layouts({k: np.asarray(v) for k, v in inputs.items()}).items():
        arrays[f"in_{name}_dram"] = a
        w[name] = nc.dram_tensor(f"in_{name}_dram", a.shape, mybir.dt.from_np(a.dtype), kind="ExternalInput").ap()
    out = nc.dram_tensor("out_0_dram", (NT * P, D), F32, kind="ExternalOutput").ap()
    two_layers(nc, w, out)
    r = _run(nc, [arrays], core_ids=[0])
    return np.asarray(r.results[0]["out_0_dram"]).reshape(B, S, D)
```

```python
from contextlib import ExitStack

import numpy as np

import concourse.bass as bass
from concourse import mybir

F32 = mybir.dt.float32
BF16 = mybir.dt.bfloat16
I32 = mybir.dt.int32
U32 = mybir.dt.uint32
ALU = mybir.AluOpType
ACT = mybir.ActivationFunctionType
AX = mybir.AxisListType

P = 128
B, S, D = 32, 256, 128
TPS = S // P
NT = B * TPS
LN_EPS = 1e-5

RH, RD = 8, D // 8
RPAD = 32
RG = RH * RPAD // P
RQ = P // RPAD

NE = 16
EF = 256
ZERO_DMA = 1024
NX = NT + NE


def after(engine, sem, count):
    if isinstance(count, int) and count <= 0:
        return
    engine.wait_ge(sem, count)


def after_apart(engine, sem, count, always):
    engine.wait_ge(*always)
    after(engine, sem, count)


def pipeline(engine, steps, n, first):
    def written(it):
        for step, lag in steps:
            if 0 <= it - lag < n:
                step(it - lag, (it - lag) % 2, (it - lag) // 2)

    for it in range(first):
        written(it)
    with engine.Fori(first // 2, n // 2) as k:
        for turn in range(2):
            for step, lag in steps:
                c = turn - lag
                step(k * 2 + c, c % 2, k + c // 2)
    for it in range(n, n + 1 + max(lag for _, lag in steps)):
        written(it)


FIRST = 8
X_PARTS = (1, 4, 8, B)


class Memory:

    def __init__(self, nc):
        self.nc, self.ctx, self.sems = nc, ExitStack(), []

    def __enter__(self):
        self.ctx.__enter__()
        return self

    def __exit__(self, *e):
        self.ctx.__exit__(*e)
        self.nc.clear_and_free_semaphores(self.sems)
        self.nc.all_engine_barrier()

    def sbuf(self, name, shape, dtype=F32):
        return self.ctx.enter_context(self.nc.sbuf_tensor(name, shape, dtype))

    def psum(self, name, shape, dtype=F32):
        return self.ctx.enter_context(self.nc.psum_tensor(name, shape, dtype))

    def sem(self, name):
        self.sems.append(self.nc.alloc_semaphore(name))
        return self.sems[-1]


def retention_phase(nc, w, keep):
    with Memory(nc) as m:
        x_sb, h2_all, h2T_all, logits_all = keep["x"], keep["h2"], keep["h2T"], keep["logits"]
        ident = keep["ident"]

        wq = m.sbuf("r_wq", [P, D])
        wk = m.sbuf("r_wk", [P, D])
        wv = m.sbuf("r_wv", [P, D])
        wo = m.sbuf("r_wo", [P, RG, D])
        router = m.sbuf("r_router", [P, NE])
        decay = m.sbuf("r_decay", [P, RH, P])
        q_decay = m.sbuf("r_q_decay", [P, P])
        k_decay = m.sbuf("r_k_decay", [P, D])
        own_head = m.sbuf("r_own_head", [P, RH, RPAD])
        half = m.sbuf("r_half", [P, TPS])
        eps = m.sbuf("r_eps", [P, TPS])

        stats = m.sbuf("r_stats", [P, 2, 2, TPS, 6])
        mv1 = m.sbuf("r_mv1", [P, 2, TPS, 2])
        mv2 = m.sbuf("r_mv2", [P, 2, TPS, 2])
        ve1 = m.sbuf("r_ve1", [P, TPS])
        ve2 = m.sbuf("r_ve2", [P, TPS])
        rstd1 = m.sbuf("r_rstd1", [P, 2, TPS])
        rstd2 = m.sbuf("r_rstd2", [P, 2, TPS])
        h = m.sbuf("r_h", [P, 2, TPS, D])
        hT = m.sbuf("r_hT", [P, 2, S])
        qT = m.sbuf("r_qT", [P, 2, S])
        kT = m.sbuf("r_kT", [P, 2, S])
        q_spread = m.sbuf("r_q_spread", [P, 2, RH, S])
        v_pad = m.sbuf("r_v_pad", [P, 2, TPS, RH, RPAD])
        k_tok = m.sbuf("r_k_tok", [P, 2, D])
        q_late = m.sbuf("r_q_late", [P, 2, P])
        state = m.sbuf("r_state", [P, 2, RH, RPAD])
        score = m.sbuf("r_score", [P, 2, TPS * RG, RQ, P])
        oT = m.sbuf("r_oT", [P, 2, RG, S])
        h2 = m.sbuf("r_h2", [P, 2, TPS, D])
        h2T = m.sbuf("r_h2T", [P, 2, S])

        ps_hT = m.psum("ps_hT", [P, S])
        ps_qk = m.psum("ps_qk", [P, 2, S])
        ps_kv = m.psum("ps_kv", [P, 3, D])
        ps_score = [m.psum(f"ps_score{i}", [P, RQ, P]) for i in range(2)]
        ps_state = m.psum("ps_state", [P, RH * RPAD])
        ps_oT = m.psum("ps_oT", [P, RG, S])
        ps_tail = m.psum("ps_tail", [P, 512])

        loaded = m.sem("r_loaded")
        x_loaded = [m.sem(f"r_x_loaded{i}") for i in range(len(X_PARTS))]
        zeroed = m.sem("r_zeroed")
        stats1_part = m.sem("r_stats1_part")
        stats1_done = m.sem("r_stats1_done")
        ve1_done = m.sem("r_ve1_done")
        rstd1_done = m.sem("r_rstd1_done")
        h_done = m.sem("r_h_done")
        hT_done = m.sem("r_hT_done")
        hT_copied = m.sem("r_hT_copied")
        qk_done = m.sem("r_qk_done")
        kv_done = m.sem("r_kv_done")
        qT_copied = m.sem("r_qT_copied")
        kT_copied = m.sem("r_kT_copied")
        v_copied = m.sem("r_v_copied")
        k_tok_done = m.sem("r_k_tok_done")
        q_late_done = m.sem("r_q_late_done")
        q_spread_done = [m.sem(f"r_q_spread_done{i}") for i in range(2)]
        state_sum = m.sem("r_state_sum")
        state_done = m.sem("r_state_done")
        score_sum = m.sem("r_score_sum")
        score_done = m.sem("r_score_done")
        oT_sum = m.sem("r_oT_sum")
        oT_copied = m.sem("r_oT_copied")
        y_done = m.sem("r_y_done")
        x1_done = m.sem("r_x1_done")
        stats2_part = m.sem("r_stats2_part")
        stats2_done = m.sem("r_stats2_done")
        ve2_done = m.sem("r_ve2_done")
        rstd2_done = m.sem("r_rstd2_done")
        h2_done = m.sem("r_h2_done")
        h2_kept = m.sem("r_h2_kept")
        h2T_done = m.sem("r_h2T_done")
        h2T_copied = m.sem("r_h2T_copied")
        h2T_kept = m.sem("r_h2T_kept")
        logits_sum = m.sem("r_logits_sum")
        logits_kept = m.sem("r_logits_kept")

        zero_rows = h2_all[:].rearrange("p t d -> p (t d)")[:, NT * D - ZERO_DMA:]
        PREPARED = 16 * (1 + NX * D // ZERO_DMA)
        prepared = m.sem("r_prepared")
        LOADS = 10
        UNITS = TPS * RG
        block = m.ctx.enter_context(nc.Block())

        @block.sync
        def _(sp):
            for part, end in enumerate(X_PARTS):
                tiles = slice(TPS * X_PARTS[part - 1] if part else 0, TPS * end)
                sp.dma_start(x_sb[:, tiles], w["x"][:, tiles]).then_inc(x_loaded[part], 16)
                if part == 0:
                    for to, name in ((wq, "r_wq"), (wk, "r_wk"), (wv, "r_wv"), (ident, "ident"), (k_decay, "k_decay"),
                                     (q_decay, "q_decay"), (decay, "decay"), (own_head, "own_head"), (wo, "r_wo"),
                                     (router, "router")):
                        sp.dma_start(to[:], w[name]).then_inc(loaded, 16)
            sp.wait_ge(zeroed, 5)

            def spread_q(s, p, r):
                after(sp, qT_copied, s + 1)
                after(sp, score_sum, UNITS * (s - 1))
                for head in range(RH):
                    rows = slice(head * RD, (head + 1) * RD)
                    sp.dma_start(q_spread[rows, p, head, :], qT[rows, p, :]).then_inc(q_spread_done[p], 16)

            pipeline(sp, [(spread_q, 3)], B, FIRST)
            sp.wait_ge(loaded, 16 * LOADS)
            for done in q_spread_done:
                sp.wait_ge(done, 16 * RH * B // 2)

        @block.gpsimd
        def _(pool):
            nc.gpsimd.memset(zero_rows, 0.0).then_inc(zeroed, 1)
            nc.gpsimd.memset(half[:], -0.5).then_inc(zeroed, 1)
            nc.gpsimd.memset(eps[:], LN_EPS).then_inc(zeroed, 1)
            nc.gpsimd.memset(v_pad[:], 0.0).then_inc(zeroed, 1)
            nc.gpsimd.memset(q_spread[:], 0.0).then_inc(zeroed, 1)
            pool.wait_ge(zeroed, 5)

            def inv_std(s, p, mv, stats_done, ve, ve_done, rstd, done, used):
                after(pool, stats_done, s + 1)
                after(pool, done, s)
                nc.gpsimd.tensor_tensor(ve[:], mv[:, p, :, 1], eps[:], ALU.add).then_inc(ve_done, 1)
                after(pool, ve_done, s + 1)
                after(pool, used, s - 1)
                nc.gpsimd.tensor_tensor(rstd[:, p], ve[:], half[:], ALU.pow).then_inc(done, 1)

            def inv_std1(s, p, r):
                inv_std(s, p, mv1, stats1_done, ve1, ve1_done, rstd1, rstd1_done, h_done)

            def inv_std2(s, p, r):
                inv_std(s, p, mv2, stats2_done, ve2, ve2_done, rstd2, rstd2_done, h2_done)

            def keep_h2(s, p, r):
                after(pool, h2_done, s + 1)
                if isinstance(s, int) and s == B - ZERO_DMA // (TPS * D):
                    pool.wait_ge(prepared, PREPARED)
                nc.gpsimd.tensor_copy(h2_all[:, bass.ds(s * TPS, TPS), :], h2[:, p]).then_inc(h2_kept, 1)

            def keep_h2T(s, p, r):
                after(pool, h2T_copied, s + 1)
                nc.gpsimd.tensor_copy(h2T_all[:, bass.ds(s * S, S)], h2T[:, p]).then_inc(h2T_kept, 1)

            def decay_q(s, p, r):
                after(pool, qT_copied, s + 1)
                after(pool, oT_sum, s - 1)
                nc.gpsimd.tensor_tensor(q_late[:, p], qT[:, p, P:], q_decay[:], ALU.mult).then_inc(q_late_done, 1)

            pipeline(pool, [(keep_h2T, 6), (decay_q, 4), (inv_std1, 1), (inv_std2, 5), (keep_h2, 6)], B, FIRST)

        @block.vector
        def _(dve):
            def stats1_of(s, p, r):
                if isinstance(s, int) and s < FIRST:
                    for part, end in enumerate(X_PARTS):
                        if s == (X_PARTS[part - 1] if part else 0) or s == FIRST - 1 and end > FIRST:
                            dve.wait_ge(x_loaded[part], 16)
                for t in range(TPS):
                    nc.vector.bn_stats(stats[:, 0, p, t], x_sb[:, s * TPS + t, :]).then_inc(stats1_part, 1)

            def settle1(s, p, r):
                after(dve, stats1_part, TPS * (s + 1))

            def moments1(s, p, r):
                for t in range(TPS):
                    ins = nc.vector.bn_aggr(mv1[:, p, t], stats[:, 0, p, t])
                ins.then_inc(stats1_done, 1)

            def norm1(s, p, r):
                after(dve, rstd1_done, s + 1)
                after(dve, hT_done, s - 1)
                for t in range(TPS):
                    ins = nc.vector.tensor_scalar(h[:, p, t], x_sb[:, s * TPS + t, :], mv1[:, p, t, 0:1],
                                                  rstd1[:, p, t:t + 1], ALU.subtract, ALU.mult)
                ins.then_inc(h_done, 1)

            def decayed(s, p, r):
                if isinstance(s, int) and s == 0:
                    dve.wait_ge(loaded, 16 * LOADS)
                after(dve, kv_done, s + 1)
                after(dve, v_copied, s + 1)
                after(dve, state_sum, s - 1)
                nc.vector.tensor_tensor(k_tok[:, p], ps_kv[:, 0], k_decay[:], ALU.mult).then_inc(k_tok_done, 1)

            def mask_state(s, p, r):
                after(dve, state_sum, s + 1)
                after(dve, oT_sum, s - 1)
                nc.vector.tensor_tensor(state[:, p], ps_state[:].rearrange("p (h e) -> p h e", h=RH), own_head[:],
                                        ALU.mult).then_inc(state_done, 1)

            def decay_scores(s, p, r):
                after(dve, oT_sum, s - 1)
                for u in range(UNITS):
                    after(dve, score_sum, UNITS * s + u + 1)
                    g = u % RG
                    nc.vector.tensor_tensor(score[:, p, u], ps_score[u % 2][:], decay[:, g * RQ:(g + 1) * RQ],
                                            ALU.mult).then_inc(score_done, 1)

            def residual(s, p, r):
                after(dve, y_done, s + 1)
                tiles = x_sb[:, bass.ds(s * TPS, TPS), :]
                nc.vector.tensor_tensor(tiles, tiles, ps_tail[:, 0:S].rearrange("p (t d) -> p t d", t=TPS),
                                        ALU.add).then_inc(x1_done, 1)

            def stats2_of(s, p, r):
                after_apart(dve, x1_done, s + 1, (loaded, 16 * LOADS))
                for t in range(TPS):
                    nc.vector.bn_stats(stats[:, 1, p, t], x_sb[:, s * TPS + t, :]).then_inc(stats2_part, 1)

            def settle2(s, p, r):
                after(dve, stats2_part, TPS * (s + 1))

            def moments2(s, p, r):
                for t in range(TPS):
                    ins = nc.vector.bn_aggr(mv2[:, p, t], stats[:, 1, p, t])
                ins.then_inc(stats2_done, 1)

            def norm2(s, p, r):
                after(dve, rstd2_done, s + 1)
                after(dve, h2T_done, s - 1)
                after(dve, h2_kept, s - 1)
                for t in range(TPS):
                    ins = nc.vector.tensor_scalar(h2[:, p, t], x_sb[:, s * TPS + t, :], mv2[:, p, t, 0:1],
                                                  rstd2[:, p, t:t + 1], ALU.subtract, ALU.mult)
                ins.then_inc(h2_done, 1)

            pipeline(dve, [(decayed, 3), (mask_state, 4), (decay_scores, 4), (residual, 5), (stats2_of, 5),
                           (stats1_of, 0), (settle2, 5), (settle1, 0), (norm1, 1), (moments2, 5), (moments1, 0),
                           (norm2, 5)], B, FIRST)

        @block.scalar
        def _(act):
            act.wait_ge(zeroed, 4)

            def prepare(s, p, r):
                if isinstance(s, int) and s == FIRST - 2:
                    nc.scalar.dma_start(keep["expert_up"][:], w["eu"]).then_inc(prepared, 16)
                    sorted_rows = keep["sorted_in"].rearrange("(p r) d -> p (r d)", p=P)
                    for at in range(0, NX * D, ZERO_DMA):
                        nc.scalar.dma_start(sorted_rows[:, at:at + ZERO_DMA], zero_rows).then_inc(prepared, 16)

            def copy_qkv(s, p, r):
                after(act, qk_done, s + 1)
                after(act, q_spread_done[p], 16 * RH * r)
                after(act, q_late_done, s - 1)
                nc.scalar.mul(qT[:, p], ps_qk[:, 0], RD ** -0.5).then_inc(qT_copied, 1)
                after(act, score_sum, UNITS * (s - 1))
                nc.scalar.copy(kT[:, p], ps_qk[:, 1]).then_inc(kT_copied, 1)
                after(act, kv_done, s + 1)
                after(act, oT_sum, s - 1)
                nc.scalar.copy(v_pad[:, p, :, :, 0:RD],
                               ps_kv[:, 1:3].rearrange("p t (h e) -> p t h e", h=RH)).then_inc(v_copied, 1)

            def copy_oT(s, p, r):
                after(act, oT_sum, s + 1)
                after(act, y_done, s - 1)
                nc.scalar.copy(oT[:, p], ps_oT[:]).then_inc(oT_copied, 1)

            def copy_hT(s, p, r):
                after(act, hT_done, s + 1)
                after(act, kv_done, s - 1)
                nc.scalar.copy(hT[:, p], ps_hT[:]).then_inc(hT_copied, 1)

            def copy_h2T(s, p, r):
                after(act, h2T_done, s + 1)
                after(act, h2T_kept, s - 1)
                after(act, logits_sum, s - 1)
                nc.scalar.copy(h2T[:, p], ps_tail[:, 0:S]).then_inc(h2T_copied, 1)

            def copy_logits(s, p, r):
                after(act, logits_sum, s + 1)
                nc.scalar.copy(logits_all[:, bass.ds(s * TPS, TPS), :],
                               ps_tail[:, 0:TPS * NE].rearrange("p (t e) -> p t e", t=TPS)).then_inc(logits_kept, 1)

            pipeline(act, [(copy_qkv, 3), (prepare, 0), (copy_h2T, 6), (copy_oT, 5), (copy_logits, 6), (copy_hT, 2)], B, FIRST)
            act.wait_ge(prepared, PREPARED)

        @block.tensor
        def _(pe):
            pe.wait_ge(loaded, 16 * LOADS)

            def transpose_h(s, p, r):
                after(pe, h_done, s + 1)
                after(pe, hT_copied, s)
                for t in range(TPS):
                    ins = nc.tensor.transpose(ps_hT[:, t * P:(t + 1) * P], h[:, p, t], ident[:])
                ins.then_inc(hT_done, 1)

            def project(s, p, r):
                after(pe, hT_copied, s + 1)
                after(pe, qT_copied, s)
                after(pe, kT_copied, s)
                nc.tensor.matmul(ps_qk[:, 0], wq[:], hT[:, p], start=True, stop=True)
                nc.tensor.matmul(ps_qk[:, 1], wk[:], hT[:, p], start=True, stop=True).then_inc(qk_done, 1)
                after(pe, k_tok_done, s)
                after(pe, v_copied, s)
                nc.tensor.matmul(ps_kv[:, 0], hT[:, p, 0:P], wk[:], start=True, stop=True)
                for t in range(TPS):
                    ins = nc.tensor.matmul(ps_kv[:, 1 + t], hT[:, p, t * P:(t + 1) * P], wv[:], start=True, stop=True)
                ins.then_inc(kv_done, 1)

            def sum_state(s, p, r):
                after(pe, k_tok_done, s + 1)
                after(pe, v_copied, s + 1)
                after(pe, state_done, s)
                nc.tensor.matmul(ps_state[:], k_tok[:, p], v_pad[:, p, 0], start=True, stop=True).then_inc(state_sum, 1)

            def scores(units):
                def step(s, p, r):
                    after(pe, kT_copied, s + 1)
                    after(pe, q_spread_done[p], 16 * RH * (r + 1))
                    for u in units:
                        c, g = u // RG, u % RG
                        after(pe, score_done, UNITS * s + u - 1)
                        nc.tensor.matmul(ps_score[u % 2][:], kT[:, p, c * P:(c + 1) * P],
                                         q_spread[:, p, g * RQ:(g + 1) * RQ, c * P:(c + 1) * P],
                                         start=True, stop=True).then_inc(score_sum, 1)
                return step

            def sum_values(s, p, r):
                after(pe, q_late_done, s + 1)
                after(pe, state_done, s + 1)
                after(pe, score_done, UNITS * (s + 1))
                after(pe, oT_copied, s)
                last = P * (TPS - 1)
                for g in range(RG):
                    nc.tensor.matmul(ps_oT[:, g, last:], state[:, p, g * RQ:(g + 1) * RQ], q_late[:, p],
                                     start=g == 0, stop=False, skip_group_check=True)
                for c in range(TPS):
                    for g in range(RG):
                        for q in range(RQ):
                            rows = slice(q * RPAD, (q + 1) * RPAD)
                            ins = nc.tensor.matmul(ps_oT[rows, g, c * P:(c + 1) * P], v_pad[:, p, c, g * RQ + q],
                                                   score[:, p, c * RG + g, q], start=False,
                                                   stop=c == TPS - 1 and g == RG - 1, skip_group_check=True)
                ins.then_inc(oT_sum, 1)

            def output(s, p, r):
                after(pe, oT_copied, s + 1)
                after(pe, logits_kept, s)
                for t in range(TPS):
                    for g in range(RG):
                        ins = nc.tensor.matmul(ps_tail[:, t * D:(t + 1) * D], oT[:, p, g, t * P:(t + 1) * P], wo[:, g],
                                               start=g == 0, stop=g == RG - 1)
                ins.then_inc(y_done, 1)

            def transpose_h2(s, p, r):
                after(pe, h2_done, s + 1)
                after(pe, x1_done, s + 1)
                for t in range(TPS):
                    ins = nc.tensor.transpose(ps_tail[:, t * P:(t + 1) * P], h2[:, p, t], ident[:])
                ins.then_inc(h2T_done, 1)

            def route(s, p, r):
                after(pe, h2T_copied, s + 1)
                for t in range(TPS):
                    ins = nc.tensor.matmul(ps_tail[:, t * NE:(t + 1) * NE], h2T[:, p, t * P:(t + 1) * P], router[:],
                                           start=True, stop=True)
                ins.then_inc(logits_sum, 1)

            pipeline(pe, [(sum_state, 4), (transpose_h2, 6), (scores((0, 1)), 4), (route, 6), (scores((2, 3)), 4),
                           (output, 5), (project, 2), (sum_values, 4), (transpose_h, 1)], B, FIRST)


def constants():
    gamma = (1.0 - np.exp2(-5.0 - np.arange(RH))).astype(np.float32).astype(np.float64)
    i = np.arange(P)
    gap = i[None, :] - i[:, None]
    decay = np.where(gap >= 0, gamma[:, None, None] ** np.maximum(gap, 0), 0.0).transpose(1, 0, 2)
    head = np.arange(D) // RD
    q_decay = gamma[head][:, None] ** (i[None, :] + 1)
    k_decay = gamma[head][None, :] ** (P - 1 - i[:, None])
    own = np.zeros((P, RH, RPAD))
    for c in range(D):
        own[c, head[c], :RD] = 1.0
    f = lambda a: np.ascontiguousarray(a, dtype=np.float32)
    return {"decay": f(decay), "q_decay": f(q_decay), "k_decay": f(k_decay), "own_head": f(own),
            "ident": f(np.eye(P))}


def pad_heads(wo, size):
    groups = D // size * RPAD // P
    padded = np.zeros((groups, P // RPAD, RPAD, D), wo.dtype)
    padded[:, :, :size] = wo.reshape(groups, P // RPAD, size, D)
    return np.ascontiguousarray(padded.reshape(groups, P, D).transpose(1, 0, 2))


EB = EF // P
PAIR = 2


GATHER_SIZES = (2, 2, 2, 4, 4, 4, 4, 6, 6, 6, 6, 6, 6, 6)
GATHERS = [range(sum(GATHER_SIZES[:n]), sum(GATHER_SIZES[:n + 1])) for n in range(len(GATHER_SIZES))]
assert sum(GATHER_SIZES) == NT


def gather_tiles(nc, keep, n):
    for t in GATHERS[n]:
        nc.gpsimd.indirect_dma_start(keep["h2"][:, t, :], None, keep["sorted_out"],
                                     bass.IndirectOffsetOnAxis(ap=keep["slot"][:, t:t + 1], axis=0)
                                     ).then_inc(keep["gathered"][n], 16)


def mixture_phase(nc, w, keep):
    with Memory(nc) as m:
        x_sb, h2_all, h2T_all, logits = keep["x"], keep["h2"], keep["h2T"], keep["logits"]
        ident, w_up = keep["ident"], keep["expert_up"]
        sorted_in, sorted_out = keep["sorted_in"], keep["sorted_out"]

        before = m.sbuf("m_before", [P, P])
        ones = m.sbuf("m_ones", [P, P])
        rank = m.sbuf("m_rank", [P, NE])
        tile_no = m.sbuf("m_tile_no", [1, NX])
        shared_up = m.sbuf("m_shared_up", [P, 2, EB, P])
        w_down = m.sbuf("m_expert_down", [P, NE, EB, D])
        shared_down = m.sbuf("m_shared_down", [P, EB, D])

        best = m.sbuf("m_best", [P, NT])
        score = m.sbuf("m_score", [P, NT])
        first = m.sbuf("m_first", [P, NT])
        chosen = m.sbuf("m_chosen", [P, NT, NE])
        work = m.sbuf("m_work", [P, NT, NE])
        total = m.sbuf("m_total", [P, NE, NT])
        running = m.sbuf("m_running", [P, NE, NT])
        same = m.sbuf("m_same", [P, NE, NT])
        count_i = m.sbuf("m_count_i", [P, NE], I32)
        tiles_i = m.sbuf("m_tiles_i", [P, NE], I32)
        tiles = m.sbuf("m_tiles", [P, NE])
        end = m.sbuf("m_end", [P, NE])
        base = m.sbuf("m_base", [P, NE])
        slot_f = m.sbuf("m_slot_f", [P, NT])
        slot = keep["slot"]
        expert_f = m.sbuf("m_expert_f", [1, NX])
        expert_i = m.sbuf("m_expert_i", [1, NX], I32)

        gate = m.sbuf("m_gate", [P, 2, EB, S])
        hidden = m.sbuf("m_hidden", [P, 2, EB, S])
        xe = m.sbuf("m_xe", [P, 2, PAIR, D])
        xeT = m.sbuf("m_xeT", [P, 2, PAIR, P])
        gate_e = m.sbuf("m_gate_e", [P, 2, PAIR, EF])
        hidden_e = m.sbuf("m_hidden_e", [P, 2, PAIR, EF])
        hiddenT_e = m.sbuf("m_hiddenT_e", [P, 2, PAIR, EB, P])
        ye = total[:].rearrange("p e t -> p (e t)")[:, 0:2 * PAIR * D].rearrange("p (b j d) -> p b j d", b=2, j=PAIR)

        banks = m.psum("m_banks", [P, 8, 512])
        bank = [banks[:, i] for i in range(8)]

        loaded = m.sem("m_loaded")
        down_loaded = m.sem("m_down_loaded")
        late_loaded = m.sem("m_late_loaded")
        tables = m.sem("m_tables")
        chain = m.sem("m_chain")
        best_done = m.sem("m_best_done")
        chosen_done = m.sem("m_chosen_done")
        counted = m.sem("m_counted")
        score_done = m.sem("m_score_done")
        slot_done = m.sem("m_slot_done")
        expert_done = m.sem("m_expert_done")
        scaled = m.sem("m_scaled")
        scattered = m.sem("m_scattered")
        up_done = m.sem("m_up_done")
        gate_done = m.sem("m_gate_done")
        hidden_done = m.sem("m_hidden_done")
        down_done = m.sem("m_down_done")
        shared_added = m.sem("m_shared_added")
        xe_loaded = [m.sem(f"m_xe_loaded{i}") for i in range(2)]
        xeT_done = m.sem("m_xeT_done")
        xeT_copied = m.sem("m_xeT_copied")
        up_e_done = m.sem("m_up_e_done")
        gate_e_done = m.sem("m_gate_e_done")
        hidden_e_done = m.sem("m_hidden_e_done")
        hiddenT_done = m.sem("m_hiddenT_done")
        hiddenT_copied = m.sem("m_hiddenT_copied")
        ye_done = m.sem("m_ye_done")
        ye_copied = m.sem("m_ye_copied")
        stored = [m.sem(f"m_stored{i}") for i in range(2)]

        LOADS = 5
        block = m.ctx.enter_context(nc.Block())

        @block.sync
        def _(sp):
            for to, name in ((before, "before"), (rank, "rank"), (tile_no, "tile_no"), (shared_up, "shared_up"),
                             (shared_down, "shared_down")):
                sp.dma_start(to[:], w[name]).then_inc(loaded, 16)
            sp.dma_start(w_down[:], w["ed"]).then_inc(down_loaded, 16)
            for name, to in keep["late"].items():
                sp.dma_start(to[:], w[name]).then_inc(late_loaded, 16)
            sp.wait_ge(scattered, 16 * NT)

            def load(t, p, r):
                after(sp, xeT_done, t - 1)
                sp.dma_start(xe[:, p], sorted_in[bass.ds(t * PAIR * P, PAIR * P), :].rearrange("(j p) d -> p j d", p=P)
                             ).then_inc(xe_loaded[p], 16)

            def store(t, p, r):
                after(sp, ye_copied, t + 1)
                sp.dma_start(sorted_out[bass.ds(t * PAIR * P, PAIR * P), :].rearrange("(j p) d -> p j d", p=P), ye[:, p]
                             ).then_inc(stored[p], 16)

            pipeline(sp, [(load, 2), (store, 8)], NX // PAIR, 10)
            for s in stored:
                sp.wait_ge(s, 16 * NX // PAIR // 2)
            for s in xe_loaded:
                sp.wait_ge(s, 16 * NX // PAIR // 2)
            sp.wait_ge(loaded, 16 * LOADS)
            sp.wait_ge(late_loaded, 16 * len(keep["late"]))

        @block.gpsimd
        def _(pool):
            nc.gpsimd.memset(ones[:], 1.0).then_inc(tables, 1)
            nc.gpsimd.memset(same[:], 1.0).then_inc(tables, 1)
            pool.wait_ge(tables, 2)
            nc.gpsimd.memset(same[:, :, 0:1], 0.0).then_inc(tables, 1)
            pool.wait_ge(slot_done, 1)
            for t in range(NT):
                if t % TPS == 0:
                    pool.wait_ge(scaled, t // TPS + 1)
                nc.gpsimd.indirect_dma_start(sorted_in, bass.IndirectOffsetOnAxis(ap=slot[:, t:t + 1], axis=0),
                                             h2_all[:, t, :], None).then_inc(scattered, 16)
            pool.wait_ge(scattered, 16 * NT)
            for s in stored:
                pool.wait_ge(s, 16 * NX // PAIR // 2)
            gather_tiles(nc, keep, 0)

        @block.vector
        def _(dve):
            steps = [0]

            def chained(ins):
                steps[0] += 1
                ins.then_inc(chain, 1)
                dve.wait_ge(chain, steps[0])

            over_experts = lambda a: a.unsqueeze(2).to_broadcast([P, NT, NE])
            over_tiles = lambda a: a.unsqueeze(1).to_broadcast([P, NT, NE])
            nc.vector.tensor_reduce(best[:], logits[:], AX.X, ALU.max).then_inc(best_done, 1)
            dve.wait_ge(best_done, 1)
            dve.wait_ge(loaded, 16 * LOADS)
            chained(nc.vector.tensor_tensor(work[:], logits[:], over_experts(best[:]), ALU.is_equal))
            chained(nc.vector.tensor_tensor(work[:], work[:], over_tiles(rank[:]), ALU.mult))
            chained(nc.vector.tensor_reduce(first[:], work[:], AX.X, ALU.max))
            nc.vector.tensor_tensor(chosen[:], over_tiles(rank[:]), over_experts(first[:]),
                                    ALU.is_equal).then_inc(chosen_done, 1)
            dve.wait_ge(counted, 2)
            dve.wait_ge(tables, 3)
            for half in range(2):
                ins = nc.vector.tensor_copy(total[:, :, half * NT // 2:(half + 1) * NT // 2],
                                            bank[6 + half].rearrange("p (t e) -> p e t", e=NE))
            chained(ins)
            flat = lambda a: a[:].rearrange("p e t -> p (e t)")
            chained(nc.vector.tensor_tensor_scan(flat(running), flat(same), flat(total), 0.0, ALU.mult, ALU.add))
            chained(nc.vector.tensor_scalar(count_i[:], running[:, :, NT - 1], float(P - 1), None, ALU.add))
            chained(nc.vector.tensor_scalar(tiles_i[:], count_i[:], P.bit_length() - 1, None, ALU.arith_shift_right))
            chained(nc.vector.tensor_copy(tiles[:], tiles_i[:]))
            chained(nc.vector.tensor_tensor_scan(end[:], ones[:, 0:NE], tiles[:], 0.0, ALU.mult, ALU.add))
            chained(nc.vector.tensor_tensor(base[:], end[:], tiles[:], ALU.subtract))
            chained(nc.vector.tensor_scalar(base[:], base[:], float(P), None, ALU.mult))
            chained(nc.vector.tensor_tensor(running[:], running[:], total[:], ALU.subtract))
            chained(nc.vector.tensor_tensor(running[:], running[:], base[:].unsqueeze(2).to_broadcast([P, NE, NT]),
                                            ALU.add))
            for half in range(2):
                ts = slice(half * NT // 2, (half + 1) * NT // 2)
                ins = nc.vector.tensor_tensor(work[:, ts], bank[4 + half].rearrange("p (t e) -> p t e", e=NE),
                                              running[:, :, ts].rearrange("p e t -> p t e"), ALU.add)
            chained(ins)
            chained(nc.vector.tensor_tensor(work[:], work[:], chosen[:], ALU.mult))
            chained(nc.vector.tensor_reduce(slot_f[:], work[:], AX.X, ALU.add))
            nc.vector.tensor_copy(slot[:], slot_f[:]).then_inc(slot_done, 1)
            dve.wait_ge(score_done, 1)

            def scale(s, p, r):
                some = h2_all[:, bass.ds(s * TPS, TPS), :]
                nc.vector.tensor_tensor(some, some, score[:, bass.ds(s * TPS, TPS)].unsqueeze(2)
                                        .to_broadcast([P, TPS, D]), ALU.mult).then_inc(scaled, 1)

            def find_experts(s, p, r):
                if not (isinstance(s, int) and s == 3):
                    return
                for half in range(2):
                    some = slice(half * NX // 2, (half + 1) * NX // 2)
                    reached = work[0:1, 0:NX // 2]
                    chained(nc.vector.tensor_tensor(reached, tile_no[:, some].unsqueeze(2).to_broadcast([1, NX // 2, NE]),
                                                    end[0:1].unsqueeze(1).to_broadcast([1, NX // 2, NE]), ALU.is_ge))
                    chained(nc.vector.tensor_reduce(expert_f[:, some], reached, AX.X, ALU.add))
                nc.vector.tensor_scalar(expert_i[:], expert_f[:], float(NE - 1), None, ALU.min).then_inc(expert_done, 1)

            def gated(s, p, r):
                after(dve, gate_done, s + 1)
                after(dve, down_done, s - 1)
                nc.vector.tensor_tensor(hidden[:, p], gate[:, p], bank[2 + p].rearrange("p (f s) -> p f s", f=EB),
                                        ALU.mult).then_inc(hidden_done, 1)

            def add_shared(s, p, r):
                after(dve, down_done, s + 1)
                some = x_sb[:, bass.ds(s * TPS, TPS), :]
                nc.vector.tensor_tensor(some, some, bank[4 + p][:, 0:S].rearrange("p (t d) -> p t d", t=TPS),
                                        ALU.add).then_inc(shared_added, 1)

            pipeline(dve, [(scale, 0), (gated, 1), (add_shared, 3), (find_experts, 0)], B, 4)

            def gated_e(t, p, r):
                after(dve, gate_e_done, t + 1)
                after(dve, hiddenT_done, t - 1)
                nc.vector.tensor_tensor(hidden_e[:, p], gate_e[:, p], banks[:, PAIR * p:PAIR * (p + 1), EF:], ALU.mult
                                        ).then_inc(hidden_e_done, 1)

            def copy_hiddenT(t, p, r):
                after(dve, hiddenT_done, t + 1)
                after(dve, ye_done, t - 1)
                nc.vector.tensor_copy(hiddenT_e[:, p], bank[4].rearrange("p (j f s) -> p j f s", j=PAIR, f=EB)
                                      ).then_inc(hiddenT_copied, 1)

            pipeline(dve, [(gated_e, 2), (copy_hiddenT, 3)], NX // PAIR, 10)

        @block.scalar
        def _(act):
            act.wait_ge(best_done, 1)
            nc.scalar.activation(score[:], best[:], ACT.Sigmoid).then_inc(score_done, 1)
            nc.scalar.preload_act_table(ACT.Silu)

            def gate_of(s, p, r):
                after(act, up_done, s + 1)
                after(act, hidden_done, s - 1)
                nc.scalar.activation(gate[:, p], bank[p].rearrange("p (f s) -> p f s", f=EB), ACT.Silu
                                     ).then_inc(gate_done, 1)

            pipeline(act, [(gate_of, 1)], B, 4)

            def copy_xeT(t, p, r):
                after(act, xeT_done, t + 1)
                after(act, up_e_done, t - 1)
                nc.scalar.copy(xeT[:, p], bank[6 + p][:, 0:PAIR * P].rearrange("p (j s) -> p j s", j=PAIR)).then_inc(xeT_copied, 1)

            def gate_of_e(t, p, r):
                after(act, up_e_done, t + 1)
                after(act, hidden_e_done, t - 1)
                nc.scalar.activation(gate_e[:, p], banks[:, PAIR * p:PAIR * (p + 1), 0:EF], ACT.Silu).then_inc(gate_e_done, 1)

            def copy_ye(t, p, r):
                after(act, ye_done, t + 1)
                after(act, stored[p], 16 * r)
                nc.scalar.copy(ye[:, p], bank[5][:, 0:PAIR * D].rearrange("p (j d) -> p j d", j=PAIR)).then_inc(ye_copied, 1)

            pipeline(act, [(copy_xeT, 2), (copy_ye, 6), (gate_of_e, 2)], NX // PAIR, 10)

        @block.tensor
        def _(pe):
            pe.wait_ge(loaded, 16 * LOADS)
            pe.wait_ge(tables, 2)
            pe.wait_ge(chosen_done, 1)
            for to, table in ((4, before), (6, ones)):
                for half in range(2):
                    ins = nc.tensor.matmul(bank[to + half], table[:], chosen[:, half * NT // 2:(half + 1) * NT // 2],
                                           start=True, stop=True)
                ins.then_inc(counted, 1)

            def up(s, p, r):
                after(pe, gate_done, s - 1)
                after(pe, hidden_done, s - 1)
                for which in range(2):
                    for f in range(EB):
                        ins = nc.tensor.matmul(bank[2 * which + p][:, f * S:(f + 1) * S], shared_up[:, which, f],
                                               h2T_all[:, bass.ds(s * S, S)], start=True, stop=True)
                ins.then_inc(up_done, 1)

            def down(s, p, r):
                if isinstance(s, int) and s == 0:
                    pe.wait_ge(slot_done, 1)
                after(pe, hidden_done, s + 1)
                after(pe, shared_added, s - 1)
                for t in range(TPS):
                    for f in range(EB):
                        ins = nc.tensor.matmul(bank[4 + p][:, t * D:(t + 1) * D], hidden[:, p, f, t * P:(t + 1) * P],
                                               shared_down[:, f], start=f == 0, stop=f == EB - 1)
                ins.then_inc(down_done, 1)

            pipeline(pe, [(up, 0), (down, 2)], B, 4)
            pe.wait_ge(shared_added, B)
            pe.wait_ge(expert_done, 1)
            pe.wait_ge(down_loaded, 16)

            def transpose_xe(t, p, r):
                after(pe, xe_loaded[p], 16 * (r + 1))
                after(pe, xeT_copied, t - 1)
                for j in range(PAIR):
                    ins = nc.tensor.transpose(bank[6 + p][:, j * P:(j + 1) * P], xe[:, p, j], ident[:])
                ins.then_inc(xeT_done, 1)

            experts = {}

            def read_experts(use):
                def step(t, p, r):
                    _, experts[use] = nc.values_load_multi_w_load_instructions(
                        expert_i[0:1, bass.ds(t * PAIR, PAIR)], engines=[mybir.EngineType.PE], min_val=0, max_val=NE - 1)
                return step

            def up_e(t, p, r):
                expert = experts["up"]
                after(pe, xeT_copied, t + 1)
                after(pe, hidden_e_done, t - 1)
                for j in range(PAIR):
                    ins = nc.tensor.matmul(bank[PAIR * p + j], xeT[:, p, j], w_up[:, expert[j]], start=True, stop=True)
                ins.then_inc(up_e_done, 1)

            def transpose_hidden(t, p, r):
                after(pe, hidden_e_done, t + 1)
                after(pe, hiddenT_copied, t)
                for j in range(PAIR):
                    for f in range(EB):
                        ins = nc.tensor.transpose(bank[4][:, (j * EB + f) * P:(j * EB + f + 1) * P],
                                                  hidden_e[:, p, j, f * P:(f + 1) * P], ident[:])
                ins.then_inc(hiddenT_done, 1)

            def down_e(t, p, r):
                expert = experts["down"]
                after(pe, hiddenT_copied, t + 1)
                after(pe, ye_copied, t)
                for j in range(PAIR):
                    for f in range(EB):
                        ins = nc.tensor.matmul(bank[5][:, j * D:(j + 1) * D], hiddenT_e[:, p, j, f],
                                               w_down[:, expert[j], f], start=f == 0, stop=f == EB - 1)
                ins.then_inc(ye_done, 1)

            pipeline(pe, [(read_experts("up"), 2), (read_experts("down"), 5), (up_e, 2), (transpose_xe, 1),
                           (transpose_hidden, 4), (down_e, 5)], NX // PAIR, 10)


def constants2():
    i = np.arange(P)
    f = lambda a: np.ascontiguousarray(a, dtype=np.float32)
    return {"before": f(i[:, None] < i[None, :]), "rank": f(np.broadcast_to(NE - np.arange(NE), (P, NE))),
            "tile_no": f(np.arange(NX)[None, :])}


AH, AD = 16, D // 16
HALVES = 2
HH = AH // HALVES
PARTS = 3
PAIRS = PARTS * PARTS
QK_ROWS = PAIRS * AD
EXP_ROWS = QK_ROWS + PARTS
UNIT = 4
M_UNITS = AH // UNIT * TPS
PT_RING = 4
APAD = 32
AG = AH // 4

ROUNDS = 14

SLOT_OF = {}
for _i in range(2 * M_UNITS):
    SLOT_OF["me"[_i % 2], _i // 2] = 1 if _i == 2 * M_UNITS - 1 else _i % 3


def last_user(kind, slot, at):
    for back in range(1, 2 * M_UNITS + 1):
        i = at - back
        j = i % (2 * M_UNITS)
        if "me"[j % 2] == kind and SLOT_OF[kind, j // 2] == slot:
            return (0 if i >= 0 else 1), j // 2
    raise ValueError(slot)


def twice(half_factor, n):
    return n * half_factor * 2


def after_most(engine, sem, count, most):
    after(engine, sem, min(count, most) if isinstance(count, int) else count)


def attention_phase(nc, w, keep, out):
    with Memory(nc) as m:
        x_sb, given = keep["x"], keep["h2"]
        ident = keep["ident"]
        gathered = keep["gathered"]

        late = keep["late"]
        wq, wk, wv, wo = late["a_wq"], late["a_wk"], late["a_wv"], late["a_wo"]
        bq, bk, bv, bo, router = late["a_bq"], late["a_bk"], late["a_bv"], late["a_bo"], late["d_rw"]
        bq_scaled = m.sbuf("a_bq_scaled", [P, 1])
        ident_b = m.sbuf("a_ident_b", [P, P], BF16)
        zeros = m.sbuf("a_zeros", [P, 1])
        half_pow = m.sbuf("a_half_pow", [P, TPS])
        eps = m.sbuf("a_eps", [P, TPS])
        ones_b = m.sbuf("a_ones_b", [PARTS, HH, S], BF16)

        stats = m.sbuf("a_stats", [P, 2, TPS, 6])
        mv = m.sbuf("a_mv", [P, 2, TPS, 2])
        ve = m.sbuf("a_ve", [P, TPS])
        rstd = m.sbuf("a_rstd", [P, 2, TPS])
        minus_mean = m.sbuf("a_minus_mean", [P, TPS])
        shift = m.sbuf("a_shift", [P, 2, TPS])
        h = m.sbuf("a_h", [P, 2, TPS, D])
        hT = m.sbuf("a_hT", [P, 2, S])
        qk = m.sbuf("a_qk", [P, 2, 2, S])
        rest = m.sbuf("a_rest", [P, 2, S])
        part = m.sbuf("a_part", [P, 2, 2, PARTS, S], BF16)
        part_dram = nc.dram_tensor("part_dram", (2, HALVES, 2, PARTS, HH * AD, S), BF16, kind="Internal").ap()
        max_dram = nc.dram_tensor("max_dram", (2, HALVES, PARTS * HH * S), BF16, kind="Internal").ap()
        q_stack = m.sbuf("a_q_stack", [P, 2, HALVES, HH, S], BF16)
        k_stack = m.sbuf("a_k_stack", [P, 2, HALVES, HH, S], BF16)
        v_tok = m.sbuf("a_v_tok", [P, 2, TPS, D])
        v_pad = m.sbuf("a_v_pad", [P, 2, TPS, AH, APAD])
        neg_max = m.sbuf("a_neg_max", [P, 2, HALVES, TPS, HH])
        max_rest = m.sbuf("a_max_rest", [P, TPS, HH])
        max_part = m.sbuf("a_max_part", [P, HALVES, TPS, PARTS, HH], BF16)
        max_T = m.sbuf("a_max_T", [PARTS * HH, HALVES, S], BF16)
        pT = m.sbuf("a_pT", [P, PT_RING, UNIT, S])
        oT_pad = m.sbuf("a_oT_pad", [P, AG, S])
        inv_sum = m.sbuf("a_inv_sum", [P, TPS, AH])
        o_tok = m.sbuf("a_o_tok", [P, 2, TPS, AH, AD])
        oT = m.sbuf("a_oT", [P, 2, S])

        stats3 = m.sbuf("e_stats", [P, 2, TPS, 6])
        mv3 = m.sbuf("e_mv", [P, 2, TPS, 2])
        ve3 = m.sbuf("e_ve", [P, TPS])
        minus_mean3 = m.sbuf("e_minus_mean", [P, TPS])
        rstd3 = m.sbuf("e_rstd", [P, 2, TPS])
        shift3 = m.sbuf("e_shift", [P, 2, TPS])
        h3 = m.sbuf("e_h", [P, 2, TPS, D])
        product = m.sbuf("e_product", [P, 2, TPS, D])
        x_plus_h = m.sbuf("e_x_plus_h", [P, 2, TPS, D])
        w_tok = keep["w_tok"]

        slots = [m.psum(f"a_slot{i}", [P, UNIT, S]) for i in range(3)]
        ps_o = m.psum("a_ps_o", [P, 2, S])
        ps_misc = m.psum("a_ps_misc", [P, 512])

        preset = m.sem("a_preset")
        preset_v = m.sem("a_preset_v")
        ones_in = m.sem("a_ones_in")
        biased = m.sem("a_biased")
        added = m.sem("a_added")
        stats_part = m.sem("a_stats_part")
        stats_done = m.sem("a_stats_done")
        ve_done = m.sem("a_ve_done")
        rstd_done = m.sem("a_rstd_done")
        shift_done = m.sem("a_shift_done")
        h_done = m.sem("a_h_done")
        hT_done = m.sem("a_hT_done")
        hT_copied = m.sem("a_hT_copied")
        qk_done = m.sem("a_qk_done")
        qk_copied = m.sem("a_qk_copied")
        v_done = m.sem("a_v_done")
        v_copied = m.sem("a_v_copied")
        v_padded = m.sem("a_v_padded")
        bias_sum = m.sem("a_bias_sum")
        part_step = m.sem("a_part_step")
        part_stored = [[m.sem(f"a_part_stored{i}{j}") for j in range(2)] for i in range(2)]
        max_stored = [[m.sem(f"a_max_stored{i}{j}") for j in range(2)] for i in range(2)]
        filled = [[m.sem(f"a_filled{i}{j}") for j in range(2)] for i in range(2)]
        m_filled = m.sem("a_m_filled")
        m_read = m.sem("a_m_read")
        max_step = m.sem("a_max_step")
        maxT_done = m.sem("a_maxT_done")
        maxT_copied = m.sem("a_maxT_copied")
        max_in = [[m.sem(f"a_max_in{i}{j}") for j in range(2)] for i in range(2)]
        e_filled = m.sem("a_e_filled")
        e_read = m.sem("a_e_read")
        o_done = m.sem("a_o_done")
        o_copied = m.sem("a_o_copied")
        otok_done = m.sem("a_otok_done")
        inv_done = m.sem("a_inv_done")
        otok_copied = m.sem("a_otok_copied")
        oT_done = m.sem("a_oT_done")
        oT_copied = m.sem("a_oT_copied")
        y_done = m.sem("a_y_done")
        y_added = m.sem("a_y_added")
        stats3_part = m.sem("e_stats_part")
        stats3_done = m.sem("e_stats_done")
        ve3_done = m.sem("e_ve_done")
        rstd3_done = m.sem("e_rstd_done")
        shift3_done = m.sem("e_shift_done")
        h3_done = m.sem("e_h_done")
        product_done = m.sem("e_product_done")
        w_done = m.sem("e_w_done")
        out_done = m.sem("e_out_done")
        x_stored = [m.sem(f"e_x_stored{i}") for i in range(2)]
        out_stored = [m.sem(f"e_out_stored{i}") for i in range(2)]

        FILLS = PARTS + 1
        ALL_M, ALL_E = M_UNITS * B, M_UNITS * B
        SCALE = AD ** -0.5
        block = m.ctx.enter_context(nc.Block())

        @block.sync
        def _(sp):
            sp.wait_ge(preset, 4)
            for p in range(2):
                for half in range(HALVES):
                    sp.dma_start(k_stack[QK_ROWS:EXP_ROWS, p, half], ones_b[:]).then_inc(ones_in, 16)

            def store_parts(s, p, r):
                after(sp, part_step, 8 * (s + 1))
                for half in range(HALVES):
                    after(sp, filled[p][half], twice(8 * FILLS, r))
                    rows = slice(half * HH * AD, (half + 1) * HH * AD)
                    sp.dma_start(part_dram[p, half].rearrange("w a r s -> r (w a) s"),
                                 part[rows, p].rearrange("r w a s -> r (w a) s")).then_inc(part_stored[p][half], 16)

            def fill(half):
                def step(s, p, r):
                    after(sp, part_stored[p][half], 16 * (r + 1))
                    after(sp, e_filled, ((s - 2) * 4 + 2 * half + 2) * (M_UNITS // 8) * 2)
                    for a in range(PARTS):
                        sp.dma_start(q_stack[a * PARTS * AD:(a + 1) * PARTS * AD, p, half],
                                     part_dram[p, half, 0, a].rearrange("(d h) s -> d (h s)", d=AD).unsqueeze(0)
                                     .to_broadcast([PARTS, AD, HH * S])).then_inc(filled[p][half], 16)
                    sp.dma_start(k_stack[0:QK_ROWS, p, half],
                                 part_dram[p, half, 1].rearrange("b (d h) s -> (b d) (h s)", d=AD).unsqueeze(0)
                                 .to_broadcast([PARTS, PARTS * AD, HH * S])).then_inc(filled[p][half], 16)
                return step

            def store_max(half):
                def step(s, p, r):
                    after(sp, maxT_copied, HALVES * s + half + 1)
                    after(sp, max_in[p][half], 16 * r)
                    sp.dma_start(max_dram[p, half].rearrange("(c s) -> c s", s=S), max_T[:, half]
                                 ).then_inc(max_stored[p][half], 16)
                return step

            def fill_max(half):
                def step(s, p, r):
                    after(sp, max_stored[p][half], 16 * (r + 1))
                    sp.dma_start(q_stack[QK_ROWS:EXP_ROWS, p, half],
                                 max_dram[p, half].rearrange("(a n) -> a n", a=PARTS)).then_inc(max_in[p][half], 16)
                return step

            by_token = lambda rows, s: rows[bass.ds(s * S, S), :].rearrange("(t p) d -> p t d", p=P)

            def store_x(s, p, r):
                after(sp, y_added, s + 1)
                sp.dma_start(by_token(keep["x_rows"], s), x_sb[:, bass.ds(s * TPS, TPS), :]).then_inc(x_stored[p], 16)

            def store_out(s, p, r):
                after(sp, out_done, s + 1)
                sp.dma_start(by_token(out, s), x_plus_h[:, p]).then_inc(out_stored[p], 16)

            pipeline(sp, [(fill(1), 3), (store_x, 8), (store_max(1), 4), (fill_max(1), 4), (store_parts, 2),
                           (fill(0), 2), (store_max(0), 3), (fill_max(0), 3), (store_out, 8)], B, ROUNDS)
            for p in range(2):
                sp.wait_ge(x_stored[p], 16 * B // 2)
                sp.wait_ge(out_stored[p], 16 * B // 2)
            for p in range(2):
                for half in range(HALVES):
                    sp.wait_ge(filled[p][half], 16 * FILLS * B // 2)
                    sp.wait_ge(max_in[p][half], 16 * B // 2)

        @block.gpsimd
        def _(pool):
            nc.gpsimd.memset(half_pow[:], -0.5).then_inc(preset, 1)
            nc.gpsimd.memset(eps[:], LN_EPS).then_inc(preset, 1)
            nc.gpsimd.memset(zeros[:], 0.0).then_inc(preset, 1)
            nc.gpsimd.memset(ones_b[:], 1.0).then_inc(preset, 1)
            pool.wait_ge(preset, 4)
            pool.wait_ge(preset_v, 3)

            def add_given(s, p, r):
                if isinstance(s, int) and s < ROUNDS:
                    for n, tiles in enumerate(GATHERS):
                        if s * TPS <= tiles[-1] and (tiles[0] < (s + 1) * TPS or s == ROUNDS - 1):
                            pool.wait_ge(gathered[n], 16 * len(tiles))
                some = x_sb[:, bass.ds(s * TPS, TPS), :]
                nc.gpsimd.tensor_tensor(some, some, given[:, bass.ds(s * TPS, TPS), :], ALU.add).then_inc(added, 1)

            def bias(s, p, r):
                after(pool, h_done, s + 1)
                some = x_sb[:, bass.ds(s * TPS, TPS), :]
                nc.gpsimd.tensor_tensor(some, some, bo[:].unsqueeze(1).to_broadcast([P, TPS, D]), ALU.add
                                        ).then_inc(biased, 1)

            def inv_std_of(s, p, stats_done, mv, ve, minus_mean, ve_done, rstd, rstd_done, shift, shift_done, used):
                after(pool, stats_done, s + 1)
                after(pool, rstd_done, s)
                nc.gpsimd.tensor_tensor(ve[:], mv[:, p, :, 1], eps[:], ALU.add).then_inc(ve_done, 1)
                after(pool, shift_done, s)
                nc.gpsimd.tensor_tensor(minus_mean[:], zeros[:].to_broadcast([P, TPS]), mv[:, p, :, 0], ALU.subtract
                                        ).then_inc(ve_done, 1)
                after(pool, ve_done, 2 * (s + 1))
                after(pool, used, s - 1)
                nc.gpsimd.tensor_tensor(rstd[:, p], ve[:], half_pow[:], ALU.pow).then_inc(rstd_done, 1)
                after(pool, rstd_done, s + 1)
                nc.gpsimd.tensor_tensor(shift[:, p], minus_mean[:], rstd[:, p], ALU.mult).then_inc(shift_done, 1)

            def inv_std(s, p, r):
                inv_std_of(s, p, stats_done, mv, ve, minus_mean, ve_done, rstd, rstd_done, shift, shift_done, h_done)

            def inv_std3(s, p, r):
                inv_std_of(s, p, stats3_done, mv3, ve3, minus_mean3, ve3_done, rstd3, rstd3_done, shift3, shift3_done,
                           h3_done)

            def split(steps, at, value, left, high, mid, low, shape):
                none = zeros[:].unsqueeze(1).to_broadcast(shape) if len(shape) == 3 else zeros[:].to_broadcast(shape)
                for n, (to, a, b, op) in enumerate(((high, value, none, ALU.add), (left, value, high, ALU.subtract),
                                                    (mid, left, none, ALU.add), (low, left, mid, ALU.subtract))):
                    nc.gpsimd.tensor_tensor(to, a, b, op).then_inc(steps, 1)
                    after(pool, steps, at + n + 1)

            def split_qk(s, p, r):
                after(pool, qk_copied, s + 1)
                for half in range(HALVES):
                    after(pool, part_stored[p][half], 16 * r)
                for which in range(2):
                    split(part_step, 8 * s + 4 * which, qk[:, p, which], rest[:, which], part[:, p, which, 0],
                          part[:, p, which, 1], part[:, p, which, 2], [P, S])

            def split_max(half):
                def step(s, p, r):
                    after(pool, m_read, M_UNITS * s + (half + 1) * M_UNITS // 2)
                    after(pool, maxT_done, HALVES * (s - 1) + half + 1)
                    split(max_step, 8 * s + 4 * half, neg_max[:, p, half], max_rest[:], max_part[:, half, :, 0],
                          max_part[:, half, :, 1], max_part[:, half, :, 2], [P, TPS, HH])
                return step

            def pad_v(s, p, r):
                after(pool, v_copied, s + 1)
                after(pool, o_done, AG * (s - 1))
                nc.gpsimd.tensor_tensor(v_pad[:, p, :, :, 0:AD].rearrange("p t h e -> p (t h) e"),
                                        v_tok[:, p].rearrange("p t (h e) -> p (t h) e", h=AH),
                                        zeros[:].unsqueeze(1).to_broadcast([P, TPS * AH, AD]), ALU.add
                                        ).then_inc(v_padded, 1)

            def weigh(s, p, r):
                after(pool, h3_done, s + 1)
                after(pool, w_done, s - 1)
                nc.gpsimd.tensor_tensor(product[:, p], h3[:, p], router[:].unsqueeze(1).to_broadcast([P, TPS, D]),
                                        ALU.mult).then_inc(product_done, 1)
                after(pool, out_stored[p], 16 * r)
                nc.gpsimd.tensor_tensor(x_plus_h[:, p], x_sb[:, bass.ds(s * TPS, TPS), :], h3[:, p], ALU.add
                                        ).then_inc(out_done, 1)

            def gather_more(s, p, r):
                if isinstance(s, int) and s + 1 < len(GATHERS):
                    gather_tiles(nc, keep, s + 1)

            pipeline(pool, [(gather_more, 0), (split_max(1), 4), (add_given, 0), (split_qk, 2), (bias, 2), (inv_std3, 7),
                           (pad_v, 3), (split_max(0), 3), (inv_std, 0), (weigh, 7)], B, ROUNDS)

        @block.vector
        def _(dve):
            nc.vector.memset(v_pad[:], 0.0).then_inc(preset_v, 1)
            dve.wait_ge(preset_v, 1)
            nc.vector.memset(v_pad[:, :, :, :, AD:AD + 1], 1.0).then_inc(preset_v, 1)
            dve.wait_ge(bias_sum, 1)
            nc.vector.tensor_tensor(bo[:], bo[:], ps_misc[:, 0:D], ALU.add)
            nc.vector.tensor_copy(ident_b[:], ident[:])
            nc.vector.tensor_scalar(bq_scaled[:], bq[:], SCALE, None, ALU.mult).then_inc(preset_v, 1)

            def given_added(s, p, r):
                after(dve, added, s + 1)

            def stats_of(s, p, r):
                for t in range(TPS):
                    nc.vector.bn_stats(stats[:, p, t], x_sb[:, s * TPS + t, :]).then_inc(stats_part, 1)

            def settle(s, p, r):
                after(dve, stats_part, TPS * (s + 1))

            def moments(s, p, r):
                for t in range(TPS):
                    ins = nc.vector.bn_aggr(mv[:, p, t], stats[:, p, t])
                ins.then_inc(stats_done, 1)

            def maximum(j):
                half, t, g = j // 4, j % 4 // 2, j % 2
                def step(s, p, r):
                    after(dve, m_filled, M_UNITS * s + j + 1)
                    if j % 4 == 0:
                        after(dve, max_step, 8 * (s - 2) + 4 * half + 4)
                    nc.vector.tensor_reduce(neg_max[:, p, half, t, g * UNIT:(g + 1) * UNIT], slots[SLOT_OF["m", j]][:],
                                            AX.X, ALU.max, negate=True).then_inc(m_read, 1)
                return step

            def normalise(t):
                def step(s, p, r):
                    after(dve, otok_done, TPS * s + t + 1)
                    o = ps_misc[:].rearrange("p (h e) -> p h e", h=AH)
                    nc.vector.reciprocal(inv_sum[:, t], o[:, :, AD]).then_inc(inv_done, 1)
                    after(dve, inv_done, TPS * s + t + 1)
                    if t == 0:
                        after(dve, oT_done, s - 1)
                    nc.vector.tensor_tensor(o_tok[:, p, t], o[:, :, 0:AD],
                                            inv_sum[:, t].unsqueeze(2).to_broadcast([P, AH, AD]), ALU.mult
                                            ).then_inc(otok_copied, 1)
                return step

            def add_y(s, p, r):
                after(dve, biased, s + 1)
                after(dve, y_done, s + 1)
                some = x_sb[:, bass.ds(s * TPS, TPS), :]
                nc.vector.tensor_tensor(some, some, ps_misc[:, 0:S].rearrange("p (t d) -> p t d", t=TPS), ALU.add
                                        ).then_inc(y_added, 1)

            def y_is_added(s, p, r):
                after(dve, y_added, s + 1)

            def stats3_of(s, p, r):
                for t in range(TPS):
                    nc.vector.bn_stats(stats3[:, p, t], x_sb[:, s * TPS + t, :]).then_inc(stats3_part, 1)

            def settle3(s, p, r):
                after(dve, stats3_part, TPS * (s + 1))

            def moments3(s, p, r):
                for t in range(TPS):
                    ins = nc.vector.bn_aggr(mv3[:, p, t], stats3[:, p, t])
                ins.then_inc(stats3_done, 1)

            def add_up(s, p, r):
                after(dve, product_done, s + 1)
                nc.vector.tensor_reduce(w_tok[:, bass.ds(s * TPS, TPS)], product[:, p], AX.X, ALU.add).then_inc(w_done, 1)

            pipeline(dve, [(maximum(0), 3), (add_y, 6), (given_added, 0), (maximum(1), 3), (y_is_added, 6),
                           (stats_of, 0), (maximum(2), 3), (settle, 0), (normalise(0), 5), (stats3_of, 6), (settle3, 6),
                           (maximum(3), 3), (moments3, 6), (moments, 0), (maximum(4), 3), (normalise(1), 5),
                           (maximum(5), 3), (add_up, 8), (maximum(6), 3), (maximum(7), 3)], B, ROUNDS)

        @block.scalar
        def _(act):
            act.wait_ge(preset_v, 3)
            nc.scalar.preload_act_table(ACT.Exp)

            def copy_hT(s, p, r):
                after(act, hT_done, s + 1)
                after(act, v_done, s - 1)
                nc.scalar.copy(hT[:, p], ps_misc[:, 0:S]).then_inc(hT_copied, 1)

            def copy_v(s, p, r):
                after(act, v_done, s + 1)
                after(act, v_padded, s - 1)
                nc.scalar.copy(v_tok[:, p], ps_misc[:, 0:S].rearrange("p (t d) -> p t d", t=TPS)).then_inc(v_copied, 1)

            def norm(s, p, r):
                after(act, shift_done, s + 1)
                after(act, hT_done, s - 1)
                for t in range(TPS):
                    ins = nc.scalar.activation(h[:, p, t], x_sb[:, s * TPS + t, :], ACT.Identity,
                                               bias=shift[:, p, t:t + 1], scale=rstd[:, p, t:t + 1])
                ins.then_inc(h_done, 1)

            def copy_qk(s, p, r):
                after(act, qk_done, s + 1)
                after(act, part_step, 8 * (s - 1))
                nc.scalar.activation(qk[:, p, 0], ps_misc[:, 0:S], ACT.Identity, bias=bq_scaled[:], scale=SCALE)
                nc.scalar.activation(qk[:, p, 1], ps_misc[:, S:], ACT.Identity, bias=bk[:]).then_inc(qk_copied, 1)

            def copy_maxT(half):
                def step(s, p, r):
                    after(act, maxT_done, HALVES * s + half + 1)
                    after(act, max_stored[1 - p][half], 16 * (r + p))
                    nc.scalar.copy(max_T[:, half], ps_misc[:].bitcast(BF16)[0:PARTS * HH, 0:S]).then_inc(maxT_copied, 1)
                return step

            def exponential(j):
                def step(s, p, r):
                    after(act, e_filled, M_UNITS * s + j + 1)
                    after(act, o_done, AG * s + j // 2 - 1)
                    nc.scalar.activation(pT[:, j % PT_RING], slots[SLOT_OF["e", j]][:], ACT.Exp).then_inc(e_read, 1)
                return step

            def copy_o(half):
                def step(s, p, r):
                    after(act, o_done, AG * s + 2 * half + 2)
                    after(act, otok_done, TPS * s)
                    nc.scalar.copy(oT_pad[:, 2 * half:2 * half + 2], ps_o[:]).then_inc(o_copied, 1)
                return step

            def copy_oT(s, p, r):
                after(act, oT_done, s + 1)
                after(act, y_done, s - 1)
                nc.scalar.copy(oT[:, p], ps_misc[:, 0:S]).then_inc(oT_copied, 1)

            def norm3(s, p, r):
                after(act, shift3_done, s + 1)
                after(act, out_done, s - 1)
                for t in range(TPS):
                    ins = nc.scalar.activation(h3[:, p, t], x_sb[:, s * TPS + t, :], ACT.Identity,
                                               bias=shift3[:, p, t:t + 1], scale=rstd3[:, p, t:t + 1])
                ins.then_inc(h3_done, 1)

            e = [(exponential(j), 4) for j in range(M_UNITS)]
            pipeline(act, [e[0], e[1], (copy_maxT(1), 4), (copy_o(1), 5), (copy_hT, 1), e[2], e[3], (copy_qk, 1),
                           (norm3, 7), e[4], e[5], (copy_maxT(0), 3), (copy_o(0), 4), e[6], (copy_v, 1), (norm, 0),
                           e[7], (copy_oT, 5)], B, ROUNDS)

        @block.tensor
        def _(pe):
            nc.tensor.matmul(ps_misc[:, 0:D], bv[:], wo[:], start=True, stop=True).then_inc(bias_sum, 1)
            pe.wait_ge(preset_v, 3)
            pe.wait_ge(ones_in, 16 * 2 * HALVES)

            def free_slot(kind, j, s):
                slot, at = SLOT_OF[kind, j], 2 * j + (kind == "e")
                s_m, s_e = (s, s - 1) if kind == "m" else (s + 1, s)
                back, unit = last_user("m", slot, at)
                after_most(pe, m_read, M_UNITS * (s_m - back) + unit + 1, ALL_M)
                back, unit = last_user("e", slot, at)
                after_most(pe, e_read, M_UNITS * (s_e - back) + unit + 1, ALL_E)

            def for_maximum(j):
                half, t, g = j // 4, j % 4 // 2, j % 2
                def step(s, p, r):
                    if j % 4 == 0:
                        after(pe, filled[p][half], 16 * FILLS * (r + 1))
                    free_slot("m", j, s)
                    for q in range(UNIT):
                        head = g * UNIT + q
                        ins = nc.tensor.matmul(slots[SLOT_OF["m", j]][:, q],
                                               q_stack[0:QK_ROWS, p, half, head, t * P:(t + 1) * P],
                                               k_stack[0:QK_ROWS, p, half, head], start=True, stop=True)
                    ins.then_inc(m_filled, 1)
                return step

            def for_exponential(j):
                half, g, t = j // 4, j % 4 // 2, j % 2
                def step(s, p, r):
                    if j % 4 == 0:
                        after(pe, max_in[p][half], 16 * (r + 1))
                    free_slot("e", j, s)
                    for q in range(UNIT):
                        head = g * UNIT + q
                        ins = nc.tensor.matmul(slots[SLOT_OF["e", j]][:, q],
                                               k_stack[0:EXP_ROWS, p, half, head, t * P:(t + 1) * P],
                                               q_stack[0:EXP_ROWS, p, half, head], start=True, stop=True)
                    ins.then_inc(e_filled, 1)
                return step

            def values(g):
                def step(s, p, r):
                    if g == 0:
                        after(pe, v_padded, s + 1)
                    if g % 2 == 0:
                        after(pe, o_copied, HALVES * s + g // 2)
                    after(pe, e_read, M_UNITS * s + 2 * g + 2)
                    for t in range(TPS):
                        for q in range(UNIT):
                            ins = nc.tensor.matmul(ps_o[q * APAD:(q + 1) * APAD, g % 2], v_pad[:, p, t, g * UNIT + q],
                                                   pT[:, (2 * g + t) % PT_RING, q], start=t == 0, stop=t == TPS - 1,
                                                   skip_group_check=True)
                    ins.then_inc(o_done, 1)
                return step

            TURNS = (("y", 6, y_added, 1, 0), ("max1", 4, maxT_copied, 2, 1), ("hT", 1, hT_copied, 1, 0),
                     ("token0", 5, otok_copied, 2, 0), ("qk", 1, qk_copied, 1, 0),
                     ("token1", 5, otok_copied, 2, 1), ("max0", 3, maxT_copied, 2, 0), ("v", 1, v_copied, 1, 0),
                     ("oT", 5, oT_copied, 1, 0))

            def misc_free(name, s):
                at = [turn[0] for turn in TURNS].index(name)
                lag = TURNS[at][1]
                for n, (_, other_lag, read, per, which) in enumerate(TURNS):
                    if isinstance(s, int) or n == (at - 1) % len(TURNS):
                        other = s + lag - other_lag - (1 if n >= at else 0)
                        if isinstance(s, int):
                            if other < 0:
                                continue
                            other = min(other, B - 1)
                        after(pe, read, per * other + which + 1)

            def transpose_h(s, p, r):
                after(pe, h_done, s + 1)
                misc_free("hT", s)
                for t in range(TPS):
                    ins = nc.tensor.transpose(ps_misc[:, t * P:(t + 1) * P], h[:, p, t], ident[:])
                ins.then_inc(hT_done, 1)

            def transpose_max(half):
                def step(s, p, r):
                    after(pe, max_step, 8 * s + 4 * half + 4)
                    misc_free(f"max{half}", s)
                    for t in range(TPS):
                        ins = nc.tensor.transpose(ps_misc[:].bitcast(BF16)[0:PARTS * HH, t * P:(t + 1) * P],
                                                  max_part[:, half, t].rearrange("p a h -> p (a h)"), ident_b[:])
                    ins.then_inc(maxT_done, 1)
                return step

            def by_token(t):
                def step(s, p, r):
                    if t == 0:
                        after(pe, o_copied, HALVES * (s + 1))
                    misc_free(f"token{t}", s)
                    for g in range(AG):
                        ins = nc.tensor.transpose(ps_misc[:, g * P:(g + 1) * P], oT_pad[:, g, t * P:(t + 1) * P],
                                                  ident[:])
                    ins.then_inc(otok_done, 1)
                return step

            def project_qk(s, p, r):
                after(pe, hT_copied, s + 1)
                misc_free("qk", s)
                nc.tensor.matmul(ps_misc[:, 0:S], wq[:], hT[:, p], start=True, stop=True)
                nc.tensor.matmul(ps_misc[:, S:], wk[:], hT[:, p], start=True, stop=True).then_inc(qk_done, 1)

            def project_v(s, p, r):
                misc_free("v", s)
                for t in range(TPS):
                    ins = nc.tensor.matmul(ps_misc[:, t * D:(t + 1) * D], hT[:, p, t * P:(t + 1) * P], wv[:],
                                           start=True, stop=True)
                ins.then_inc(v_done, 1)

            def transpose_o(s, p, r):
                after(pe, otok_copied, TPS * (s + 1))
                misc_free("oT", s)
                for t in range(TPS):
                    ins = nc.tensor.transpose(ps_misc[:, t * P:(t + 1) * P],
                                              o_tok[:, p, t].rearrange("p h e -> p (h e)"), ident[:])
                ins.then_inc(oT_done, 1)

            def output(s, p, r):
                after(pe, oT_copied, s + 1)
                misc_free("y", s)
                for t in range(TPS):
                    ins = nc.tensor.matmul(ps_misc[:, t * D:(t + 1) * D], oT[:, p, t * P:(t + 1) * P], wo[:],
                                           start=True, stop=True)
                ins.then_inc(y_done, 1)

            M = [(for_maximum(j), 3) for j in range(M_UNITS)]
            E = [(for_exponential(j), 4) for j in range(M_UNITS)]
            pipeline(pe, [M[0], (output, 6), E[0], M[1], E[1], (transpose_max(1), 4), (values(3), 5), M[2],
                           (transpose_h, 1), E[2], (by_token(0), 5), M[3], E[3], (project_qk, 1), (values(0), 4), M[4],
                           E[4], (by_token(1), 5), M[5], E[5], (values(1), 4), (transpose_max(0), 3), M[6], E[6],
                           (project_v, 1), M[7], E[7], (transpose_o, 5), (values(2), 4)], B, ROUNDS)


def by_half(weight):
    return np.ascontiguousarray(weight.reshape(-1, HALVES, HH, AD).transpose(0, 1, 3, 2).reshape(-1, D))


SEL = S // 8
GB = P // SEL
G = B // GB
HG = 4
SPREADS = 4
FF = 512
FB = FF // P
LATE = {"a_wq": [P, D], "a_wk": [P, D], "a_wv": [P, D], "a_wo": [P, D], "a_bq": [P, 1], "a_bk": [P, 1], "a_bv": [P, D],
        "a_bo": [P, D], "d_rw": [P, D], "d_rb": [P, 1], "d_wqkv": [P, 3 * D], "d_wo": [P, AG, D],
        "d_ln1": [P, 1], "d_ln2": [P, 1], "d_own_head": [P, AH], "d_pick": [B, GB, G],
        "d_row": [P, G], "d_row_ids": [P, G], "d_real": [P, 1], "d_inv": [P, AD // 2], "d_column": [P, TPS]}
IDS = 4
RMS_EPS = 1e-6
TWO_PI = 2 * np.pi
C1 = 6.28125
C2 = float(np.float32(np.round((TWO_PI - C1) * 2.0 ** 21) / 2.0 ** 21))
C3 = float(TWO_PI - C1 - C2)
ROUND = 1.5 * 2.0 ** 23


def routed_phase(nc, w, keep, out):
    with Memory(nc) as m:
        work, w_tok = keep["h2"], keep["w_tok"]
        ident = keep["ident"]

        t = keep["late"]
        w1 = m.sbuf("d_w1", [P, FF])
        w2 = m.sbuf("d_w2", [P, FB, D])
        half_pow = m.sbuf("d_half_pow", [P, G])
        ones = m.sbuf("d_ones", [B, P])
        w_row = m.sbuf("d_w_row", [B, S])
        top = m.sbuf("d_top", [B, SEL])
        top_u = m.sbuf("d_top_u", [B, SEL], U32)
        top_i = m.sbuf("d_top_i", [B, SEL])
        coef_row = m.sbuf("d_coef_row", [B, SEL])
        spread_i = m.sbuf("d_spread_i", [B, B, SEL])
        row_f = m.sbuf("d_row_f", [P, G])
        rows = m.sbuf("d_rows", [P, G], I32)
        row_ids_f = m.sbuf("d_row_ids_f", [P, G])
        rows_ids = m.sbuf("d_rows_ids", [P, G], I32)
        w_sel = m.sbuf("d_w_sel", [P, G])
        coef = m.sbuf("d_coef", [P, G])
        one_hot = m.sbuf("d_one_hot", [P, TPS, B * SEL])
        flat = work[:].rearrange("p t d -> p (t d)")
        half_flat = NT * D // 2
        prob = flat[:, 0:half_flat].rearrange("p (g h j) -> p g h j", g=G, h=AH)
        mask_rows = flat[:, half_flat:half_flat + G * S].rearrange("p (g s) -> p g s", g=G)
        mask_T = flat[:, half_flat + G * S:].rearrange("p (g c i) -> p g c i", g=G, c=TPS)
        hidden = flat[:, half_flat:].rearrange("p (f n) -> p f n", f=FB)
        mask = m.sbuf("d_mask", [P, G, SEL])
        pos = m.sbuf("d_pos", [P, G], I32)
        pos_f = m.sbuf("d_pos_f", [P, G])
        angle = m.sbuf("d_angle", [P, G, AD // 2])
        turns = m.sbuf("d_turns", [P, G, AD // 2])
        angle_c = m.sbuf("d_angle_c", [P, G, AD // 2])
        cos = m.sbuf("d_cos", [P, G, 2, AD // 2])
        sin = m.sbuf("d_sin", [P, G, 2, AD // 2])
        x_sel = m.sbuf("d_x_sel", [P, G, D])
        h_sel = m.sbuf("d_h_sel", [P, G, D])
        stats_sel = m.sbuf("d_stats_sel", [P, G, 6])
        mv_sel = m.sbuf("d_mv_sel", [P, G, 2])
        square = m.sbuf("d_square", [P, G, D])
        ms = m.sbuf("d_ms", [P, G])
        rstd = m.sbuf("d_rstd", [P, G])
        xn = m.sbuf("d_xn", [P, G, D])
        xnT = m.sbuf("d_xnT", [P, G, P])
        qk = m.sbuf("d_qk", [P, G, 2 * AH, AD])
        swapped = m.sbuf("d_swapped", [P, G, 2 * AH, AD])
        v_pad = m.sbuf("d_v_pad", [P, G, AH, APAD])
        qT = m.sbuf("d_qT", [P, G, P])
        kT = m.sbuf("d_kT", [P, G, P])
        k_spread = m.sbuf("d_k_spread", [P, SPREADS, GB, AH, SEL])
        top_score = m.sbuf("d_top_score", [P, G, AH])
        total = m.sbuf("d_total", [P, G, AH])
        probT = m.sbuf("d_probT", [P, 2, AH, P])
        oT = m.sbuf("d_oT", [P, 2, AG, P])
        ps = m.psum("d_ps", [P, G, 512])

        loaded = m.sem("d_loaded")
        preset = m.sem("d_preset")
        chain = m.sem("d_chain")
        wT_done = m.sem("d_wT_done")
        top_done = m.sem("d_top_done")
        picked = m.sem("d_picked")
        picked_read = m.sem("d_picked_read")
        mask_in = m.sem("d_mask_in")
        pos_in = m.sem("d_pos_in")
        x_in = m.sem("d_x_in")
        clamped = m.sem("d_clamped")
        maskT_done = m.sem("d_maskT_done")
        maskT_copied = m.sem("d_maskT_copied")
        mask_done = m.sem("d_mask_done")
        mask_read = m.sem("d_mask_read")
        angle_done = m.sem("d_angle_done")
        rope_ready = m.sem("d_rope_ready")
        ms_done = m.sem("d_ms_done")
        rstd_done = m.sem("d_rstd_done")
        xn_done = m.sem("d_xn_done")
        xnT_done = m.sem("d_xnT_done")
        xnT_copied = m.sem("d_xnT_copied")
        qkv_done = m.sem("d_qkv_done")
        v_copied = m.sem("d_v_copied")
        roped = m.sem("d_roped")
        qkT_done = m.sem("d_qkT_done")
        qkT_copied = m.sem("d_qkT_copied")
        k_spread_dve = m.sem("d_k_spread_dve")
        k_spread_pool = m.sem("d_k_spread_pool")
        score_done = m.sem("d_score_done")
        score_read = m.sem("d_score_read")
        top_score_done = m.sem("d_top_score_done")
        less_max = m.sem("d_less_max")
        less_max_dve = m.sem("d_less_max_dve")
        total_done = m.sem("d_total_done")
        normed = m.sem("d_normed")
        exp_done = m.sem("d_exp_done")
        probT_done = m.sem("d_probT_done")
        oT_done = m.sem("d_oT_done")
        oT_copied = m.sem("d_oT_copied")
        y_done = m.sem("d_y_done")
        x1_done = m.sem("d_x1_done")
        up_done = m.sem("d_up_done")
        gelu_done = m.sem("d_gelu_done")
        down_done = m.sem("d_down_done")
        result_done = m.sem("d_result_done")
        scattered = m.sem("d_scattered")
        block = m.ctx.enter_context(nc.Block())
        halves = [slice(half * HG, (half + 1) * HG) for half in range(2)]
        K = SEL - 1

        def subtract_max(engine, half):
            some = prob[:, halves[half], :, 0:K]
            return engine.tensor_tensor(some, some, top_score[:, halves[half]].unsqueeze(3).to_broadcast([P, HG, AH, K]),
                                        ALU.subtract)

        def normalise(engine, half):
            some = prob[:, halves[half], :, 0:K]
            return engine.tensor_tensor(some, some, total[:, halves[half]].unsqueeze(3).to_broadcast([P, HG, AH, K]),
                                        ALU.mult)

        by_pool = range(1, G, 3)
        by_dve = [g for g in range(G) if g not in by_pool]

        def spread_ready(g):
            return (k_spread_pool, by_pool.index(g) + 1) if g in by_pool else (k_spread_dve, by_dve.index(g) + 1)

        def spread_k(engine, wait, g, done):
            wait.wait_ge(qkT_copied, g + 1)
            after(wait, score_done, g - SPREADS + 1)
            engine.tensor_tensor(k_spread[:, g % SPREADS],
                                 kT[:, g].rearrange("p (b j) -> p b j", b=GB).unsqueeze(2).to_broadcast([P, GB, AH, SEL]),
                                 t["d_own_head"][:].unsqueeze(1).unsqueeze(3).to_broadcast([P, GB, AH, SEL]),
                                 ALU.mult).then_inc(done, 1)

        @block.sync
        def _(sp):
            for to, name in ((w1, "d_w1"), (w2, "d_w2")):
                sp.dma_start(to[:], w[name]).then_inc(loaded, 16)
            sp.wait_ge(scattered, 16 * G)

        @block.gpsimd
        def _(pool):
            nc.gpsimd.memset(half_pow[:], -0.5).then_inc(preset, 1)
            nc.gpsimd.memset(ones[:], 1.0).then_inc(preset, 1)
            nc.gpsimd.memset(v_pad[:], 0.0).then_inc(preset, 1)
            nc.gpsimd.memset(probT[:], 0.0).then_inc(preset, 1)
            pool.wait_ge(preset, 4)
            pool.wait_ge(picked_read, 1)
            index = lambda a, g: bass.IndirectOffsetOnAxis(ap=a[:, g:g + 1], axis=0)

            def gather(to, table, at, done):
                for g in range(G):
                    nc.gpsimd.indirect_dma_start(to(g), None, table, index(at, g)).then_inc(done, 16)

            def inv_root(n):
                pool.wait_ge(ms_done, n)
                nc.gpsimd.tensor_tensor(rstd[:], ms[:], half_pow[:], ALU.pow).then_inc(rstd_done, 1)

            gather(lambda g: x_sel[:, g], keep["x_rows"], rows, x_in)
            gather(lambda g: pos[:, g:g + 1], w["d_position"], rows_ids, pos_in)
            inv_root(1)
            gather(lambda g: mask_rows[:, g], w["d_mask"], rows_ids, mask_in)
            inv_root(2)
            for g in by_pool:
                spread_k(nc.gpsimd, pool, g, k_spread_pool)
            pool.wait_ge(top_score_done, 1)
            subtract_max(nc.gpsimd, 0).then_inc(less_max, 1)
            pool.wait_ge(total_done, 1)
            normalise(nc.gpsimd, 1).then_inc(normed, 1)
            inv_root(3)
            for g in range(G):
                pool.wait_ge(result_done, g // HG + 1)
                nc.gpsimd.indirect_dma_start(out, index(rows, g), square[:, g], None).then_inc(scattered, 16)

        @block.vector
        def _(dve):
            steps = [0]

            def chained(ins):
                steps[0] += 1
                ins.then_inc(chain, 1)
                dve.wait_ge(chain, steps[0])

            v = nc.vector
            dve.wait_ge(wT_done, 1)
            chained(v.tensor_scalar(w_row[:], ps[0:B, 0, 0:S], t["d_rb"][0:B], None, ALU.add))
            for k in range(0, SEL, 8):
                chained(v.max(top[:, k:k + 8], w_row[:]))
                chained(v.max_index(top_u[:, k:k + 8], top[:, k:k + 8], w_row[:]))
                if k + 8 < SEL:
                    chained(v.match_replace(w_row[:], top[:, k:k + 8], w_row[:], -3.0e38))
            chained(v.tensor_scalar(coef_row[:], top[:], top[:, SEL - 1:SEL], None, ALU.is_gt))
            chained(v.tensor_scalar(coef_row[:], coef_row[:], -1.0, 1.0, ALU.mult, ALU.add))
            v.tensor_copy(top_i[:], top_u[:]).then_inc(top_done, 1)
            dve.wait_ge(top_done, 1)
            v.tensor_tensor(spread_i[:], top_i[:].unsqueeze(1).to_broadcast([B, B, SEL]),
                            ident[0:B, 0:B].unsqueeze(2).to_broadcast([B, B, SEL]), ALU.mult).then_inc(top_done, 1)
            dve.wait_ge(picked, 1)
            v.tensor_tensor(row_f[:], ps[:, 3, 0:G], t["d_row"][:], ALU.add)
            chained(v.tensor_tensor(row_ids_f[:], ps[:, 3, 0:G], t["d_row_ids"][:], ALU.add))
            v.tensor_copy(rows[:], row_f[:])
            v.tensor_copy(rows_ids[:], row_ids_f[:]).then_inc(picked_read, 1)
            v.tensor_scalar(w_sel[:], ps[:, 3, G:2 * G], t["d_real"][:], None, ALU.mult)
            v.tensor_copy(coef[:], ps[:, 3, 2 * G:3 * G])
            dve.wait_ge(picked, 2)
            for c in range(TPS):
                ins = v.tensor_scalar(one_hot[:, c].rearrange("p (a n) -> p a n", a=2), ps[:, 1:3],
                                      t["d_column"][:, c:c + 1], None, ALU.is_equal)
            ins.then_inc(picked_read, 1)
            dve.wait_ge(x_in, 16 * G)
            for g in range(G):
                ins = v.bn_stats(stats_sel[:, g], x_sel[:, g])
            chained(ins)
            for g in range(G):
                ins = v.bn_aggr(mv_sel[:, g], stats_sel[:, g])
            chained(ins)
            v.tensor_scalar(ms[:], mv_sel[:, :, 1], LN_EPS, None, ALU.add).then_inc(ms_done, 1)
            dve.wait_ge(rstd_done, 1)
            for g in range(G):
                ins = v.tensor_scalar(h_sel[:, g], x_sel[:, g], mv_sel[:, g, 0:1], rstd[:, g:g + 1],
                                      ALU.subtract, ALU.mult)
            chained(ins)

            def mean_square(x):
                chained(v.tensor_tensor(square[:], x[:], x[:], ALU.mult))
                chained(v.tensor_reduce(ms[:], square[:], AX.X, ALU.add))
                v.tensor_scalar(ms[:], ms[:], 1.0 / D, RMS_EPS, ALU.mult, ALU.add).then_inc(ms_done, 1)

            by_token = lambda a: a[:].unsqueeze(2).to_broadcast([P, G, D])
            mean_square(h_sel)
            dve.wait_ge(rstd_done, 2)
            v.tensor_tensor(xn[:], h_sel[:], by_token(rstd), ALU.mult).then_inc(xn_done, 1)
            dve.wait_ge(pos_in, 16 * G)
            chained(v.tensor_copy(pos_f[:], pos[:]))
            chained(v.tensor_tensor(angle[:], pos_f[:].unsqueeze(2).to_broadcast([P, G, AD // 2]),
                                    t["d_inv"][:].unsqueeze(1).to_broadcast([P, G, AD // 2]), ALU.mult))
            chained(v.tensor_scalar(turns[:], angle[:], 1 / TWO_PI, ROUND, ALU.mult, ALU.add))
            chained(v.tensor_scalar(turns[:], turns[:], ROUND, None, ALU.subtract))
            for part in (C1, C2, C3):
                chained(v.tensor_scalar(angle_c[:], turns[:], -part, None, ALU.mult))
                chained(v.tensor_tensor(angle[:], angle[:], angle_c[:], ALU.add))
            PI = 3.1415925
            chained(v.tensor_scalar(angle[:], angle[:], PI, -PI, ALU.min, ALU.max))
            chained(v.tensor_scalar(angle_c[:], angle[:], np.pi / 2, None, ALU.add))
            chained(v.tensor_scalar(turns[:], angle_c[:], PI, -TWO_PI, ALU.is_gt, ALU.mult))
            chained(v.tensor_tensor(angle_c[:], angle_c[:], turns[:], ALU.add))
            v.tensor_scalar(angle_c[:], angle_c[:], PI, -PI, ALU.min, ALU.max).then_inc(angle_done, 1)
            dve.wait_ge(mask_in, 16 * G)
            v.tensor_scalar(mask_rows, mask_rows, -3.0e38, None, ALU.max).then_inc(clamped, 1)

            dve.wait_ge(rope_ready, 1)
            for half in range(2):
                gs = slice(half * HG, (half + 1) * HG)
                dve.wait_ge(qkv_done, (half + 1) * HG)
                dve.wait_ge(v_copied, (half + 1) * HG)
                value = ps[:, gs, 0:2 * D].rearrange("p g (h e) -> p g h e", e=AD)
                v.tensor_tensor(qk[:, gs], value,
                                cos[:, gs].rearrange("p g u f -> p g (u f)").unsqueeze(2).to_broadcast([P, HG, 2 * AH, AD]),
                                ALU.mult)
                F = AD // 2
                for u in range(2):
                    ins = v.tensor_tensor(swapped[:, gs, :, u * F:(u + 1) * F], value[:, :, :, (1 - u) * F:(2 - u) * F],
                                          sin[:, gs, u].unsqueeze(2).to_broadcast([P, HG, 2 * AH, F]), ALU.mult)
                chained(ins)
                v.tensor_tensor(qk[:, gs], qk[:, gs], swapped[:, gs], ALU.add).then_inc(roped, 1)
            for g in by_dve:
                spread_k(v, dve, g, k_spread_dve)
            dve.wait_ge(mask_read, G)
            chained(v.memset(prob[:, :, :, K:SEL], 0.0))
            for half, gs in enumerate(halves):
                dve.wait_ge(score_done, (half + 1) * HG)
                chained(v.tensor_tensor(prob[:, gs, :, 0:K],
                                        ps[:, gs].rearrange("p g (h j) -> p g h j", h=AH)[:, :, :, 0:K],
                                        mask[:, gs, 0:K].unsqueeze(2).to_broadcast([P, HG, AH, K]), ALU.add))
                v.tensor_reduce(top_score[:, gs], prob[:, gs, :, 0:K], AX.X, ALU.max).then_inc(top_score_done, 1)
            dve.wait_ge(top_score_done, 2)
            subtract_max(v, 1).then_inc(less_max_dve, 1)
            for half, gs in enumerate(halves):
                dve.wait_ge(exp_done, half + 1)
                chained(v.tensor_reduce(total[:, gs], prob[:, gs, :, 0:K], AX.X, ALU.add))
                if half == 0:
                    chained(v.reciprocal(total[:, gs], total[:, gs]))
                    chained(normalise(v, half))
                else:
                    v.reciprocal(total[:, gs], total[:, gs]).then_inc(total_done, 1)
            dve.wait_ge(preset, 4)
            for half, gs in enumerate(halves):
                for g in range(half * HG, (half + 1) * HG):
                    if half == 1 and g == HG:
                        dve.wait_ge(normed, 1)
                    after(dve, oT_done, g - 1)
                    for b in range(GB):
                        rows_b = slice(b * SEL, (b + 1) * SEL)
                        ins = v.transpose(probT[rows_b, g % 2, :, rows_b], prob[rows_b, g])
                    ins.then_inc(probT_done, 1)
            dve.wait_ge(y_done, G)
            x1 = xn
            v.tensor_tensor(x1[:], h_sel[:], ps[:, :, 0:D], ALU.add).then_inc(x1_done, 1)
            dve.wait_ge(x1_done, 1)
            mean_square(x1)
            chained(v.tensor_tensor(h_sel[:], h_sel[:], by_token(coef), ALU.mult))
            chained(v.tensor_tensor(x_sel[:], x_sel[:], h_sel[:], ALU.add))
            dve.wait_ge(rstd_done, 3)
            v.tensor_tensor(square[:], x1[:], by_token(rstd), ALU.mult).then_inc(xn_done, 1)
            for gs in halves:
                dve.wait_ge(down_done, gs.stop)
                chained(v.tensor_tensor(xn[:, gs], x1[:, gs], ps[:, gs, 0:D], ALU.add))
                chained(v.tensor_tensor(xn[:, gs], xn[:, gs], w_sel[:, gs].unsqueeze(2).to_broadcast([P, HG, D]), ALU.mult))
                v.tensor_tensor(square[:, gs], xn[:, gs], x_sel[:, gs], ALU.add).then_inc(result_done, 1)

        @block.scalar
        def _(act):
            for g in range(G):
                act.wait_ge(xnT_done, g + 1)
                nc.scalar.activation(xnT[:, g], ps[:, g, 0:P], ACT.Copy, scale=t["d_ln1"][:]).then_inc(xnT_copied, 1)
            act.wait_ge(preset, 4)
            for g in range(G):
                act.wait_ge(qkv_done, g + 1)
                nc.scalar.copy(v_pad[:, g, :, 0:AD], ps[:, g, 2 * D:3 * D].rearrange("p (h e) -> p h e", h=AH)
                               ).then_inc(v_copied, 1)
            act.wait_ge(angle_done, 1)
            for u in range(2):
                nc.scalar.activation(cos[:, :, u], angle_c[:], ACT.Sin)
            nc.scalar.activation(sin[:, :, 0], angle[:], ACT.Sin, scale=-1.0)
            nc.scalar.activation(sin[:, :, 1], angle[:], ACT.Sin).then_inc(rope_ready, 1)
            for g in range(G):
                act.wait_ge(qkT_done, g + 1)
                nc.scalar.mul(qT[:, g], ps[:, g, 0:P], AD ** -0.5)
                nc.scalar.copy(kT[:, g], ps[:, g, P:2 * P]).then_inc(qkT_copied, 1)
            for g in range(G):
                act.wait_ge(maskT_done, g + 1)
                nc.scalar.copy(mask_T[:, g].rearrange("p c i -> p (c i)"), ps[:, g, 0:S]).then_inc(maskT_copied, 1)
            for g in range(G):
                act.wait_ge(mask_done, g + 1)
                nc.scalar.copy(mask[:, g], ps[:, g, 0:SEL]).then_inc(mask_read, 1)
            for half in range(2):
                act.wait_ge(less_max_dve if half else less_max, 1)
                some = prob[:, half * HG:(half + 1) * HG, :, 0:SEL - 1]
                nc.scalar.activation(some, some, ACT.Exp).then_inc(exp_done, 1)
            for g in range(G):
                act.wait_ge(oT_done, g + 1)
                after(act, y_done, g - 1)
                nc.scalar.copy(oT[:, g % 2].rearrange("p a i -> p (a i)"), ps[:, g]).then_inc(oT_copied, 1)
            for g in range(G):
                act.wait_ge(xnT_done, G + g + 1)
                nc.scalar.activation(xnT[:, g], ps[:, g, 0:P], ACT.Copy, scale=t["d_ln2"][:]).then_inc(xnT_copied, 1)
            for u in range(2 * FB):
                act.wait_ge(up_done, u + 1)
                half, f = u // FB, u % FB
                nc.scalar.activation(hidden[:, f, half * 512:(half + 1) * 512], ps[:, u], ACT.Gelu_apprx_tanh
                                     ).then_inc(gelu_done, 1)

        @block.tensor
        def _(pe):
            for c in range(TPS):
                ins = nc.tensor.transpose(ps[0:B, 0, c * P:(c + 1) * P], w_tok[:].rearrange("p (b c) -> p b c", c=TPS)[:, :, c],
                                          ident[:])
            ins.then_inc(wT_done, 1)
            pe.wait_ge(top_done, 1)
            pe.wait_ge(preset, 2)
            for n, row in enumerate((top_i, top, coef_row)):
                for b in range(GB):
                    ins = nc.tensor.matmul(ps[b * SEL:(b + 1) * SEL, 3, n * G:(n + 1) * G], row[:], t["d_pick"][:, b],
                                           start=True, stop=True)
            ins.then_inc(picked, 1)
            pe.wait_ge(top_done, 2)
            for half in range(2):
                ins = nc.tensor.matmul(ps[:, 1 + half], ones[:],
                                       spread_i[:, half * B // 2:(half + 1) * B // 2], start=True, stop=True)
            ins.then_inc(picked, 1)
            pe.wait_ge(picked_read, 2)

            def transpose_xn(n, xn):
                pe.wait_ge(xn_done, n + 1)
                for g in range(G):
                    nc.tensor.transpose(ps[:, g, 0:P], xn[:, g], ident[:]).then_inc(xnT_done, 1)

            transpose_xn(0, xn)
            for g in range(G):
                pe.wait_ge(xnT_copied, g + 1)
                nc.tensor.matmul(ps[:, g, 0:3 * D], xnT[:, g], t["d_wqkv"][:], start=True, stop=True).then_inc(qkv_done, 1)
            for g in range(G):
                pe.wait_ge(roped, g // HG + 1)
                for which in range(2):
                    ins = nc.tensor.transpose(ps[:, g, which * P:(which + 1) * P],
                                              qk[:, g, which * AH:(which + 1) * AH].rearrange("p h e -> p (h e)"), ident[:])
                ins.then_inc(qkT_done, 1)
            pe.wait_ge(clamped, 1)
            for g in range(G):
                pe.wait_ge(qkT_copied, g + 1)
                for c in range(TPS):
                    ins = nc.tensor.transpose(ps[:, g, c * P:(c + 1) * P], mask_rows[:, g, c * P:(c + 1) * P], ident[:])
                ins.then_inc(maskT_done, 1)
            for g in range(G):
                pe.wait_ge(maskT_copied, g + 1)
                for b in range(GB):
                    rows_b = slice(b * SEL, (b + 1) * SEL)
                    for c in range(TPS):
                        ins = nc.tensor.matmul(ps[rows_b, g, 0:SEL], mask_T[:, g, c, rows_b],
                                               one_hot[:, c, (g * GB + b) * SEL:(g * GB + b + 1) * SEL],
                                               start=c == 0, stop=c == TPS - 1)
                ins.then_inc(mask_done, 1)
            for g in range(G):
                pe.wait_ge(mask_read, g + 1)
                pe.wait_ge(*spread_ready(g))
                for b in range(GB):
                    rows_b = slice(b * SEL, (b + 1) * SEL)
                    ins = nc.tensor.matmul(ps[rows_b, g], qT[:, g, rows_b], k_spread[:, g % SPREADS, b], start=True, stop=True)
                ins.then_inc(score_done, 1)

            def transpose_and_output(g):
                pe.wait_ge(oT_copied, g + 1)
                for a in range(AG):
                    ins = nc.tensor.matmul(ps[:, g, 0:D], oT[:, g % 2, a], t["d_wo"][:, a], start=a == 0, stop=a == AG - 1)
                ins.then_inc(y_done, 1)

            for g in range(G):
                pe.wait_ge(probT_done, g + 1)
                for head in range(AH):
                    a, q = head // 4, head % 4
                    ins = nc.tensor.matmul(ps[q * APAD:(q + 1) * APAD, g, a * P:(a + 1) * P], v_pad[:, g, head],
                                           probT[:, g % 2, head], start=True, stop=True, skip_group_check=True)
                ins.then_inc(oT_done, 1)
                if g > 0:
                    transpose_and_output(g - 1)
            transpose_and_output(G - 1)
            pe.wait_ge(x1_done, 1)
            transpose_xn(1, square)
            pe.wait_ge(loaded, 2 * 16)
            for u in range(2 * FB):
                half, f = u // FB, u % FB
                pe.wait_ge(xnT_copied, G + (half + 1) * HG)
                nc.tensor.matmul(ps[:, u], w1[:, f * P:(f + 1) * P], xnT[:, half * HG:(half + 1) * HG],
                                 start=True, stop=True).then_inc(up_done, 1)
            for g in range(G):
                pe.wait_ge(gelu_done, FB * (g // HG + 1))
                for f in range(FB):
                    ins = nc.tensor.matmul(ps[:, g, 0:D], hidden[:, f, g * P:(g + 1) * P], w2[:, f],
                                           start=f == 0, stop=f == FB - 1)
                ins.then_inc(down_done, 1)


def constants4():
    f = lambda a: np.ascontiguousarray(a, dtype=np.float32)
    p, g = np.arange(P), np.arange(G)
    b = g[None, :] * GB + p[:, None] // SEL
    return {"d_own_head": f(p[:, None] // AD == np.arange(AH)), "d_row": f(b * S), "d_row_ids": f(np.minimum(b, IDS - 1) * S),
            "d_pick": f(np.arange(B)[:, None, None] == g[None, None, :] * GB + np.arange(GB)[None, :, None]),
            "d_real": f((p % SEL != SEL - 1)[:, None]), "d_column": f(p[:, None] + P * np.arange(TPS)),
            "d_inv": f(np.broadcast_to(1.0 / np.float32(10000.0) ** (np.arange(0, AD, 2, dtype=np.float32) / AD),
                                       (P, AD // 2)))}


def two_layers(nc, w, out):
    with Memory(nc) as m:
        internal = lambda name, rows: nc.dram_tensor(name, (rows, D), F32, kind="Internal").ap()
        keep = {"x": m.sbuf("x", [P, NT, D]), "h2": m.sbuf("h2", [P, NT, D]), "ident": m.sbuf("ident", [P, P]),
                "w_tok": m.sbuf("w_tok", [P, NT]), "slot": m.sbuf("slot", [P, NT], I32), "gathered": [m.sem(f"gathered{n}") for n in range(len(GATHERS))], "x_rows": internal("x_rows", NT * P),
                "sorted_in": internal("sorted_in", NX * P), "sorted_out": internal("sorted_out", NX * P)}
        keep["late"] = {name: m.sbuf(name, shape) for name, shape in LATE.items()}
        with Memory(nc) as early:
            keep.update(h2T=early.sbuf("h2T", [P, B * S]), logits=early.sbuf("logits", [P, NT, NE]),
                        expert_up=early.sbuf("expert_up", [P, NE, 2 * EF]))
            retention_phase(nc, w, keep)
            mixture_phase(nc, w, keep)
        attention_phase(nc, w, keep, out)
        routed_phase(nc, w, keep, out)


def layouts(inputs):
    a0 = {k[8:]: v for k, v in inputs.items() if k.startswith("L0_attn_")}
    f0 = {k[7:]: v for k, v in inputs.items() if k.startswith("L0_ffn_")}
    a1 = {k[8:]: v for k, v in inputs.items() if k.startswith("L1_attn_")}
    f1 = {k[7:]: v for k, v in inputs.items() if k.startswith("L1_ffn_")}
    on_all = lambda v: np.broadcast_to(v[None], (P,) + v.shape)
    w = {**constants(), **constants2(), **constants4(),
         "x": a0["hidden_states"].reshape(NT, P, D).transpose(1, 0, 2),
         "r_wq": a0["Wq"], "r_wk": a0["Wk"], "r_wv": a0["Wv"], "r_wo": pad_heads(a0["Wo"], RD),
         "router": f0["w_router"].T, "eu": f0["gate_up_proj"].transpose(1, 0, 2),
         "ed": f0["down_proj"].reshape(NE, EB, P, D).transpose(2, 0, 1, 3),
         "shared_up": np.stack([f0["w_gate"].T, f0["w_up"].T], 1).reshape(P, 2, EB, P),
         "shared_down": f0["w_down"].T.reshape(EB, P, D).transpose(1, 0, 2),
         "a_wq": by_half(a1["Wq"].T), "a_wk": by_half(a1["Wk"].T), "a_wv": a1["Wv"].T, "a_wo": a1["Wo"].T,
         "a_bq": by_half(a1["bq"][None]).T, "a_bk": by_half(a1["bk"][None]).T,
         "a_bv": on_all(a1["bv"]).T, "a_bo": on_all(a1["bo"]),
         "d_rw": on_all(f1["router_w"][:, 0]), "d_rb": on_all(f1["router_b"]),
         "d_wqkv": np.concatenate([f1["wq"], f1["wk"], f1["wv"]], 1), "d_wo": pad_heads(f1["wo"], AD),
         "d_w1": f1["w1"], "d_w2": f1["w2"].reshape(FB, P, D).transpose(1, 0, 2),
         "d_ln1": f1["ln1"][:, None], "d_ln2": f1["ln2"][:, None],
         "d_position": f1["position_ids"][:, :S].reshape(IDS * S, 1),
         "d_mask": f1["attention_mask"][:, 0, :S, :S].reshape(IDS * S, S)}
    return {name: np.ascontiguousarray(a) for name, a in w.items()}


def kernel(**inputs):
    import concourse.bacc as _bacc
    from concourse.bass_utils import run_bass_kernel_spmd as _run

    nc = _bacc.Bacc("TRN2", target_bir_lowering=False, num_devices=1)
    arrays, w = {}, {}
    for name, a in layouts({k: np.asarray(v) for k, v in inputs.items()}).items():
        arrays[f"in_{name}_dram"] = a
        w[name] = nc.dram_tensor(f"in_{name}_dram", a.shape, mybir.dt.from_np(a.dtype), kind="ExternalInput").ap()
    out = nc.dram_tensor("out_0_dram", (NT * P, D), F32, kind="ExternalOutput").ap()
    two_layers(nc, w, out)
    r = _run(nc, [arrays], core_ids=[0])
    return np.asarray(r.results[0]["out_0_dram"]).reshape(B, S, D)
```
